# Optimizing a Trainium2 kernel written in Bass

```python
import numpy as np
import jax
import jax.numpy as jnp

def _softmax(x, axis=-1):
    return jax.nn.softmax(x, axis=axis)

def _gelu(x):
    return jax.nn.gelu(x, approximate=True)

def _silu(x):
    return jax.nn.silu(x)

def _sigmoid(x):
    return jax.nn.sigmoid(x)

def _layernorm(x, axis=-1, eps=1e-05):
    m = jnp.mean(x, axis=axis, keepdims=True)
    v = jnp.var(x, axis=axis, keepdims=True)
    return (x - m) / jnp.sqrt(v + eps)

def _scatter_add(tgt, idx, src, axis=0):
    return tgt.at[idx].add(src)

def _segment_sum(src, seg, n):
    return jax.ops.segment_sum(src, seg, n)
kernel_name = 'mk_gnn_ffn_d1_gnn_r64_346c1d'

def setup_inputs(seed: int=0):
    np.random.seed(seed)
    _w = jnp.asarray

    def _rec_inputs():
        import jax
        import jax.numpy as jnp
        _gk = jax.random.key(seed)
        x = -0.0002117 + 1 * jax.random.normal(jax.random.fold_in(_gk, 1), (10000, 512), jnp.float32)
        src = jax.random.randint(jax.random.fold_in(_gk, 2), (2500,), 0, 10000, jnp.int32)
        dst = jnp.minimum((10000 * jax.random.uniform(jax.random.fold_in(_gk, 3), (2500,)) ** 2.0).astype(jnp.int32), 9999)
        _o = jnp.argsort(dst, stable=True)
        src = src[_o]
        dst = dst[_o]
        return (x, src, dst)
    x, src, dst = _rec_inputs()

    def _L0_gnn_setup():
        import jax, jax.numpy as jnp
        import numpy as np
        N_NODES = 50000
        N_EDGES = 6250
        IN_DIM = 512
        OUT_DIM = 512
        key = jax.random.key(seed)
        k1, k2, k3, k4 = jax.random.split(key, 4)
        x = jax.random.normal(k1, (N_NODES, IN_DIM), dtype=jnp.float32)
        edge_index = jax.random.randint(k2, (2, N_EDGES), 0, N_NODES, dtype=jnp.int64)
        W = jax.random.normal(k3, (OUT_DIM, IN_DIM), dtype=jnp.float32) / np.sqrt(IN_DIM)
        b = jax.random.normal(k4, (OUT_DIM,), dtype=jnp.float32) * 0.01
        return {'x': x, 'edge_index': edge_index, 'W': W, 'b': b}
    _L0_gnn_all = _L0_gnn_setup()
    _L0_gnn_in = {k: v for k, v in _L0_gnn_all.items() if k in ('W', 'b')}
    del _L0_gnn_all

    def _L0_ffn_setup():
        import jax, jax.numpy as jnp
        import numpy as np
        H = 512
        F = 32
        E = 16
        SHARED = 2
        TOP_K = 4
        B, S = (2, 32)

        def _mlp(x, w1, b1, w2, b2):
            return jax.nn.gelu(x @ w1 + b1, approximate=False) @ w2 + b2
        key = jax.random.key(seed)
        ks = jax.random.split(key, 10)
        sc = 0.02
        return {'hidden_states': jax.random.normal(ks[0], (B, S, H), dtype=jnp.float32), 'gate_w': jax.random.normal(ks[1], (E, H), dtype=jnp.float32) * sc, 're_w1': jax.random.normal(ks[2], (E, H, F), dtype=jnp.float32) * sc, 're_b1': jnp.zeros((E, F), dtype=jnp.float32), 're_w2': jax.random.normal(ks[3], (E, F, H), dtype=jnp.float32) * sc, 're_b2': jnp.zeros((E, H), dtype=jnp.float32), 'se_w1': jax.random.normal(ks[4], (SHARED, H, F), dtype=jnp.float32) * sc, 'se_b1': jnp.zeros((SHARED, F), dtype=jnp.float32), 'se_w2': jax.random.normal(ks[5], (SHARED, F, H), dtype=jnp.float32) * sc, 'se_b2': jnp.zeros((SHARED, H), dtype=jnp.float32)}
    _L0_ffn_all = _L0_ffn_setup()
    _L0_ffn_in = {k: v for k, v in _L0_ffn_all.items() if k in ('gate_w', 're_w1', 're_b1', 're_w2', 're_b2', 'se_w1', 'se_b1', 'se_w2', 'se_b2')}
    del _L0_ffn_all
    return {'x': x, 'src': src, 'dst': dst, 'L0_gnn_W': _L0_gnn_in['W'], 'L0_gnn_b': _L0_gnn_in['b'], 'L0_ffn_gate_w': _L0_ffn_in['gate_w'], 'L0_ffn_re_w1': _L0_ffn_in['re_w1'], 'L0_ffn_re_b1': _L0_ffn_in['re_b1'], 'L0_ffn_re_w2': _L0_ffn_in['re_w2'], 'L0_ffn_re_b2': _L0_ffn_in['re_b2'], 'L0_ffn_se_w1': _L0_ffn_in['se_w1'], 'L0_ffn_se_b1': _L0_ffn_in['se_b1'], 'L0_ffn_se_w2': _L0_ffn_in['se_w2'], 'L0_ffn_se_b2': _L0_ffn_in['se_b2']}

def reference(x, src, dst, L0_gnn_W, L0_gnn_b, L0_ffn_gate_w, L0_ffn_re_w1, L0_ffn_re_b1, L0_ffn_re_w2, L0_ffn_re_b2, L0_ffn_se_w1, L0_ffn_se_b1, L0_ffn_se_w2, L0_ffn_se_b2):
    import jax
    import jax.numpy as jnp

    def _L0_gnn_ref(x, edge_index, W, b):
        import jax, jax.numpy as jnp
        import numpy as np
        N_NODES = 50000
        N_EDGES = 6250
        IN_DIM = 512
        OUT_DIM = 512
        n = x.shape[0]
        loops = jnp.arange(n, dtype=edge_index.dtype)
        row = jnp.concatenate([edge_index[0], loops])
        col = jnp.concatenate([edge_index[1], loops])
        deg = jax.ops.segment_sum(jnp.ones(row.shape[0], dtype=x.dtype), row, num_segments=n)
        dis = jax.lax.rsqrt(deg)
        norm = dis[row] * dis[col]
        h = x @ W.T + b
        out = jax.ops.segment_sum(norm[:, None] * h[row], col, num_segments=n)
        return jax.nn.relu(out)

    def _L0_ffn_ref(hidden_states, gate_w, re_w1, re_b1, re_w2, re_b2, se_w1, se_b1, se_w2, se_b2):
        import jax, jax.numpy as jnp
        import numpy as np
        H = 512
        F = 32
        E = 16
        SHARED = 2
        TOP_K = 4
        B, S = (2, 32)

        def _mlp(x, w1, b1, w2, b2):
            return jax.nn.gelu(x @ w1 + b1, approximate=False) @ w2 + b2
        b, s, h = hidden_states.shape
        x = hidden_states.reshape(-1, h)
        gate_probs = jax.nn.softmax(x @ gate_w.T, axis=-1)
        top_v, top_i = jax.lax.top_k(gate_probs, TOP_K)
        top_v = jax.nn.softmax(top_v, axis=-1)
        combine = jnp.einsum('tk,tke->te', top_v, jax.nn.one_hot(top_i, E, dtype=x.dtype))
        routed = jnp.zeros_like(x)
        for e in range(E):
            routed = routed + combine[:, e:e + 1] * _mlp(x, re_w1[e], re_b1[e], re_w2[e], re_b2[e])
        shared = jnp.zeros_like(x)
        for j in range(SHARED):
            shared = shared + _mlp(x, se_w1[j], se_b1[j], se_w2[j], se_b2[j])
        shared = shared / SHARED
        return (routed + shared).reshape(b, s, h)
    edge_index = jnp.stack([src, dst])
    x = x + _L0_gnn_ref(_layernorm(x, axis=-1), edge_index, L0_gnn_W, L0_gnn_b)
    x = x + _L0_ffn_ref(_layernorm(x, axis=-1)[None], L0_ffn_gate_w, L0_ffn_re_w1, L0_ffn_re_b1, L0_ffn_re_w2, L0_ffn_re_b2, L0_ffn_se_w1, L0_ffn_se_b1, L0_ffn_se_w2, L0_ffn_se_b2)[0]
    return x

_drawn_inputs = setup_inputs


def setup_inputs(seed=0):
    import zlib

    import numpy as np

    out = dict(_drawn_inputs(seed))
    spreads = {'L0_ffn_re_b1': (0.0, 0.8),
     'L0_ffn_re_b2': (0.0, 0.1),
     'L0_ffn_se_b1': (0.0, 0.8),
     'L0_ffn_se_b2': (0.0, 0.1)}
    factors = {'L0_gnn_b': 8.0,
     'L0_ffn_re_w1': 4.906,
     'L0_ffn_re_w2': 4.595,
     'L0_ffn_se_w1': 3.479,
     'L0_ffn_se_w2': 3.27}
    for name, (base, spread) in spreads.items():
        noise = np.random.default_rng([zlib.crc32(name.encode()), seed]).standard_normal(out[name].shape)
        drawn = base * np.exp(spread * noise) if base else spread * noise
        out[name] = jnp.asarray(drawn.astype(out[name].dtype))
    for name, factor in factors.items():
        out[name] = (out[name] * factor).astype(out[name].dtype)
    return out
```

```python
from contextlib import ExitStack

import concourse.bass as bass
from concourse import mybir

F32 = mybir.dt.float32
F32R = mybir.dt.float32r
BF16 = mybir.dt.bfloat16
I32 = mybir.dt.int32
U32 = mybir.dt.uint32
ALU = mybir.AluOpType
ACT = mybir.ActivationFunctionType
AX_X = mybir.AxisListType.X

EPS = 1e-5
ROUND = 12582912.0
NOWHERE = 1048576.0
LOWEST = -3.0e38


def gnn_moe(nc, x, src, dst, gnn_w, gnn_b, gate_w, re_w1, re_b1, re_w2, re_b2, se_w1, se_b1, se_w2, se_b2, out):
    N, D = x.shape
    NE = src.shape[0]
    E, _, F = re_w1.shape
    SH = se_w1.shape[0]
    TOP = 4
    KC = D // 128
    J = 4
    P = 125
    T = N // P
    G = T // J
    GN = P * J
    NB = NE // P
    NS = NB // J
    MC = E * F // 128
    SF = SH * F
    SH0 = 128 - SF
    LN = 12
    XS = 4
    HALF = 112
    assert N == P * T and T == J * G and NE == P * NB and NB == J * NS and E * F == 128 * MC and SH == 2

    x_v = x.rearrange("(p t) d -> p (t d)", t=T)
    out_v = out.rearrange("(p t) d -> p (t d)", t=T)
    table = nc.dram_tensor("edge_sums", [NE, D], F32, kind="Internal").ap()

    ctx = ExitStack()
    with ctx:
        def sb(name, shape, dt=F32, scope=ctx):
            return scope.enter_context(nc.sbuf_tensor(name, shape, dt))

        def sem(name):
            return ctx.enter_context(nc.semaphore(name))

        ps = ctx.enter_context(nc.psum_tensor("ps", [128, 8, 512], F32))

        x_tile = [sb(f"x_tile{i}", [128, J, D]) for i in range(XS)]
        wg_hi, wg_lo = sb("wg_hi", [128, KC, D], F32R), sb("wg_lo", [128, KC, D], F32R)
        w1_hi, w1_lo = sb("w1_hi", [128, KC, MC + 1, 128], F32R), sb("w1_lo", [128, KC, MC + 1, 128], F32R)
        w2_hi, w2_lo = sb("w2_hi", [128, MC + 1, D], F32R), sb("w2_lo", [128, MC + 1, D], F32R)
        b1 = sb("b1", [128, MC + 1])
        ident = sb("ident", [128, 128])
        expert_of = sb("expert_of", [128, MC, 128], F32R)
        neg_half = sb("neg_half", [128, 80])
        half, inv_128, eps4, zero4 = sb("half", [128, J]), sb("inv_128", [128, J]), sb("eps4", [128, J]), sb("zero4", [128, J])
        dis = sb("dis", [128, T])
        dis2, dis2x2 = sb("dis2", [128, T]), sb("dis2x2", [128, T])
        s_node = sb("s_node", [128, T])
        table_row = sb("table_row", [128, T], U32)
        dst_bc = sb("dst_bc", [128, NE], I32)
        node_f = sb("node_f", [128, 2, NB])
        node_u = sb("node_u", [128, 2, NB], U32)
        norm = sb("norm", [128, NB])
        prior_row = sb("prior_row", [128, NB], U32)

        early = ExitStack()
        idx_rows = sb("idx_rows", [NB, 2, P], I32, early)
        idx_rows_f = sb("idx_rows_f", [NB, 2, P], F32, early)
        src_bc = sb("src_bc", [128, NE], I32, early)
        at_ge = sb("at_ge", [128, NE], F32, early)
        at_src = sb("at_src", [128, NE], F32, early)
        at_dst = sb("at_dst", [128, NE], F32, early)
        a_src = sb("a_src", [128, NB, P], BF16, early)
        b_src = sb("b_src", [128, NB, T], BF16, early)
        a_dst = sb("a_dst", [128, NB, P], F32, early)
        b_dst = sb("b_dst", [128, NB, T], F32, early)
        b_norm = sb("b_norm", [128, NB, T], F32, early)
        picked = sb("picked", [128, NB, T], F32, early)
        row_iota = sb("row_iota", [128, 128], I32, early)
        row_iota_f = sb("row_iota_f", [128, 128], F32, early)
        part80 = sb("part80", [128, 2], I32, early)
        part80_f = sb("part80_f", [128, 2], F32, early)
        quot = sb("quot", [128, 2, NB], F32, early)
        quot_r = sb("quot_r", [128, 2, NB], F32, early)
        rest = sb("rest", [128, 2, NB], F32, early)
        deg = sb("deg", [128, T], F32, early)
        dis_end = sb("dis_end", [128, 2, NB], F32, early)
        no_edge = sb("no_edge", [128, T], F32, early)
        expert_f = sb("expert_f", [128, MC, 128], F32, early)
        earlier = sb("earlier", [128, GN], F32, early)
        before = sb("before", [128, NB], F32, early)
        repeat = sb("repeat", [128, GN], F32, early)
        edge_row = sb("edge_row", [128, NB], I32, early)
        first_row = sb("first_row", [128, NB], F32, early)
        kept = sb("kept", [128, NS, T], F32, early)
        newest = sb("newest", [128, NS, T], F32, early)
        prior_f = sb("prior_f", [128, 3, NB], F32, early)
        early.close()

        edges = ExitStack()
        same = [sb(f"same{i}", [128, J, GN], F32R, edges) for i in range(2)]
        e_hi = sb("e_hi", [128, J, D], F32R, edges)
        e_lo = sb("e_lo", [128, J, D], F32R, edges)
        prior = sb("prior", [128, J, D], F32, edges)
        summed = [sb(f"summed{i}", [128, J, D], F32, edges) for i in range(2)]
        e_stats = sb("e_stats", [128, J, 6], F32, edges)
        e_mv = sb("e_mv", [128, J, 2], F32, edges)
        e_sc = sb("e_sc", [128, 6, J], F32, edges)
        wn = sb("wn", [128, KC, D], F32, edges)
        gate_n = sb("gate_n", [E, D], F32, edges)
        w1_n = sb("w1_n", [128, KC, MC + 1, 128], F32, edges)
        w2_n = sb("w2_n", [128, MC + 1, D], F32, edges)
        gb = sb("gb", [128, KC], F32, edges)
        w_sum = sb("w_sum", [128, KC], F32, edges)
        beta = sb("beta", [128, KC], F32, edges)
        edges.close()

        u_tile = sb("u_tile", [128, J, D])
        z_tile = sb("z_tile", [128, J, D])
        zT_hi, zT_lo = sb("zT_hi", [128, J, KC, P], F32R), sb("zT_lo", [128, J, KC, P], F32R)
        xn_tile = sb("xn_tile", [128, J, D])
        xT_hi, xT_lo = sb("xT_hi", [128, KC, J, P], F32R), sb("xT_lo", [128, KC, J, P], F32R)
        hid = sb("hid", [128, MC + 1, GN])
        h_hi, h_lo = sb("h_hi", [128, MC + 1, GN], F32R), sb("h_lo", [128, MC + 1, GN], F32R)
        logits_f = sb("logits_f", [128, GN])
        row_idx = sb("row_idx", [128, J], U32)
        st1, sc1 = sb("st1", [128, J, 6]), sb("sc1", [128, LN, J])
        st2, sc2 = sb("st2", [128, J, 6]), sb("sc2", [128, LN, J])
        lg = sb("lg", [128, J, E + TOP])
        top8 = sb("top8", [128, J, 8])
        left = sb("left", [128, J, E + TOP])
        gt = sb("gt", [128, 12, J, E])
        gs = sb("gs", [128, 5, J])
        comb = sb("comb", [128, J, E + SH])

        idx_in, bc_in, w_in, w1_in, w2_in = sem("idx_in"), sem("bc_in"), sem("w_in"), sem("w1_in"), sem("w2_in")
        consts, setup, idx_tr = sem("consts"), sem("setup"), sem("idx_tr")
        flagged, newest_ready = sem("flagged"), sem("newest_ready")
        counted, dis_ready, looked, weighted = sem("counted"), sem("dis_ready"), sem("looked"), sem("weighted")
        w2_clear, w1_clear = sem("w2_clear"), sem("w1_clear")
        wprep, w_tr, w_hi = sem("wprep"), sem("w_tr"), sem("w_hi")
        xe_in = [sem(f"xe_in{s}") for s in range(NS)]
        prior_clear, e_dve, e_mv_ready = sem("prior_clear"), sem("e_dve"), sem("e_mv_ready")
        e_scalars, e_normed, e_split_hi, e_split_lo = sem("e_scalars"), sem("e_normed"), sem("e_split_hi"), sem("e_split_lo")
        same_ready, e_summed, prior_in, sum_ready, table_in = (
            sem("same_ready"), sem("e_summed"), sem("prior_in"), sem("sum_ready"), sem("table_in"))
        main_clear = sem("main_clear")
        x_loaded = [sem(f"x_loaded{i}") for i in range(XS)]
        stored = [sem(f"stored{i}") for i in range(XS)]
        u_zeroed, u_in, idx_copied = sem("u_zeroed"), sem("u_in"), sem("idx_copied")
        st1_done, ln1_done = sem("st1_done"), sem("ln1_done")
        z_scaled, z_ready, z_turned = sem("z_scaled"), sem("z_ready"), sem("z_turned")
        zT_hi_ok, zT_lo_ok = sem("zT_hi_ok"), sem("zT_lo_ok")
        gnn_done, x1_done = sem("gnn_done"), sem("x1_done")
        st2_done, ln2_done = sem("st2_done"), sem("ln2_done")
        xn_ready, xn_turned = sem("xn_ready"), sem("xn_turned")
        xT_hi_ok, xT_lo_ok = sem("xT_hi_ok"), sem("xT_lo_ok")
        ffn1_done, act_done = sem("ffn1_done"), sem("act_done")
        lg_turned, gated, tanh_done = sem("lg_turned"), sem("gated"), sem("tanh_done")
        comb_turned, h_hi_ok, h_lo_ok = sem("comb_turned"), sem("h_hi_ok"), sem("h_lo_ok")
        spread, weighed = sem("spread"), sem("weighed")
        ffn2_done, out_ready = sem("ffn2_done"), sem("out_ready")
        GATE = 25

        ACC = [0, 1, 2]
        BANK = [ACC[i] for i in (0, 1, 2, 0, 1, 2, 0, 1, 2, 0, 1, 2, 1)]
        TR = [3, 4]
        SPREAD = [5, 6]
        SMALL = 7

        def after(eng, semaphore, value):
            if isinstance(value, int) and value <= 0:
                return
            eng.wait_ge(semaphore, value)

        def f32(ap):
            return ap.bitcast(F32)

        def steps(k, u):
            return XS * k + u, u % XS, k + u // XS

        def pipeline(eng, first, body, last):
            first()
            for u in range(2):
                body(0, u)
            with eng.Fori(0, (G - 4) // XS) as k:
                for u in range(2, 2 + XS):
                    body(k, u)
            for u in range(G - 2, G):
                last(0, u)

        def passes(hi_l, lo_l, hi_r, lo_r):
            return ((hi_l, hi_r), (lo_l, hi_r), (hi_l, lo_r))

        block = ctx.enter_context(nc.Block())

        @block.sync
        def _(sp):
            sp.dma_start(idx_rows[:, 0, :], src.rearrange("(b q) -> b q", q=P)).then_inc(idx_in, 16)
            sp.dma_start(idx_rows[:, 1, :], dst.rearrange("(b q) -> b q", q=P)).then_inc(idx_in, 16)
            sp.dma_start(src_bc[0:P, :], src.rearrange("(a e) -> a e", a=1).to_broadcast((P, NE))).then_inc(bc_in, 16)
            sp.dma_start(dst_bc[0:P, :], dst.rearrange("(a e) -> a e", a=1).to_broadcast((P, NE))).then_inc(bc_in, 16)
            sp.wait_ge(main_clear, 1)
            sp.dma_start(wn[:, :, :], gnn_w.rearrange("(c p) i -> p c i", p=128)).then_inc(w_in, 16)
            sp.dma_start(gb[:, :], gnn_b.rearrange("(c p) -> p c", p=128), allow_slow_non_contiguous=True).then_inc(w_in, 16)
            sp.dma_start(gate_n[:, :], gate_w).then_inc(w_in, 16)
            sp.dma_start(b1[:, 0:MC], re_b1.rearrange("(m a) f -> (a f) m", m=MC), allow_slow_non_contiguous=True).then_inc(w_in, 16)
            sp.dma_start(b1[SH0:128, MC:MC + 1], se_b1.rearrange("j (f a) -> (j f) a", a=1), allow_slow_non_contiguous=True).then_inc(w_in, 16)
            sp.wait_ge(w1_clear, 1)
            for c in range(KC):
                rows = slice(c * 128, (c + 1) * 128)
                sp.dma_start(w1_n[:, c, 0:MC, :].rearrange("p m (a f) -> p (m a) f", f=F),
                             re_w1[:, rows, :].rearrange("e p f -> p e f")).then_inc(w1_in, 16)
                sp.dma_start(w1_n[:, c, MC, SH0:128].rearrange("p (j f) -> p j f", f=F),
                             se_w1[:, rows, :].rearrange("j p f -> p j f")).then_inc(w1_in, 16)
            sp.dma_start(w2_n[:, 0:MC, :], re_w2.rearrange("(m a) f d -> (a f) m d", m=MC)).then_inc(w2_in, 16)
            sp.wait_ge(w2_clear, 1)
            sp.dma_start(w2_n[0:E, MC, :], re_b2).then_inc(w2_in, 16)
            sp.dma_start(w2_n[E:E + SH, MC, :], se_b2).then_inc(w2_in, 16)
            sp.dma_start(w2_n[SH0:128, MC, :], se_w2.rearrange("j f d -> (j f) d")).then_inc(w2_in, 16)

            for s in range(NS):
                sp.wait_ge(sum_ready, J * (s + 1))
                rows_v = table[s * GN:(s + 1) * GN, :].rearrange("(q j) d -> q (j d)", j=J)
                for rows in (slice(0, HALF), slice(HALF, P)):
                    sp.dma_start(rows_v[rows, :], summed[s % 2][rows, :, :].rearrange("q j d -> q (j d)")).then_inc(table_in, 16)

            def load(k, u):
                g, slot, rnd = steps(k, u)
                after(sp, stored[slot], 32 * rnd)
                for rows in (slice(0, HALF), slice(HALF, P)):
                    sp.dma_start(x_tile[slot][rows, :, :].rearrange("p j d -> p (j d)"),
                                 x_v[rows, bass.ds(g * J * D, J * D)]).then_inc(x_loaded[slot], 16)

            def store(k, u):
                g, slot, rnd = steps(k, u)
                sp.wait_ge(out_ready, J * (g + 1))
                for rows in (slice(0, HALF), slice(HALF, P)):
                    sp.dma_start(out_v[rows, bass.ds(g * J * D, J * D)],
                                 x_tile[slot][rows, :, :].rearrange("p j d -> p (j d)")).then_inc(stored[slot], 16)

            def first():
                for u in range(1, XS):
                    sp.wait_ge(e_split_lo, u + 1)
                    load(0, u)
                sp.wait_ge(e_split_lo, NS)
                load(0, 0)

            def body(k, u):
                store(k, u)
                load(k, u + XS)

            first()
            with sp.Fori(0, (G - XS) // XS) as k:
                for u in range(XS):
                    body(k, u)
            for u in range(G - XS, G):
                store(0, u)
            for slot in range(XS):
                sp.wait_ge(stored[slot], 32 * len(range(slot, G, XS)))

        @block.gpsimd
        def _(pool):
            gp = nc.gpsimd
            gp.memset(ident[:, :], 0.0).then_inc(consts, 1)
            gp.memset(expert_f[:, :, :], 0.0).then_inc(consts, 1)
            gp.memset(earlier[:, :], 1.0).then_inc(consts, 1)
            gp.memset(neg_half[:, :], -0.5).then_inc(consts, 1)
            gp.iota(row_iota[:, :], [[1, 128]], base=0, channel_multiplier=0).then_inc(consts, 1)
            gp.iota(part80[:, :], [[T, 2]], base=0, channel_multiplier=T).then_inc(consts, 1)
            gp.memset(half[:, :], 0.5).then_inc(consts, 1)
            gp.memset(inv_128[:, :], 4.0 / D).then_inc(consts, 1)
            gp.memset(eps4[:, :], 4.0 * EPS).then_inc(consts, 1)
            gp.memset(zero4[:, :], 0.0).then_inc(consts, 1)
            pool.wait_ge(consts, 10)
            gp.affine_select(out=ident[:, :], in_=ident[:, :], compare_op=ALU.not_equal, fill=1.0, base=0,
                             pattern=[[-1, 128]], channel_multiplier=1).then_inc(consts, 1)
            gp.affine_select(out=expert_f[:, :, :].rearrange("p m (a f) -> p m a f", f=F),
                             in_=expert_f[:, :, :].rearrange("p m (a f) -> p m a f", f=F),
                             compare_op=ALU.not_equal, fill=1.0, base=0,
                             pattern=[[-(128 // F), MC], [-1, 128 // F], [0, F]], channel_multiplier=1).then_inc(consts, 1)
            gp.affine_select(out=earlier[0:P, (J - 1) * P:J * P], in_=earlier[0:P, (J - 1) * P:J * P], compare_op=ALU.is_gt,
                             fill=0.0, base=0, pattern=[[-1, P]], channel_multiplier=1).then_inc(consts, 1)
            gp.iota(edge_row[:, :], [[GN, NS], [1, J]], base=1, channel_multiplier=J).then_inc(consts, 1)
            pool.wait_ge(consts, 14)
            gp.tensor_copy(expert_of[:, :, :], expert_f[:, :, :]).then_inc(consts, 1)

            last_row = pool.snap(pool.to_reg(NE - 1))

            def gather_edges(s):
                if s >= XS:
                    pool.wait_ge(e_split_lo, s - XS + 1)
                for i in range(J):
                    gp.indirect_dma_start(x_tile[s % XS][0:P, i, :], None, x,
                                          bass.IndirectOffsetOnAxis(node_u[0:P, 0, J * s + i:J * s + i + 1], 0),
                                          bounds_check=N - 1, oob_is_err=False).then_inc(xe_in[s], 16)

            pool.wait_ge(setup, 3)
            for s in range(XS):
                gather_edges(s)
            pool.wait_ge(counted, 2)
            gp.tensor_tensor(dis[0:P, :], deg[0:P, :], neg_half[0:P, :], ALU.pow).then_inc(dis_ready, 1)

            def edge_scalars(s):
                pool.wait_ge(e_mv_ready, J * (s + 1))
                if s:
                    pool.wait_ge(e_normed, s)
                at = 5 * s
                gp.tensor_scalar(e_sc[0:P, 0, :], e_mv[0:P, :, 1], EPS, None, ALU.add).then_inc(e_scalars, 1)
                pool.wait_ge(e_scalars, at + 1)
                gp.tensor_tensor(e_sc[0:P, 1, :], e_sc[0:P, 0, :], neg_half[0:P, 0:J], ALU.pow).then_inc(e_scalars, 1)
                pool.wait_ge(e_scalars, at + 2)
                gp.tensor_tensor(e_sc[0:P, 2, :], e_sc[0:P, 1, :], norm[0:P, J * s:J * s + J], ALU.mult).then_inc(e_scalars, 1)
                pool.wait_ge(e_scalars, at + 3)
                gp.tensor_tensor(e_sc[0:P, 3, :], e_sc[0:P, 2, :], e_mv[0:P, :, 0], ALU.mult).then_inc(e_scalars, 1)
                pool.wait_ge(e_scalars, at + 4)
                gp.tensor_scalar(e_sc[0:P, 4, :], e_sc[0:P, 3, :], -1.0, None, ALU.mult).then_inc(e_scalars, 1)

            def gather_prior(s):
                gp.memset(prior[0:P, :, :], 0.0).then_inc(prior_clear, 1)
                pool.wait_ge(prior_clear, s)
                pool.wait_ge(table_in, 32 * s)
                for i in range(J):
                    gp.indirect_dma_start(prior[0:P, i, :], None, table[0:s * GN, :],
                                          bass.IndirectOffsetOnAxis(prior_row[0:P, J * s + i:J * s + i + 1], 0),
                                          bounds_check=s * GN - 1, oob_is_err=False).then_inc(prior_in, 16)

            edge_scalars(0)
            edge_scalars(1)
            for s in range(NS):
                if s + 2 < NS:
                    edge_scalars(s + 2)
                if s + XS < NS:
                    gather_edges(s + XS)
                if s:
                    pool.wait_ge(sum_ready, J * s)
                    gather_prior(s)

            def half_rstd(stats, t, done, at):
                tt = gp.tensor_tensor
                tt(t[0:P, 0, :], stats[0:P, :, 1], stats[0:P, :, 4], ALU.add).then_inc(done, 1)
                tt(t[0:P, 1, :], stats[0:P, :, 1], stats[0:P, :, 4], ALU.subtract).then_inc(done, 1)
                tt(t[0:P, 2, :], stats[0:P, :, 2], stats[0:P, :, 5], ALU.add).then_inc(done, 1)
                pool.wait_ge(done, at + 3)
                tt(t[0:P, 3, :], t[0:P, 1, :], t[0:P, 1, :], ALU.mult).then_inc(done, 1)
                tt(t[0:P, 4, :], t[0:P, 2, :], inv_128[0:P, :], ALU.mult).then_inc(done, 1)
                tt(t[0:P, 5, :], t[0:P, 0, :], half[0:P, :], ALU.mult).then_inc(done, 1)
                pool.wait_ge(done, at + 6)
                tt(t[0:P, 6, :], t[0:P, 3, :], t[0:P, 4, :], ALU.add).then_inc(done, 1)
                pool.wait_ge(done, at + 7)
                tt(t[0:P, 7, :], t[0:P, 6, :], eps4[0:P, :], ALU.add).then_inc(done, 1)
                pool.wait_ge(done, at + 8)
                tt(t[0:P, 8, :], t[0:P, 7, :], neg_half[0:P, 0:J], ALU.pow).then_inc(done, 1)

            def ln1(k, u):
                g, _, _ = steps(k, u)
                cols = bass.ds(g * J, J)
                at = LN * g
                after(pool, z_scaled, J * g)
                pool.wait_ge(st1_done, J * (g + 1))
                half_rstd(st1, sc1, ln1_done, at)
                pool.wait_ge(ln1_done, at + 9)
                gp.tensor_tensor(sc1[0:P, 9, :], sc1[0:P, 8, :], dis2x2[0:P, cols], ALU.mult).then_inc(ln1_done, 1)
                pool.wait_ge(ln1_done, at + 10)
                gp.tensor_tensor(sc1[0:P, 10, :], sc1[0:P, 9, :], sc1[0:P, 5, :], ALU.mult).then_inc(ln1_done, 1)
                pool.wait_ge(ln1_done, at + 11)
                pool.wait_ge(idx_copied, g + 1)
                pool.wait_ge(u_zeroed, g + 1)
                gp.tensor_tensor(sc1[0:P, 11, :], s_node[0:P, cols], sc1[0:P, 10, :], ALU.subtract).then_inc(ln1_done, 1)

            def fetch(k, u):
                g, _, _ = steps(k, u)
                after(pool, z_ready, J * g)
                gp.tensor_copy(row_idx[0:P, :], table_row[0:P, bass.ds(g * J, J)]).then_inc(idx_copied, 1)
                gp.memset(u_tile[0:P, :, :], 0.0).then_inc(u_zeroed, 1)
                ln1(k, u)
                for j in range(J):
                    gp.indirect_dma_start(u_tile[0:P, j, :], None, table,
                                          bass.IndirectOffsetOnAxis(row_idx[0:P, j:j + 1], 0),
                                          bounds_check=last_row, oob_is_err=False).then_inc(u_in, 16)

            def ln2(k, u):
                g, _, _ = steps(k, u)
                at = LN * g
                after(pool, xn_ready, J * g)
                pool.wait_ge(st2_done, J * (g + 1))
                half_rstd(st2, sc2, ln2_done, at)
                pool.wait_ge(ln2_done, at + 9)
                gp.tensor_tensor(sc2[0:P, 9, :], sc2[0:P, 8, :], sc2[0:P, 8, :], ALU.add).then_inc(ln2_done, 1)
                pool.wait_ge(ln2_done, at + 10)
                gp.tensor_tensor(sc2[0:P, 10, :], sc2[0:P, 9, :], sc2[0:P, 5, :], ALU.mult).then_inc(ln2_done, 1)
                pool.wait_ge(ln2_done, at + 11)
                gp.tensor_tensor(sc2[0:P, 11, :], zero4[0:P, :], sc2[0:P, 10, :], ALU.subtract).then_inc(ln2_done, 1)

            def first():
                pool.wait_ge(table_in, 32 * NS)
                pool.wait_ge(wprep, 15)
                fetch(0, 0)
                fetch(0, 1)
                ln2(0, 0)

            def body(k, u):
                fetch(k, u + 2)
                ln2(k, u + 1)

            def last(k, u):
                if u + 1 < G:
                    ln2(k, u + 1)

            pipeline(pool, first, body, last)

        @block.scalar
        def _(act):
            sc = nc.scalar

            def split_hi_edges(s):
                x_e = x_tile[s % XS]
                act.wait_ge(e_scalars, 5 * (s + 1))
                for i in range(J):
                    op = sc.activation(x_e[0:P, i, :], x_e[0:P, i, :], ACT.Identity,
                                       bias=e_sc[0:P, 4, i:i + 1], scale=e_sc[0:P, 2, i:i + 1])
                op.then_inc(e_normed, 1)
                act.wait_ge(e_normed, s + 1)
                if s:
                    act.wait_ge(e_summed, J * s)
                sc.activation(e_hi[0:P, :, :], x_e[0:P, :, :], ACT.Copy).then_inc(e_split_hi, 1)

            act.wait_ge(main_clear, 1)
            for s in range(NS):
                split_hi_edges(s)
            act.wait_ge(w_tr, 1)
            for c in range(KC):
                op = sc.activation(wg_hi[:, c, :], ps[:, c, :], ACT.Copy)
            op.then_inc(w_hi, 1)
            act.wait_ge(wprep, 9)
            sc.activation(w1_hi[:, :, :, :], w1_n[:, :, :, :], ACT.Copy).then_inc(w_hi, 1)
            sc.activation(w2_hi[:, :, :], w2_n[:, :, :], ACT.Copy).then_inc(w_hi, 1)

            def scale1(k, u):
                g, slot, _ = steps(k, u)
                act.wait_ge(ln1_done, LN * (g + 1))
                for j in range(J):
                    after(act, z_turned, J * (g - 1) + j + 1)
                    sc.activation(z_tile[0:P, j, :], x_tile[slot][0:P, j, :], ACT.Identity,
                                  bias=sc1[0:P, 11, j:j + 1], scale=sc1[0:P, 9, j:j + 1]).then_inc(z_scaled, 1)

            def scale2(k, u):
                g, slot, _ = steps(k, u)
                act.wait_ge(ln2_done, LN * (g + 1))
                for j in range(J):
                    after(act, xn_turned, J * (g - 1) + j + 1)
                    sc.activation(xn_tile[0:P, j, :], x_tile[slot][0:P, j, :], ACT.Identity,
                                  bias=sc2[0:P, 11, j:j + 1], scale=sc2[0:P, 9, j:j + 1]).then_inc(xn_ready, 1)

            def z_hi(k, u, j):
                g, _, _ = steps(k, u)
                act.wait_ge(z_turned, J * g + j + 1)
                sc.activation(zT_hi[:, j, :, :].rearrange("p c q -> p (c q)"), ps[:, TR[j % 2], 0:KC * P],
                              ACT.Copy).then_inc(zT_hi_ok, 1)

            def xn_hi(k, u, j):
                g, _, _ = steps(k, u)
                act.wait_ge(xn_turned, J * g + j + 1)
                sc.activation(xT_hi[:, :, j, :], ps[:, TR[j % 2], 0:KC * P].rearrange("p (c q) -> p c q", q=P),
                              ACT.Copy).then_inc(xT_hi_ok, 1)

            def gelu(k, u, m):
                g, _, _ = steps(k, u)
                act.wait_ge(ffn1_done, 5 * g + 2 + m)
                after(act, h_lo_ok, 6 * (g - 1) + 3 + m)
                sc.activation(hid[:, m, :], ps[:, BANK[1 + m], 0:GN], ACT.Gelu, bias=b1[:, m:m + 1]).then_inc(act_done, 1)

            def h_high(k, u, m):
                g, _, _ = steps(k, u)
                act.wait_ge(weighed, J * g + m + 1)
                sc.activation(h_hi[:, m, :], hid[:, m, :], ACT.Copy).then_inc(h_hi_ok, 1)

            def tanh(k, u, n):
                g, _, _ = steps(k, u)
                act.wait_ge(gated, GATE * g + (7, 14)[n])
                sc.activation(gt[0:P, (1, 6)[n], :, :], gt[0:P, (0, 5)[n], :, :], ACT.Tanh, scale=0.5).then_inc(tanh_done, 1)

            def first():
                scale1(0, 0)
                for j in range(J):
                    z_hi(0, 0, j)
                scale1(0, 1)
                for j in range(J):
                    z_hi(0, 1, j)
                scale2(0, 0)
                for j in range(J):
                    xn_hi(0, 0, j)

            def body(k, u, more=2):
                g, _, _ = steps(k, u)
                act.wait_ge(ffn1_done, 5 * g + 1)
                after(act, lg_turned, g)
                sc.activation(logits_f[0:E, :], ps[0:E, BANK[0], 0:GN], ACT.Copy).then_inc(act_done, 1)
                after(act, h_lo_ok, 6 * (g - 1) + 1)
                sc.activation(hid[SH0:128, MC, :], ps[SH0:128, BANK[0], 0:GN], ACT.Gelu,
                              bias=b1[SH0:128, MC:MC + 1]).then_inc(act_done, 1)
                act.wait_ge(act_done, 6 * g + 2)
                sc.activation(h_hi[SH0:128, MC, :], hid[SH0:128, MC, :], ACT.Copy).then_inc(h_hi_ok, 1)
                if more == 2:
                    scale1(k, u + 2)
                gelu(k, u, 0)
                tanh(k, u, 0)
                gelu(k, u, 1)
                tanh(k, u, 1)
                gelu(k, u, 2)
                gelu(k, u, 3)
                act.wait_ge(comb_turned, g + 1)
                sc.activation(h_hi[0:E + SH, MC, :], ps[0:E + SH, SMALL, 0:GN], ACT.Copy).then_inc(h_hi_ok, 1)
                if more == 2:
                    z_hi(k, u + 2, 0)
                h_high(k, u, 0)
                h_high(k, u, 1)
                if more == 2:
                    z_hi(k, u + 2, 1)
                h_high(k, u, 2)
                h_high(k, u, 3)
                if more == 2:
                    z_hi(k, u + 2, 2)
                    z_hi(k, u + 2, 3)
                if more:
                    scale2(k, u + 1)
                    for j in range(J):
                        xn_hi(k, u + 1, j)

            pipeline(act, first, body, lambda k, u: body(k, u, more=G - 1 - u))

        @block.vector
        def _(dve):
            v = nc.vector

            dve.wait_ge(idx_in, 32)
            v.tensor_copy(idx_rows_f[:, :, :], idx_rows[:, :, :]).then_inc(setup, 1)
            dve.wait_ge(idx_tr, 1)
            v.tensor_copy(node_f[0:P, :, :], ps[0:P, 6, 0:2 * NB].rearrange("p (a b) -> p a b", a=2)).then_inc(setup, 1)
            v.tensor_copy(node_u[0:P, :, :], ps[0:P, 6, 0:2 * NB].rearrange("p (a b) -> p a b", a=2)).then_inc(setup, 1)
            dve.wait_ge(setup, 3)
            v.tensor_scalar(quot_r[0:P], node_f[0:P], -(T - 1) / 2.0, 1.0 / T, ALU.add, ALU.mult).then_inc(setup, 1)
            dve.wait_ge(setup, 4)
            v.tensor_scalar(quot[0:P], quot_r[0:P], ROUND, ROUND, ALU.add, ALU.subtract).then_inc(setup, 1)
            dve.wait_ge(setup, 5)
            v.scalar_tensor_tensor(out=rest[0:P], in0=quot[0:P], scalar=-float(T), in1=node_f[0:P],
                                   op0=ALU.mult, op1=ALU.add).then_inc(setup, 1)
            dve.wait_ge(consts, 10)
            v.tensor_copy(row_iota_f[:, :], row_iota[:, :]).then_inc(setup, 1)
            v.tensor_copy(part80_f[:, :], part80[:, :]).then_inc(setup, 1)
            v.memset(kept[:, 0, :], 0.0).then_inc(setup, 1)
            dve.wait_ge(setup, 9)

            def hot(out_ap, value, a, width):
                return v.tensor_tensor(out_ap, value[0:P, a, :].unsqueeze(2).to_broadcast((P, NB, width)),
                                       row_iota_f[0:P, 0:width].unsqueeze(1).to_broadcast((P, NB, width)), ALU.is_equal)

            hot(a_src[0:P], quot, 0, P).then_inc(setup, 1)
            hot(b_src[0:P], rest, 0, T).then_inc(setup, 1)
            dve.wait_ge(bc_in, 32)
            v.tensor_scalar(at_ge[0:P, :], src_bc[0:P, :], part80_f[0:P, 0:1], None, ALU.is_ge).then_inc(setup, 1)
            dve.wait_ge(setup, 12)
            v.scalar_tensor_tensor(out=at_src[0:P, :], in0=src_bc[0:P, :], scalar=part80_f[0:P, 1:2], in1=at_ge[0:P, :],
                                   op0=ALU.is_lt, op1=ALU.mult).then_inc(setup, 1)
            dve.wait_ge(counted, 1)
            v.tensor_scalar(deg[0:P, :], ps[0:P, 7, 0:T], 1.0, None, ALU.add).then_inc(counted, 1)
            dve.wait_ge(setup, 13)
            v.tensor_scalar(at_ge[0:P, :], dst_bc[0:P, :], part80_f[0:P, 0:1], None, ALU.is_ge).then_inc(setup, 1)
            dve.wait_ge(setup, 14)
            v.scalar_tensor_tensor(out=at_dst[0:P, :], in0=dst_bc[0:P, :], scalar=part80_f[0:P, 1:2], in1=at_ge[0:P, :],
                                   op0=ALU.is_lt, op1=ALU.mult).then_inc(setup, 1)
            hot(a_dst[0:P], quot, 1, P).then_inc(setup, 1)
            hot(b_dst[0:P], rest, 1, T).then_inc(setup, 1)
            dve.wait_ge(setup, 17)
            for a, onehot in ((0, b_src[0:P]), (1, b_dst[0:P])):
                dve.wait_ge(looked, a + 1)
                if a:
                    dve.wait_ge(weighted, 2)
                v.tensor_tensor(picked[0:P].rearrange("p (k b) t -> p k b t", k=4),
                                ps[0:P, 4 * a:4 * a + 4, 0:NB // 4 * T].rearrange("p k (b t) -> p k b t", t=T),
                                onehot.rearrange("p (k b) t -> p k b t", k=4), ALU.mult).then_inc(weighted, 1)
                dve.wait_ge(weighted, 2 * a + 1)
                v.tensor_reduce(dis_end[0:P, a, :], picked[0:P], AX_X, ALU.add).then_inc(weighted, 1)
            dve.wait_ge(weighted, 4)
            v.tensor_tensor(norm[0:P, :], dis_end[0:P, 0, :], dis_end[0:P, 1, :], ALU.mult).then_inc(setup, 1)
            dve.wait_ge(setup, 18)
            v.tensor_tensor(b_norm[0:P], b_dst[0:P], norm[0:P, :].unsqueeze(2).to_broadcast((P, NB, T)), ALU.mult).then_inc(setup, 1)
            dve.wait_ge(dis_ready, 1)
            v.tensor_tensor(dis2[0:P, :], dis[0:P, :], dis[0:P, :], ALU.mult).then_inc(setup, 1)
            dve.wait_ge(consts, 15)
            for b in range(NB):
                i, at = b % J, b // J * GN
                w = (i + 1) * P
                if b:
                    dve.wait_ge(flagged, b)
                v.scalar_tensor_tensor(out=repeat[0:P, 0:w], in0=dst_bc[0:P, at:at + w], scalar=node_f[0:P, 1, b:b + 1],
                                       in1=earlier[0:P, GN - w:GN], op0=ALU.is_equal, op1=ALU.mult,
                                       accum_out=before[0:P, b:b + 1]).then_inc(flagged, 1)
            dve.wait_ge(flagged, NB)
            v.scalar_tensor_tensor(out=first_row[0:P, :], in0=before[0:P, :], scalar=0.0, in1=edge_row[0:P, :],
                                   op0=ALU.is_equal, op1=ALU.mult).then_inc(flagged, 1)
            dve.wait_ge(flagged, NB + 1)
            v.tensor_tensor(picked[0:P], b_dst[0:P], first_row[0:P, :].unsqueeze(2).to_broadcast((P, NB, T)),
                            ALU.mult).then_inc(flagged, 1)
            dve.wait_ge(dis_ready, 1)
            dve.wait_ge(counted, 3)
            v.tensor_tensor(s_node[0:P, :], ps[0:P, 0, 0:T], dis2[0:P, :], ALU.add).then_inc(weighted, 1)
            v.tensor_tensor(dis2x2[0:P, :], dis2[0:P, :], dis2[0:P, :], ALU.add).then_inc(weighted, 1)
            dve.wait_ge(counted, 4)
            v.tensor_copy(newest[0:P, 0, :], ps[0:P, 1, 0:T]).then_inc(newest_ready, 1)
            for s in range(1, NS):
                dve.wait_ge(newest_ready, 2 * s - 1)
                here = ps[0:P, 1, s * T:(s + 1) * T]
                v.scalar_tensor_tensor(out=kept[0:P, s, :], in0=here, scalar=0.0, in1=newest[0:P, s - 1, :],
                                       op0=ALU.is_equal, op1=ALU.mult).then_inc(newest_ready, 1)
                dve.wait_ge(newest_ready, 2 * s)
                v.tensor_tensor(newest[0:P, s, :], here, kept[0:P, s, :], ALU.add).then_inc(newest_ready, 1)
            dve.wait_ge(newest_ready, 2 * NS - 1)
            v.tensor_scalar(no_edge[0:P, :], newest[0:P, NS - 1, :], 0.0, NOWHERE, ALU.is_equal, ALU.mult).then_inc(setup, 1)
            dve.wait_ge(setup, 21)
            v.scalar_tensor_tensor(out=table_row[0:P, :], in0=newest[0:P, NS - 1, :], scalar=-1.0, in1=no_edge[0:P, :],
                                   op0=ALU.add, op1=ALU.add).then_inc(setup, 1)
            dve.wait_ge(looked, 3)
            n1 = NB - J
            v.tensor_tensor(picked[0:P, 0:n1].rearrange("p (k b) t -> p k b t", k=4),
                            ps[0:P, 2:6, 0:J * T].rearrange("p k (b t) -> p k b t", t=T),
                            b_dst[0:P, J:NB].rearrange("p (k b) t -> p k b t", k=4), ALU.mult).then_inc(setup, 1)
            dve.wait_ge(setup, 23)
            v.tensor_reduce(prior_f[0:P, 0, 0:n1], picked[0:P, 0:n1], AX_X, ALU.add).then_inc(setup, 1)
            dve.wait_ge(setup, 24)
            v.tensor_scalar(prior_f[0:P, 1, 0:n1], prior_f[0:P, 0, 0:n1], 0.0, NOWHERE, ALU.is_equal, ALU.mult).then_inc(setup, 1)
            dve.wait_ge(setup, 25)
            v.scalar_tensor_tensor(out=prior_row[0:P, J:NB], in0=prior_f[0:P, 0, 0:n1], scalar=-1.0, in1=prior_f[0:P, 1, 0:n1],
                                   op0=ALU.add, op1=ALU.add).then_inc(setup, 1)
            dve.wait_ge(setup, 26)
            dve.wait_ge(weighted, 6)
            v.memset(w1_n[:, :, MC, E:SH0], 0.0).then_inc(w1_clear, 1)
            v.memset(w2_n[0:SH0, MC, :], 0.0).then_inc(w2_clear, 1)
            v.memset(b1[0:SH0, MC:MC + 1], 0.0).then_inc(main_clear, 1)

            def edge_stats(s):
                x_e = x_tile[s % XS]
                dve.wait_ge(xe_in[s], 16 * J)
                if s:
                    dve.wait_ge(e_scalars, 5 * s)
                for i in range(J):
                    v.bn_stats(e_stats[0:P, i, :], x_e[0:P, i, :]).then_inc(e_dve, 1)
                for i in range(J):
                    dve.wait_ge(e_dve, J * s + i + 1)
                    v.bn_aggr(e_mv[0:P, i, :], e_stats[0:P, i, :]).then_inc(e_mv_ready, 1)

            def edge_same(s):
                if s >= 2:
                    dve.wait_ge(e_summed, J * (s - 1))
                for i in range(J):
                    op = v.tensor_scalar(same[s % 2][0:P, i, :], dst_bc[0:P, s * GN:(s + 1) * GN],
                                         node_f[0:P, 1, J * s + i:J * s + i + 1], None, ALU.is_equal)
                op.then_inc(same_ready, 1)

            def edge_lo(s):
                dve.wait_ge(e_split_hi, s + 1)
                v.tensor_tensor(e_lo[0:P], x_tile[s % XS][0:P], f32(e_hi[0:P]), ALU.subtract).then_inc(e_split_lo, 1)

            def edge_add(s):
                if s >= 2:
                    dve.wait_ge(table_in, 32 * (s - 1))
                if s:
                    dve.wait_ge(prior_in, 64 * s)
                for i in range(J):
                    dve.wait_ge(e_summed, J * s + i + 1)
                    bank = 4 * (s % 2) + i
                    if s:
                        v.tensor_tensor(summed[s % 2][0:P, i, :], ps[0:P, bank, :], prior[0:P, i, :], ALU.add).then_inc(sum_ready, 1)
                    else:
                        v.tensor_copy(summed[0][0:P, i, :], ps[0:P, bank, :]).then_inc(sum_ready, 1)

            edge_stats(0)
            edge_same(0)
            edge_stats(1)
            edge_lo(0)
            for s in range(NS):
                if s + 1 < NS:
                    edge_same(s + 1)
                if s + 2 < NS:
                    edge_stats(s + 2)
                if s + 1 < NS:
                    edge_lo(s + 1)
                edge_add(s)
                if s == 0:
                    dve.wait_ge(w_in, 80)
                    v.tensor_reduce(w_sum[:, :], wn[:, :, :], AX_X, ALU.add).then_inc(wprep, 1)
                    dve.wait_ge(wprep, 1)
                    v.tensor_tensor(beta[:, :], gb[:, :], w_sum[:, :], ALU.subtract).then_inc(wprep, 1)
                    dve.wait_ge(wprep, 2)
                    v.tensor_scalar(w_sum[:, :], beta[:, :], 1.0 / D, None, ALU.mult).then_inc(wprep, 1)
                    dve.wait_ge(wprep, 3)
                    for c in range(KC):
                        v.tensor_scalar(wn[:, c, :], wn[:, c, :], w_sum[:, c:c + 1], None, ALU.add).then_inc(wprep, 1)
                    dve.wait_ge(w2_in, 64)
                    v.tensor_scalar(w2_n[SH0:128, MC, :], w2_n[SH0:128, MC, :], 1.0 / SH, None, ALU.mult).then_inc(wprep, 1)
            dve.wait_ge(w_tr, 2)
            dve.wait_ge(w1_in, 16 * 2 * KC)
            v.tensor_copy(w1_n[:, :, MC, 0:E], ps[:, 4, 0:KC * E].rearrange("p (c e) -> p c e", e=E)).then_inc(wprep, 1)
            dve.wait_ge(w_hi, 1)
            for c in range(KC):
                v.tensor_tensor(wg_lo[:, c, :], ps[:, c, :], f32(wg_hi[:, c, :]), ALU.subtract).then_inc(wprep, 1)
            dve.wait_ge(w_hi, 2)
            v.tensor_tensor(w1_lo[:, :, :, :], w1_n[:, :, :, :], f32(w1_hi[:, :, :, :]), ALU.subtract).then_inc(wprep, 1)
            dve.wait_ge(w_hi, 3)
            v.tensor_tensor(w2_lo[:, :, :], w2_n[:, :, :], f32(w2_hi[:, :, :]), ALU.subtract).then_inc(wprep, 1)
            dve.wait_ge(wprep, 15)
            dve.wait_ge(table_in, 32 * NS)
            v.memset(f32(h_hi[:, MC, :]), 0.0).then_inc(wprep, 1)
            v.memset(f32(h_lo[:, MC, :]), 0.0).then_inc(wprep, 1)
            v.memset(lg[0:P, :, E:E + TOP], LOWEST).then_inc(wprep, 1)
            v.memset(logits_f[:, :], 0.0).then_inc(wprep, 1)
            v.memset(comb[0:P, :, E:E + SH], 1.0 / SH).then_inc(wprep, 1)
            dve.wait_ge(wprep, 20)

            def stats1(k, u):
                g, slot, rnd = steps(k, u)
                dve.wait_ge(x_loaded[slot], 32 * (rnd + 1))
                after(dve, ln1_done, LN * g)
                for j in range(J):
                    v.bn_stats(st1[0:P, j, :], x_tile[slot][0:P, j, :]).then_inc(st1_done, 1)

            def add_edges(k, u):
                g, _, _ = steps(k, u)
                dve.wait_ge(u_in, 64 * (g + 1))
                for j in range(J):
                    dve.wait_ge(z_scaled, J * g + j + 1)
                    v.tensor_tensor(z_tile[0:P, j, :], z_tile[0:P, j, :], u_tile[0:P, j, :], ALU.add).then_inc(z_ready, 1)

            def z_low(k, u, j):
                g, _, _ = steps(k, u)
                dve.wait_ge(zT_hi_ok, J * g + j + 1)
                hi = zT_hi[:, j, :, :].rearrange("p c q -> p (c q)")
                v.tensor_tensor(zT_lo[:, j, :, :].rearrange("p c q -> p (c q)"), ps[:, TR[j % 2], 0:KC * P], f32(hi),
                                ALU.subtract).then_inc(zT_lo_ok, 1)

            def xn_low(k, u, j):
                g, _, _ = steps(k, u)
                dve.wait_ge(xT_hi_ok, J * g + j + 1)
                v.tensor_tensor(xT_lo[:, :, j, :], ps[:, TR[j % 2], 0:KC * P].rearrange("p (c q) -> p c q", q=P),
                                f32(xT_hi[:, :, j, :]), ALU.subtract).then_inc(xT_lo_ok, 1)

            def residual1(k, u, j):
                g, slot, _ = steps(k, u)
                x_j = x_tile[slot][0:P, j, :]
                dve.wait_ge(gnn_done, J * g + j + 1)
                v.scalar_tensor_tensor(out=x_j, in0=ps[0:P, BANK[5 + j], :], scalar=0.0, in1=x_j,
                                       op0=ALU.max, op1=ALU.add).then_inc(x1_done, 1)
                if j == 0:
                    after(dve, ln2_done, LN * g)
                dve.wait_ge(x1_done, J * g + j + 1)
                v.bn_stats(st2[0:P, j, :], x_j).then_inc(st2_done, 1)

            def residual2(k, u, j):
                g, slot, _ = steps(k, u)
                x_j = x_tile[slot][0:P, j, :]
                dve.wait_ge(ffn2_done, J * g + j + 1)
                v.tensor_tensor(x_j, ps[0:P, BANK[9 + j], :], x_j, ALU.add).then_inc(out_ready, 1)

            def weigh(k, u, m):
                g, _, _ = steps(k, u)
                dve.wait_ge(act_done, 6 * g + 3 + m)
                dve.wait_ge(spread, J * g + m + 1)
                v.tensor_tensor(hid[:, m, :], ps[:, SPREAD[m % 2], 0:GN], hid[:, m, :], ALU.mult).then_inc(weighed, 1)

            def h_low(k, u, m):
                g, _, _ = steps(k, u)
                dve.wait_ge(h_hi_ok, 6 * g + 3 + m)
                v.tensor_tensor(h_lo[:, m, :], hid[:, m, :], f32(h_hi[:, m, :]), ALU.subtract).then_inc(h_lo_ok, 1)

            def wide(col):
                return col.unsqueeze(2).to_broadcast((P, J, E))

            def gate_probs(k, u):
                g, _, _ = steps(k, u)
                at = GATE * g
                after(dve, gated, GATE * g)
                dve.wait_ge(lg_turned, g + 1)
                v.tensor_copy(lg[0:P, :, 0:E], ps[0:P, SMALL, :].rearrange("p (j e) -> p j e", e=128)[:, :, 0:E]).then_inc(gated, 1)
                dve.wait_ge(gated, at + 1)
                v.tensor_reduce(gs[0:P, 4, :], lg[0:P, :, 0:E], AX_X, ALU.max).then_inc(gated, 1)
                for j in range(J):
                    v.max(top8[0:P, j, :], lg[0:P, j, 0:E]).then_inc(gated, 1)
                dve.wait_ge(gated, at + 6)
                v.tensor_tensor(gt[0:P, 0], lg[0:P, :, 0:E], wide(gs[0:P, 4, :]), ALU.subtract).then_inc(gated, 1)
                v.memset(top8[0:P, :, TOP:8], LOWEST).then_inc(gated, 1)

            def gate_combine(k, u):
                g, _, _ = steps(k, u)
                at = GATE * g
                dve.wait_ge(tanh_done, 2 * g + 1)
                v.tensor_scalar(gt[0:P, 2], gt[0:P, 1], -1.0, 1.0, ALU.mult, ALU.add).then_inc(gated, 1)
                dve.wait_ge(gated, at + 9)
                v.reciprocal(gt[0:P, 3], gt[0:P, 2]).then_inc(gated, 1)
                dve.wait_ge(gated, at + 10)
                v.scalar_tensor_tensor(out=gt[0:P, 4], in0=gt[0:P, 1], scalar=1.0, in1=gt[0:P, 3],
                                       op0=ALU.add, op1=ALU.mult).then_inc(gated, 1)
                dve.wait_ge(gated, at + 11)
                v.tensor_reduce(gs[0:P, 0, :], gt[0:P, 4], AX_X, ALU.add).then_inc(gated, 1)
                dve.wait_ge(gated, at + 12)
                v.reciprocal(gs[0:P, 1, :], gs[0:P, 0, :]).then_inc(gated, 1)
                dve.wait_ge(gated, at + 13)
                v.scalar_tensor_tensor(out=gt[0:P, 5], in0=gt[0:P, 4], scalar=-1.0, in1=wide(gs[0:P, 1, :]),
                                       op0=ALU.add, op1=ALU.mult).then_inc(gated, 1)
                for j in range(J):
                    v.match_replace(left[0:P, j, :], top8[0:P, j, :], lg[0:P, j, :], -LOWEST).then_inc(gated, 1)
                dve.wait_ge(tanh_done, 2 * g + 2)
                v.tensor_scalar(gt[0:P, 7], gt[0:P, 6], -1.0, 1.0, ALU.mult, ALU.add).then_inc(gated, 1)
                dve.wait_ge(gated, at + 19)
                v.reciprocal(gt[0:P, 8], gt[0:P, 7]).then_inc(gated, 1)
                dve.wait_ge(gated, at + 20)
                v.scalar_tensor_tensor(out=gt[0:P, 9], in0=gt[0:P, 6], scalar=1.0, in1=gt[0:P, 8],
                                       op0=ALU.add, op1=ALU.mult).then_inc(gated, 1)
                dve.wait_ge(gated, at + 21)
                v.scalar_tensor_tensor(out=gt[0:P, 10], in0=left[0:P, :, 0:E], scalar=-LOWEST, in1=gt[0:P, 9],
                                       op0=ALU.is_equal, op1=ALU.mult).then_inc(gated, 1)
                dve.wait_ge(gated, at + 22)
                v.tensor_reduce(gs[0:P, 2, :], gt[0:P, 10], AX_X, ALU.add).then_inc(gated, 1)
                dve.wait_ge(gated, at + 23)
                v.reciprocal(gs[0:P, 3, :], gs[0:P, 2, :]).then_inc(gated, 1)
                dve.wait_ge(gated, at + 24)
                v.tensor_tensor(comb[0:P, :, 0:E], gt[0:P, 10], wide(gs[0:P, 3, :]), ALU.mult).then_inc(gated, 1)

            def first():
                stats1(0, 0)
                add_edges(0, 0)
                for j in range(J):
                    z_low(0, 0, j)
                stats1(0, 1)
                for j in range(J):
                    residual1(0, 0, j)
                add_edges(0, 1)
                for j in range(J):
                    z_low(0, 1, j)
                for j in range(J):
                    xn_low(0, 0, j)

            def body(k, u, more=2):
                g, _, _ = steps(k, u)
                if more == 2:
                    stats1(k, u + 2)
                gate_probs(k, u)
                dve.wait_ge(h_hi_ok, 6 * g + 1)
                v.tensor_tensor(h_lo[SH0:128, MC, :], hid[SH0:128, MC, :], f32(h_hi[SH0:128, MC, :]),
                                ALU.subtract).then_inc(h_lo_ok, 1)
                if more == 2:
                    add_edges(k, u + 2)
                gate_combine(k, u)
                if more:
                    residual1(k, u + 1, 0)
                dve.wait_ge(h_hi_ok, 6 * g + 2)
                v.tensor_tensor(h_lo[0:E + SH, MC, :], ps[0:E + SH, SMALL, 0:GN], f32(h_hi[0:E + SH, MC, :]),
                                ALU.subtract).then_inc(h_lo_ok, 1)
                if more:
                    residual1(k, u + 1, 1)
                if more == 2:
                    z_low(k, u + 2, 0)
                weigh(k, u, 0)
                weigh(k, u, 1)
                h_low(k, u, 0)
                h_low(k, u, 1)
                if more:
                    residual1(k, u + 1, 2)
                if more == 2:
                    z_low(k, u + 2, 1)
                weigh(k, u, 2)
                weigh(k, u, 3)
                if more:
                    residual1(k, u + 1, 3)
                h_low(k, u, 2)
                h_low(k, u, 3)
                if more == 2:
                    z_low(k, u + 2, 2)
                residual2(k, u, 0)
                if more == 2:
                    z_low(k, u + 2, 3)
                residual2(k, u, 1)
                if more:
                    xn_low(k, u + 1, 0)
                    xn_low(k, u + 1, 1)
                residual2(k, u, 2)
                if more:
                    xn_low(k, u + 1, 2)
                    xn_low(k, u + 1, 3)
                residual2(k, u, 3)

            pipeline(dve, first, body, lambda k, u: body(k, u, more=G - 1 - u))

        @block.tensor
        def _(pe):
            t = nc.tensor
            pe.wait_ge(setup, 1)
            pe.wait_ge(consts, 15)
            for a in range(2):
                op = t.transpose(ps[0:P, 6, a * NB:(a + 1) * NB], idx_rows_f[:, a, :], ident[0:NB, 0:NB])
            op.then_inc(idx_tr, 1)
            pe.wait_ge(setup, 11)
            for b in range(NB):
                op = t.matmul(ps[0:P, 7, 0:T], a_src[0:P, b, :], b_src[0:P, b, :], start=b == 0, stop=b == NB - 1)
            op.then_inc(counted, 1)
            for a, at in ((0, at_src), (1, at_dst)):
                pe.wait_ge(dis_ready, 1)
                pe.wait_ge(setup, (13, 15)[a])
                for b in range(NB):
                    bank, col = 4 * a + b // (NB // 4), b % (NB // 4) * T
                    op = t.matmul(ps[0:P, bank, col:col + T], at[0:P, b * P:(b + 1) * P], dis[0:P, :], start=True, stop=True)
                op.then_inc(looked, 1)
            pe.wait_ge(setup, 19)
            pe.wait_ge(weighted, 4)
            for b in range(NB):
                op = t.matmul(ps[0:P, 0, 0:T], a_dst[0:P, b, :], b_norm[0:P, b, :], start=b == 0, stop=b == NB - 1)
            op.then_inc(counted, 1)
            pe.wait_ge(flagged, NB + 2)
            for b in range(NB):
                s = b // J
                op = t.matmul(ps[0:P, 1, s * T:(s + 1) * T], a_dst[0:P, b, :], picked[0:P, b, :], start=b % J == 0, stop=b % J == J - 1)
            op.then_inc(counted, 1)
            for b in range(J, NB):
                s = b // J
                if b % J == 0:
                    pe.wait_ge(newest_ready, 2 * s - 1)
                op = t.matmul(ps[0:P, 1 + s, b % J * T:(b % J + 1) * T], at_dst[0:P, b * P:(b + 1) * P],
                              newest[0:P, s - 1, :], start=True, stop=True)
            op.then_inc(looked, 1)

            for s in range(NS):
                pe.wait_ge(same_ready, s + 1)
                pe.wait_ge(e_split_lo, s + 1)
                if s == 0:
                    pe.wait_ge(setup, 23)
                if s >= 2:
                    pe.wait_ge(sum_ready, J * (s - 1))
                for j in range(J):
                    for n, (i, part) in enumerate((i, part) for i in range(J) for part in (e_hi, e_lo)):
                        op = t.matmul(ps[0:P, 4 * (s % 2) + j, :], same[s % 2][0:P, i, j * P:(j + 1) * P],
                                      part[0:P, i, :], start=n == 0, stop=n == 2 * J - 1)
                    op.then_inc(e_summed, 1)

            pe.wait_ge(wprep, 7)
            pe.wait_ge(sum_ready, J * NS)
            for c in range(KC):
                for o in range(KC):
                    op = t.transpose(ps[:, c, o * 128:(o + 1) * 128], wn[:, o, c * 128:(c + 1) * 128], ident[:, :])
            op.then_inc(w_tr, 1)
            for c in range(KC):
                op = t.transpose(ps[:, 4, c * E:(c + 1) * E], gate_n[:, c * 128:(c + 1) * 128], ident[0:E, 0:E])
            op.then_inc(w_tr, 1)

            def turn_z(k, u, j):
                g, _, _ = steps(k, u)
                pe.wait_ge(z_ready, J * g + j + 1)
                if j >= 2:
                    pe.wait_ge(zT_lo_ok, J * g + j - 1)
                else:
                    after(pe, xT_lo_ok, J * (g - 2) + j + 3)
                for c in range(KC):
                    op = t.transpose(ps[:, TR[j % 2], c * P:(c + 1) * P], z_tile[0:P, j, c * 128:(c + 1) * 128],
                                     ident[0:P, 0:P])
                op.then_inc(z_turned, 1)

            def turn_xn(k, u, j, more):
                g, _, _ = steps(k, u)
                pe.wait_ge(xn_ready, J * g + j + 1)
                if j >= 2:
                    pe.wait_ge(xT_lo_ok, J * g + j - 1)
                elif more:
                    pe.wait_ge(zT_lo_ok, J * (g + 1) + j + 3)
                for c in range(KC):
                    op = t.transpose(ps[:, TR[j % 2], c * P:(c + 1) * P], xn_tile[0:P, j, c * 128:(c + 1) * 128],
                                     ident[0:P, 0:P])
                op.then_inc(xn_turned, 1)

            def gnn(k, u, j, steady=True):
                g, _, _ = steps(k, u)
                pe.wait_ge(zT_lo_ok, J * g + j + 1)
                if steady:
                    if j < 3:
                        pe.wait_ge(act_done, 6 * (g - 1) + 4 + j)
                    else:
                        pe.wait_ge(x1_done, J * g + 1)
                elif j == 3:
                    pe.wait_ge(x1_done, 1)
                n = 0
                for lhs, rhs in passes(zT_hi, zT_lo, wg_hi, wg_lo):
                    for c in range(KC):
                        op = t.matmul(ps[0:P, BANK[5 + j], :], lhs[:, j, c, :], rhs[:, c, :], start=n == 0, stop=n == 3 * KC - 1)
                        n += 1
                op.then_inc(gnn_done, 1)

            def ffn1(k, u, m):
                g, _, _ = steps(k, u)
                pos = (m + 1) % (MC + 1)
                if pos == 0:
                    pe.wait_ge(xT_lo_ok, J * (g + 1))
                    after(pe, out_ready, J * (g - 1) + 1)
                    pe.wait_ge(x1_done, J * (g + 1))
                elif pos == 1:
                    after(pe, out_ready, J * (g - 1) + 4)
                elif pos >= 3:
                    pe.wait_ge(act_done, 6 * g + pos - 1)
                n = 0
                for lhs, rhs in ((w1_hi, xT_hi), (w1_lo, xT_hi), (w1_hi, xT_lo)):
                    for c in range(KC):
                        op = t.matmul(ps[:, BANK[pos], 0:GN], lhs[:, c, m, :], rhs[:, c, :, :].rearrange("p j q -> p (j q)"),
                                      start=n == 0, stop=n == 3 * KC - 1)
                        n += 1
                op.then_inc(ffn1_done, 1)

            def ffn2(k, u, j, more):
                g, _, _ = steps(k, u)
                if more and j < 3:
                    pe.wait_ge(x1_done, J * (g + 1) + j + 2)
                if j == 3:
                    pe.wait_ge(out_ready, J * g + 2)
                order = [MC] + list(range(MC))
                n = 0
                for m in order:
                    if j == 0 and m < MC:
                        pe.wait_ge(h_lo_ok, 6 * g + 3 + m)
                    cols = slice(j * P, (j + 1) * P)
                    for lhs, rhs in passes(h_hi, h_lo, w2_hi, w2_lo):
                        op = t.matmul(ps[0:P, BANK[9 + j], :], lhs[:, m, cols], rhs[:, m, :],
                                      start=n == 0, stop=n == 3 * (MC + 1) - 1)
                        n += 1
                op.then_inc(ffn2_done, 1)

            def turn_logits(k, u):
                g, _, _ = steps(k, u)
                pe.wait_ge(act_done, 6 * g + 1)
                after(pe, h_lo_ok, 6 * (g - 1) + 2)
                for j in range(J):
                    op = t.transpose(ps[0:P, SMALL, j * 128:(j + 1) * 128], logits_f[:, j * P:(j + 1) * P], ident[:, :])
                op.then_inc(lg_turned, 1)

            def turn_comb(k, u):
                g, _, _ = steps(k, u)
                pe.wait_ge(gated, GATE * (g + 1))
                for j in range(J):
                    op = t.transpose(ps[0:E + SH, SMALL, j * P:(j + 1) * P], comb[0:P, j, :], ident[0:P, 0:P])
                op.then_inc(comb_turned, 1)

            def spread_comb(k, u, m):
                g, _, _ = steps(k, u)
                if m == 0:
                    pe.wait_ge(h_lo_ok, 6 * g + 2)
                if m >= 2:
                    pe.wait_ge(weighed, J * g + m - 1)
                else:
                    after(pe, weighed, J * (g - 1) + m + 3)
                for n, part in enumerate((h_hi, h_lo)):
                    op = t.matmul(ps[:, SPREAD[m % 2], 0:GN], expert_of[:, m, :], part[:, MC, :], start=n == 0, stop=n == 1)
                op.then_inc(spread, 1)

            def first():
                pe.wait_ge(wprep, 20)
                for j in range(J):
                    turn_z(0, 0, j)
                for j in range(J):
                    gnn(0, 0, j, steady=False)
                for j in range(J):
                    turn_z(0, 1, j)
                for j in range(J):
                    turn_xn(0, 0, j, True)

            def body(k, u, more=2):
                ffn1(k, u, MC)
                ffn1(k, u, 0)
                turn_logits(k, u)
                for m in range(1, MC):
                    ffn1(k, u, m)
                if more:
                    gnn(k, u + 1, 0)
                turn_comb(k, u)
                if more:
                    gnn(k, u + 1, 1)
                spread_comb(k, u, 0)
                spread_comb(k, u, 1)
                if more == 2:
                    turn_z(k, u + 2, 0)
                if more:
                    gnn(k, u + 1, 2)
                spread_comb(k, u, 2)
                spread_comb(k, u, 3)
                if more == 2:
                    turn_z(k, u + 2, 1)
                if more:
                    gnn(k, u + 1, 3)
                if more == 2:
                    turn_z(k, u + 2, 2)
                ffn2(k, u, 0, more)
                if more == 2:
                    turn_z(k, u + 2, 3)
                ffn2(k, u, 1, more)
                if more:
                    turn_xn(k, u + 1, 0, more == 2)
                    turn_xn(k, u + 1, 1, more == 2)
                ffn2(k, u, 2, more)
                if more:
                    turn_xn(k, u + 1, 2, more == 2)
                    turn_xn(k, u + 1, 3, more == 2)
                ffn2(k, u, 3, more)

            pipeline(pe, first, body, lambda k, u: body(k, u, more=G - 1 - u))


_INS = ["x", "src", "dst", "L0_gnn_W", "L0_gnn_b", "L0_ffn_gate_w", "L0_ffn_re_w1", "L0_ffn_re_b1", "L0_ffn_re_w2",
        "L0_ffn_re_b2", "L0_ffn_se_w1", "L0_ffn_se_b1", "L0_ffn_se_w2", "L0_ffn_se_b2"]


def kernel(**inputs):
    import numpy as _np
    import concourse.bacc as _bacc
    from concourse import mybir as _mybir
    from concourse.bass_utils import run_bass_kernel_spmd as _run

    nc = _bacc.Bacc("TRN2", target_bir_lowering=False, num_devices=1)
    arrays, args = {}, []
    for name in _INS:
        a = _np.ascontiguousarray(inputs[name])
        arrays[f"in_{name}"] = a
        args.append(nc.dram_tensor(f"in_{name}", a.shape, _mybir.dt.from_np(a.dtype), kind="ExternalInput").ap())
    shape = _np.shape(inputs["x"])
    args.append(nc.dram_tensor("out_0", shape, _mybir.dt.float32, kind="ExternalOutput").ap())
    gnn_moe(nc, *args)
    r = _run(nc, [arrays], core_ids=[0])
    return r.results[0]["out_0"]
```

```python
from contextlib import ExitStack

import concourse.bass as bass
from concourse import mybir

F32 = mybir.dt.float32
F32R = mybir.dt.float32r
BF16 = mybir.dt.bfloat16
I32 = mybir.dt.int32
U32 = mybir.dt.uint32
ALU = mybir.AluOpType
ACT = mybir.ActivationFunctionType
AX_X = mybir.AxisListType.X

EPS = 1e-5
ROUND = 12582912.0
NOWHERE = 1048576.0
LOWEST = -3.0e38


def gnn_moe(nc, x, src, dst, gnn_w, gnn_b, gate_w, re_w1, re_b1, re_w2, re_b2, se_w1, se_b1, se_w2, se_b2, out):
    N, D = x.shape
    NE = src.shape[0]
    E, _, F = re_w1.shape
    SH = se_w1.shape[0]
    TOP = 4
    KC = D // 128
    J = 4
    P = 125
    T = N // P
    G = T // J
    GN = P * J
    NB = NE // P
    K = 5
    NS = NB // K
    SB = K * P
    MC = E * F // 128
    SF = SH * F
    SH0 = 128 - SF
    LN = 13
    XS = 4
    HALF = 112
    assert N == P * T and T == J * G and NE == P * NB and NB == K * NS and E * F == 128 * MC and SH == 2

    x_v = x.rearrange("(p t) d -> p (t d)", t=T)
    out_v = out.rearrange("(p t) d -> p (t d)", t=T)
    table = nc.dram_tensor("edge_sums", [NE, D], F32, kind="Internal").ap()

    ctx = ExitStack()
    with ctx:
        def sb(name, shape, dt=F32, scope=ctx):
            return scope.enter_context(nc.sbuf_tensor(name, shape, dt))

        def sem(name):
            return ctx.enter_context(nc.semaphore(name))

        ps = ctx.enter_context(nc.psum_tensor("ps", [128, 8, 512], F32))

        in_place = ExitStack()
        low_rows = [sb(f"low_rows{i}", [128, J, D], F32R, in_place) for i in range(XS)]
        in_place.close()
        x_tile = [sb(f"x_tile{i}", [128, J, D]) for i in range(XS)]
        b1 = sb("b1", [128, MC + 1])
        ident = sb("ident", [128, 128])
        expert_of = sb("expert_of", [128, MC, 128], F32R)
        neg_half = sb("neg_half", [128, NB])
        half, inv_128, eps4, zero4 = sb("half", [128, J]), sb("inv_128", [128, J]), sb("eps4", [128, J]), sb("zero4", [128, J])
        dis, dis2x2 = sb("dis", [128, T]), sb("dis2x2", [128, T])
        s_node = sb("s_node", [128, T])
        table_row = sb("table_row", [128, T], U32)

        gb, w_sum, beta = sb("gb", [128, KC]), sb("w_sum", [128, KC]), sb("beta", [128, KC])

        early = ExitStack()
        at_src = sb("at_src", [128, NE], F32, early)
        a_src = sb("a_src", [128, NB, P], BF16, early)
        b_src = sb("b_src", [128, NB, T], BF16, early)
        a_dst16 = sb("a_dst16", [128, NB, P], BF16, early)
        picked = sb("picked", [128, NB, T], F32, early)
        idx_rows = sb("idx_rows", [NB, 2, P], I32, early)
        idx_rows_f = sb("idx_rows_f", [NB, 2, P], F32, early)
        row_iota = sb("row_iota", [128, 128], I32, early)
        row_iota_f = sb("row_iota_f", [128, 128], F32, early)
        ident16 = sb("ident16", [128, 128], BF16, early)
        expert_f = sb("expert_f", [128, MC, 128], F32, early)
        quot = sb("quot", [128, 2, NB], F32, early)
        quot_r = sb("quot_r", [128, 2, NB], F32, early)
        rest = sb("rest", [128, 2, NB], F32, early)
        deg = sb("deg", [128, T], F32, early)
        filler = sb("filler", [128, 320], F32, early)
        at_dst = sb("at_dst", [128, NE], F32, early)
        a_dst = sb("a_dst", [128, NB, P], F32, early)
        b_dst = sb("b_dst", [128, NB, T], F32, early)
        b_norm = sb("b_norm", [128, NB, T], F32, early)
        b_last = sb("b_last", [128, NB, T], F32, early)
        b_prior = sb("b_prior", [128, NB, T], F32, early)
        dst_bc = sb("dst_bc", [128, NE], I32, early)
        not_before = sb("not_before", [128, SB], F32, early)
        node_f = sb("node_f", [128, 2, NB], F32, early)
        node_u = sb("node_u", [128, 2, NB], U32, early)
        deg_src = sb("deg_src", [128, NB], F32, early)
        dis_src = sb("dis_src", [128, NB], F32, early)
        degree = sb("degree", [128, T], F32, early)
        dis2 = sb("dis2", [128, T], F32, early)
        edge_row = sb("edge_row", [128, NB], I32, early)
        matches = sb("matches", [128, NB], F32, early)
        last_row = sb("last_row", [128, NB], F32, early)
        kept = sb("kept", [128, NS, T], F32, early)
        newest = sb("newest", [128, NS, T], F32, early)
        no_edge = sb("no_edge", [128, T], F32, early)
        prior_f = sb("prior_f", [128, 2, NB], F32, early)
        prior_row = sb("prior_row", [128, NB], U32, early)
        with ExitStack() as in_place:
            low_more = sb("low_more", [128, NB - XS * J, D], F32R, in_place)
        x_more = sb("x_more", [128, NB - XS * J, D], F32, early)
        e_hi = sb("e_hi", [128, 2, K, D], F32R, early)
        same = sb("same", [128, 2, (K * (K + 1) // 2) * P], F32R, early)
        sums = sb("sums", [128, 2, K, D], F32, early)
        e_stats = sb("e_stats", [128, NB, 6], F32, early)
        e_mv = sb("e_mv", [128, NB, 2], F32, early)
        e_sc = sb("e_sc", [128, 5, NB], F32, early)
        early.close()
        wg_lo = sb("wg_lo", [128, KC, D], F32R)
        with ExitStack() as as_read:
            w1_n = sb("w1_n", [128, KC, MC + 1, 128], F32, as_read)
        w1_lo = sb("w1_lo", [128, KC, MC + 1, 128], F32R)
        with ExitStack() as as_read:
            wn = sb("wn", [128, KC, D], F32, as_read)
            gate_n = sb("gate_n", [E, D], F32, as_read)
        w1_hi = sb("w1_hi", [128, KC, MC + 1, 128], F32R)
        wg_hi = sb("wg_hi", [128, KC, D], F32R)
        with ExitStack() as as_read:
            w2_n = sb("w2_n", [128, MC + 1, D], F32, as_read)
        w2_lo, w2_hi = sb("w2_lo", [128, MC + 1, D], F32R), sb("w2_hi", [128, MC + 1, D], F32R)

        u_tile = sb("u_tile", [128, J, D])
        z_tile = sb("z_tile", [128, J, D])
        zT_hi, zT_lo = sb("zT_hi", [128, J, KC, P], F32R), sb("zT_lo", [128, J, KC, P], F32R)
        xn_tile = sb("xn_tile", [128, J, D])
        xT_hi, xT_lo = sb("xT_hi", [128, KC, J, P], F32R), sb("xT_lo", [128, KC, J, P], F32R)
        hid = sb("hid", [128, MC + 1, GN])
        h_hi, h_lo = sb("h_hi", [128, MC + 1, GN], F32R), sb("h_lo", [128, MC + 1, GN], F32R)
        logits_f = sb("logits_f", [128, GN])
        row_idx = sb("row_idx", [128, J], U32)
        st1, sc1 = sb("st1", [128, J, 6]), sb("sc1", [128, LN, J])
        st2, sc2 = sb("st2", [128, J, 6]), sb("sc2", [128, LN, J])
        lg = sb("lg", [128, J, E + TOP])
        top8 = sb("top8", [128, J, 8])
        left = sb("left", [128, J, E + TOP])
        gt = sb("gt", [128, 12, J, E])
        gs = sb("gs", [128, 5, J])
        comb = sb("comb", [128, J, E + SH])

        idx_in, bc_in, w_in, w1_in, w2_in = sem("idx_in"), sem("bc_in"), sem("w_in"), sem("w1_in"), sem("w2_in")
        consts, copied, idx_turned, node_ready = sem("consts"), sem("copied"), sem("idx_turned"), sem("node_ready")
        hot_ready, at_turned, at_ready, a_dst_ready = sem("hot_ready"), sem("at_turned"), sem("at_ready"), sem("a_dst_ready")
        deg_counted, deg_ready, deg_looked, deg_src_ready = (
            sem("deg_counted"), sem("deg_ready"), sem("deg_looked"), sem("deg_src_ready"))
        same_ready, last_ready, last_spread, newest_ready = (
            sem("same_ready"), sem("last_ready"), sem("last_spread"), sem("newest_ready"))
        prior_looked, prior_rows, rows_ready = sem("prior_looked"), sem("prior_rows"), sem("rows_ready")
        dis_src_ready, dis_ready, b_norm_ready, s_summed, s_ready = (
            sem("dis_src_ready"), sem("dis_ready"), sem("b_norm_ready"), sem("s_summed"), sem("s_ready"))
        w1_clear, w2_clear, b1_clear = sem("w1_clear"), sem("w2_clear"), sem("b1_clear")
        wsum_ready, w_biased, w_turned, w_hi, w_lo, gate_in, halved, cleared = (
            sem("wsum_ready"), sem("w_biased"), sem("w_turned"), sem("w_hi"), sem("w_lo"), sem("gate_in"), sem("halved"), sem("cleared"))
        xe_in = [sem(f"xe_in{s}") for s in range(NS)]
        e_stats_ready, e_mv_ready, e_scalars, e_normed = sem("e_stats_ready"), sem("e_mv_ready"), sem("e_scalars"), sem("e_normed")
        e_split_hi, e_split_lo, e_summed = sem("e_split_hi"), sem("e_split_lo"), sem("e_summed")
        prior_clear, prior_in, sum_ready, table_in = sem("prior_clear"), sem("prior_in"), sem("sum_ready"), sem("table_in")
        x_loaded = [sem(f"x_loaded{i}") for i in range(XS)]
        stored = [sem(f"stored{i}") for i in range(XS)]
        u_zeroed, u_in, idx_copied = sem("u_zeroed"), sem("u_in"), sem("idx_copied")
        st1_done, ln1_done = sem("st1_done"), sem("ln1_done")
        z_scaled, z_ready, z_turned = sem("z_scaled"), sem("z_ready"), sem("z_turned")
        zT_hi_ok, zT_lo_ok = sem("zT_hi_ok"), sem("zT_lo_ok")
        gnn_done, x1_done = sem("gnn_done"), sem("x1_done")
        st2_done, ln2_done = sem("st2_done"), sem("ln2_done")
        xn_ready, xn_turned = sem("xn_ready"), sem("xn_turned")
        xT_hi_ok, xT_lo_ok = sem("xT_hi_ok"), sem("xT_lo_ok")
        ffn1_done, act_done = sem("ffn1_done"), sem("act_done")
        lg_turned, gated, tanh_done = sem("lg_turned"), sem("gated"), sem("tanh_done")
        comb_turned, h_hi_ok, h_lo_ok = sem("comb_turned"), sem("h_hi_ok"), sem("h_lo_ok")
        spread, weighed = sem("spread"), sem("weighed")
        ffn2_done, out_ready = sem("ffn2_done"), sem("out_ready")
        GATE = 25

        ACC = [0, 1, 2]
        BANK = [ACC[i] for i in (0, 1, 2, 0, 1, 2, 0, 1, 2, 0, 1, 2, 1)]
        TR = [3, 4]
        SPREAD = [5, 6]
        SMALL = 7

        W_BANK = [6, 7, 6, 7]

        def after(eng, semaphore, value):
            if isinstance(value, int) and value <= 0:
                return
            eng.wait_ge(semaphore, value)

        def f32(ap):
            return ap.bitcast(F32)

        def steps(k, u):
            return XS * k + u, u % XS, k + u // XS

        def pipeline(eng, first, body, last):
            first()
            for u in range(2):
                body(0, u)
            with eng.Fori(0, (G - 4) // XS) as k:
                for u in range(2, 2 + XS):
                    body(k, u)
            for u in range(G - 2, G):
                last(0, u)

        def edge_rows(b):
            return x_tile[b // J][0:P, b % J, :] if b < XS * J else x_more[0:P, b - XS * J, :]

        def low_edge_rows(b):
            return low_rows[b // J][0:P, b % J, :] if b < XS * J else low_more[0:P, b - XS * J, :]

        def same_cols(i, i2):
            at = (i * K - i * (i - 1) // 2 + i2 - i) * P
            return slice(at, at + P)

        def passes(hi_l, lo_l, hi_r, lo_r):
            return ((hi_l, hi_r), (lo_l, hi_r), (hi_l, lo_r))

        block = ctx.enter_context(nc.Block())

        @block.sync
        def _(sp):
            sp.dma_start(idx_rows[:, 0, :], src.rearrange("(b q) -> b q", q=P)).then_inc(idx_in, 16)
            sp.dma_start(idx_rows[:, 1, :], dst.rearrange("(b q) -> b q", q=P)).then_inc(idx_in, 16)
            sp.dma_start(dst_bc[0:P, :], dst.rearrange("(a e) -> a e", a=1).to_broadcast((P, NE))).then_inc(bc_in, 16)
            sp.dma_start(b1[:, 0:MC], re_b1.rearrange("(m a) f -> (a f) m", m=MC), allow_slow_non_contiguous=True).then_inc(w_in, 16)
            sp.wait_ge(b1_clear, 1)
            sp.dma_start(b1[SH0:128, MC:MC + 1], se_b1.rearrange("j (f a) -> (j f) a", a=1), allow_slow_non_contiguous=True).then_inc(w_in, 16)
            sp.wait_ge(w1_clear, 1)
            sp.dma_start(wn[:, :, :], gnn_w.rearrange("(c p) i -> p c i", p=128)).then_inc(w_in, 16)
            sp.dma_start(gate_n[:, :], gate_w).then_inc(w_in, 16)
            for c in range(KC):
                rows = slice(c * 128, (c + 1) * 128)
                sp.dma_start(w1_n[:, c, 0:MC, :].rearrange("p m (a f) -> p (m a) f", f=F),
                             re_w1[:, rows, :].rearrange("e p f -> p e f")).then_inc(w1_in, 16)
                sp.dma_start(w1_n[:, c, MC, SH0:128].rearrange("p (j f) -> p j f", f=F),
                             se_w1[:, rows, :].rearrange("j p f -> p j f")).then_inc(w1_in, 16)

            def write_sums(s):
                for b0, b1_ in ((0, 3), (3, K)):
                    sp.wait_ge(sum_ready, K * s + b1_)
                    rows_v = table[(K * s + b0) * P:(K * s + b1_) * P, :].rearrange("(i q) d -> q i d", q=P)
                    for rows in (slice(0, HALF), slice(HALF, P)):
                        sp.dma_start(rows_v[rows, :, :], sums[rows, s % 2, b0:b1_, :]).then_inc(table_in, 16)

            def load(k, u):
                g, slot, rnd = steps(k, u)
                after(sp, stored[slot], 32 * rnd)
                for rows in (slice(0, HALF), slice(HALF, P)):
                    sp.dma_start(x_tile[slot][rows, :, :].rearrange("p j d -> p (j d)"),
                                 x_v[rows, bass.ds(g * J * D, J * D)]).then_inc(x_loaded[slot], 16)

            def store(k, u):
                g, slot, rnd = steps(k, u)
                sp.wait_ge(out_ready, J * (g + 1))
                for rows in (slice(0, HALF), slice(HALF, P)):
                    sp.dma_start(out_v[rows, bass.ds(g * J * D, J * D)],
                                 x_tile[slot][rows, :, :].rearrange("p j d -> p (j d)")).then_inc(stored[slot], 16)

            def first():
                for s in range(NS):
                    write_sums(s)
                    sp.wait_ge(e_summed, K * (s + 1))
                    load(0, s)
                    if s == 0:
                        sp.dma_start(gb[:, :], gnn_b.rearrange("(c p) -> p c", p=128), allow_slow_non_contiguous=True).then_inc(w_in, 16)
                    if s == NS - 2:
                        sp.wait_ge(w2_clear, 1)
                        sp.dma_start(w2_n[:, 0:MC, :], re_w2.rearrange("(m a) f d -> (a f) m d", m=MC)).then_inc(w2_in, 16)
                        sp.dma_start(w2_n[0:E, MC, :], re_b2).then_inc(w2_in, 16)
                        sp.dma_start(w2_n[E:E + SH, MC, :], se_b2).then_inc(w2_in, 16)
                        sp.dma_start(w2_n[SH0:128, MC, :], se_w2.rearrange("j f d -> (j f) d")).then_inc(w2_in, 16)

            def body(k, u):
                store(k, u)
                load(k, u + XS)

            first()
            with sp.Fori(0, (G - XS) // XS) as k:
                for u in range(XS):
                    body(k, u)
            for u in range(G - XS, G):
                store(0, u)
            for slot in range(XS):
                sp.wait_ge(stored[slot], 32 * len(range(slot, G, XS)))

        @block.gpsimd
        def _(pool):
            gp = nc.gpsimd
            gp.memset(ident[:, :], 0.0).then_inc(consts, 1)
            gp.memset(expert_f[:, :, :], 0.0).then_inc(consts, 1)
            gp.memset(not_before[:, :], 1.0).then_inc(consts, 1)
            gp.memset(neg_half[:, :], -0.5).then_inc(consts, 1)
            gp.iota(row_iota[:, :], [[1, 128]], base=0, channel_multiplier=0).then_inc(consts, 1)
            gp.iota(edge_row[:, :], [[P, NB]], base=1, channel_multiplier=1).then_inc(consts, 1)
            gp.memset(half[:, :], 0.5).then_inc(consts, 1)
            gp.memset(inv_128[:, :], 4.0 / D).then_inc(consts, 1)
            gp.memset(eps4[:, :], 4.0 * EPS).then_inc(consts, 1)
            gp.memset(zero4[:, :], 0.0).then_inc(consts, 1)
            pool.wait_ge(consts, 10)
            gp.affine_select(out=ident[:, :], in_=ident[:, :], compare_op=ALU.not_equal, fill=1.0, base=0,
                             pattern=[[-1, 128]], channel_multiplier=1).then_inc(consts, 1)
            gp.affine_select(out=not_before[0:P, 0:P], in_=not_before[0:P, 0:P], compare_op=ALU.is_ge,
                             fill=0.0, base=0, pattern=[[1, P]], channel_multiplier=-1).then_inc(consts, 1)
            gp.affine_select(out=expert_f[:, :, :].rearrange("p m (a f) -> p m a f", f=F),
                             in_=expert_f[:, :, :].rearrange("p m (a f) -> p m a f", f=F),
                             compare_op=ALU.not_equal, fill=1.0, base=0,
                             pattern=[[-(128 // F), MC], [-1, 128 // F], [0, F]], channel_multiplier=1).then_inc(consts, 1)
            pool.wait_ge(consts, 13)
            gp.tensor_copy(expert_of[:, :, :], expert_f[:, :, :]).then_inc(consts, 1)

            table_end = pool.snap(pool.to_reg(NE - 1))

            def gather_edges(b):
                gp.indirect_dma_start(edge_rows(b), None, x, bass.IndirectOffsetOnAxis(node_u[0:P, 0, b:b + 1], 0),
                                      bounds_check=N - 1, oob_is_err=False).then_inc(xe_in[b // K], 16)

            def edge_scalars(s):
                cols = slice(K * s, K * (s + 1))
                pool.wait_ge(e_mv_ready, K * (s + 1))
                at = 5 * s
                gp.tensor_scalar(e_sc[0:P, 0, cols], e_mv[0:P, cols, 1], EPS, None, ALU.add).then_inc(e_scalars, 1)
                pool.wait_ge(e_scalars, at + 1)
                pool.wait_ge(deg_src_ready, 2 * (s + 1))
                gp.tensor_tensor(e_sc[0:P, 1, cols], e_sc[0:P, 0, cols], deg_src[0:P, cols], ALU.mult).then_inc(e_scalars, 1)
                pool.wait_ge(e_scalars, at + 2)
                gp.tensor_tensor(e_sc[0:P, 2, cols], e_sc[0:P, 1, cols], neg_half[0:P, cols], ALU.pow).then_inc(e_scalars, 1)
                pool.wait_ge(e_scalars, at + 3)
                gp.tensor_tensor(e_sc[0:P, 3, cols], e_sc[0:P, 2, cols], e_mv[0:P, cols, 0], ALU.mult).then_inc(e_scalars, 1)
                pool.wait_ge(e_scalars, at + 4)
                gp.tensor_scalar(e_sc[0:P, 4, cols], e_sc[0:P, 3, cols], -1.0, None, ALU.mult).then_inc(e_scalars, 1)

            def clear_prior(s):
                if s >= 2:
                    pool.wait_ge(table_in, 64 * (s - 1))
                gp.memset(sums[0:P, s % 2, :, :], 0.0).then_inc(prior_clear, 1)

            def gather_prior(s):
                pool.wait_ge(prior_clear, s)
                pool.wait_ge(prior_rows, 4 * s)
                pool.wait_ge(table_in, 64 * s)
                for i in range(K):
                    gp.indirect_dma_start(sums[0:P, s % 2, i, :], None, table[0:s * SB, :],
                                          bass.IndirectOffsetOnAxis(prior_row[0:P, K * s + i:K * s + i + 1], 0),
                                          bounds_check=s * SB - 1, oob_is_err=False).then_inc(prior_in, 16)

            def dis_quarter(n):
                cols = slice(n * NB, (n + 1) * NB)
                gp.tensor_tensor(dis[0:P, cols], degree[0:P, cols], neg_half[0:P, :], ALU.pow).then_inc(dis_ready, 1)

            pool.wait_ge(node_ready, 3)
            for b in range(3 * K):
                gather_edges(b)
            edge_scalars(0)
            for b in range(3 * K, NB):
                gather_edges(b)
            edge_scalars(1)
            clear_prior(1)
            edge_scalars(2)
            gather_prior(1)
            clear_prior(2)
            edge_scalars(3)
            gp.tensor_tensor(dis_src[0:P, :], deg_src[0:P, :], neg_half[0:P, :], ALU.pow).then_inc(dis_src_ready, 1)
            gather_prior(2)
            clear_prior(3)
            dis_quarter(0)
            gather_prior(3)
            for n in range(1, T // NB):
                dis_quarter(n)

            def half_rstd(stats, t, done, at):
                tt = gp.tensor_tensor
                tt(t[0:P, 0, :], stats[0:P, :, 1], stats[0:P, :, 4], ALU.add).then_inc(done, 1)
                tt(t[0:P, 1, :], stats[0:P, :, 1], stats[0:P, :, 4], ALU.subtract).then_inc(done, 1)
                tt(t[0:P, 2, :], stats[0:P, :, 2], stats[0:P, :, 5], ALU.add).then_inc(done, 1)
                pool.wait_ge(done, at + 3)
                tt(t[0:P, 3, :], t[0:P, 1, :], t[0:P, 1, :], ALU.mult).then_inc(done, 1)
                tt(t[0:P, 4, :], t[0:P, 2, :], inv_128[0:P, :], ALU.mult).then_inc(done, 1)
                tt(t[0:P, 5, :], t[0:P, 0, :], half[0:P, :], ALU.mult).then_inc(done, 1)
                pool.wait_ge(done, at + 6)
                tt(t[0:P, 6, :], t[0:P, 3, :], t[0:P, 4, :], ALU.add).then_inc(done, 1)
                pool.wait_ge(done, at + 7)
                tt(t[0:P, 7, :], t[0:P, 6, :], eps4[0:P, :], ALU.add).then_inc(done, 1)
                pool.wait_ge(done, at + 8)
                tt(t[0:P, 8, :], t[0:P, 7, :], neg_half[0:P, 0:J], ALU.pow).then_inc(done, 1)

            def ln1(k, u):
                g, _, _ = steps(k, u)
                cols = bass.ds(g * J, J)
                at = LN * g
                after(pool, z_ready, J * g)
                pool.wait_ge(st1_done, J * (g + 1))
                half_rstd(st1, sc1, ln1_done, at)
                pool.wait_ge(ln1_done, at + 9)
                gp.tensor_tensor(sc1[0:P, 9, :], sc1[0:P, 8, :], dis2x2[0:P, cols], ALU.mult).then_inc(ln1_done, 1)
                pool.wait_ge(ln1_done, at + 10)
                gp.tensor_tensor(sc1[0:P, 10, :], sc1[0:P, 9, :], sc1[0:P, 5, :], ALU.mult).then_inc(ln1_done, 1)
                pool.wait_ge(ln1_done, at + 11)
                pool.wait_ge(idx_copied, g + 1)
                pool.wait_ge(u_zeroed, g + 1)
                gp.tensor_tensor(sc1[0:P, 11, :], s_node[0:P, cols], sc1[0:P, 10, :], ALU.subtract).then_inc(ln1_done, 1)
                gp.tensor_tensor(sc1[0:P, 12, :], dis[0:P, cols], zero4[0:P, :], ALU.add).then_inc(ln1_done, 1)

            def fetch(k, u):
                g, _, _ = steps(k, u)
                after(pool, z_ready, J * g)
                gp.tensor_copy(row_idx[0:P, :], table_row[0:P, bass.ds(g * J, J)]).then_inc(idx_copied, 1)
                gp.memset(u_tile[0:P, :, :], 0.0).then_inc(u_zeroed, 1)
                ln1(k, u)
                for j in range(J):
                    gp.indirect_dma_start(u_tile[0:P, j, :], None, table,
                                          bass.IndirectOffsetOnAxis(row_idx[0:P, j:j + 1], 0),
                                          bounds_check=table_end, oob_is_err=False).then_inc(u_in, 16)

            def ln2(k, u):
                g, _, _ = steps(k, u)
                at = (LN - 1) * g
                after(pool, xn_ready, J * g)
                pool.wait_ge(st2_done, J * (g + 1))
                half_rstd(st2, sc2, ln2_done, at)
                pool.wait_ge(ln2_done, at + 9)
                gp.tensor_tensor(sc2[0:P, 9, :], sc2[0:P, 8, :], sc2[0:P, 8, :], ALU.add).then_inc(ln2_done, 1)
                pool.wait_ge(ln2_done, at + 10)
                gp.tensor_tensor(sc2[0:P, 10, :], sc2[0:P, 9, :], sc2[0:P, 5, :], ALU.mult).then_inc(ln2_done, 1)
                pool.wait_ge(ln2_done, at + 11)
                gp.tensor_tensor(sc2[0:P, 11, :], zero4[0:P, :], sc2[0:P, 10, :], ALU.subtract).then_inc(ln2_done, 1)

            def first():
                pool.wait_ge(table_in, 64 * NS)
                pool.wait_ge(rows_ready, 2)
                pool.wait_ge(s_ready, 4)
                fetch(0, 0)
                fetch(0, 1)
                ln2(0, 0)

            def body(k, u):
                fetch(k, u + 2)
                ln2(k, u + 1)

            def last(k, u):
                if u + 1 < G:
                    ln2(k, u + 1)

            pipeline(pool, first, body, last)

        @block.scalar
        def _(act):
            sc = nc.scalar

            def turn_evacuate(n, bank):
                act.wait_ge(at_turned, n + 1)
                at = at_src if n < 5 else at_dst
                cols = slice(n % 5 * GN, (n % 5 + 1) * GN)
                sc.activation(at[0:P, cols], ps[0:P, bank, 0:GN], ACT.Copy).then_inc(at_ready, 1)

            def split_hi_edges(s):
                act.wait_ge(e_scalars, 5 * (s + 1))
                for b in range(K * s, K * (s + 1)):
                    sc.activation(edge_rows(b), edge_rows(b), ACT.Identity,
                                  bias=e_sc[0:P, 4, b:b + 1], scale=e_sc[0:P, 2, b:b + 1]).then_inc(e_normed, 1)
                if s >= 2:
                    act.wait_ge(e_summed, K * (s - 1))
                for b in range(K * s, K * (s + 1)):
                    act.wait_ge(e_normed, b + 1)
                    sc.activation(e_hi[0:P, s % 2, b - K * s, :], edge_rows(b), ACT.Copy).then_inc(e_split_hi, 1)

            for n in range(5):
                turn_evacuate(n, 3 + n)
            act.wait_ge(hot_ready, 3)
            sc.activation(a_dst[0:P, :, :], a_dst16[0:P, :, :], ACT.Copy).then_inc(a_dst_ready, 1)
            for n in range(5, 10):
                turn_evacuate(n, 5 + (n - 5) % 3)
            split_hi_edges(0)
            split_hi_edges(1)
            for i in range(K):
                act.wait_ge(e_summed, i + 1)
                sc.activation(sums[0:P, 0, i, :], ps[0:P, i, :], ACT.Copy).then_inc(sum_ready, 1)
            split_hi_edges(2)
            act.wait_ge(wsum_ready, 3)
            for c in range(KC):
                sc.activation(wn[:, c, :], wn[:, c, :], ACT.Identity, bias=beta[:, c:c + 1]).then_inc(w_biased, 1)
            split_hi_edges(3)
            for c in range(KC):
                act.wait_ge(w_turned, c + 1)
                sc.activation(wg_hi[:, c, :], ps[:, W_BANK[c], :], ACT.Copy).then_inc(w_hi, 1)
            act.wait_ge(w_turned, KC + 1)
            act.wait_ge(gate_in, 1)
            sc.activation(w1_hi[:, :, :, :], w1_n[:, :, :, :], ACT.Copy).then_inc(w_hi, 1)
            act.wait_ge(halved, 1)
            sc.activation(w2_hi[:, :, :], w2_n[:, :, :], ACT.Copy).then_inc(w_hi, 1)

            def scale1(k, u):
                g, slot, _ = steps(k, u)
                act.wait_ge(ln1_done, LN * (g + 1))
                for j in range(J):
                    after(act, z_turned, J * (g - 1) + j + 1)
                    sc.activation(z_tile[0:P, j, :], x_tile[slot][0:P, j, :], ACT.Identity,
                                  bias=sc1[0:P, 11, j:j + 1], scale=sc1[0:P, 9, j:j + 1]).then_inc(z_scaled, 1)

            def scale2(k, u):
                g, slot, _ = steps(k, u)
                act.wait_ge(ln2_done, (LN - 1) * (g + 1))
                for j in range(J):
                    after(act, xn_turned, J * (g - 1) + j + 1)
                    sc.activation(xn_tile[0:P, j, :], x_tile[slot][0:P, j, :], ACT.Identity,
                                  bias=sc2[0:P, 11, j:j + 1], scale=sc2[0:P, 9, j:j + 1]).then_inc(xn_ready, 1)

            def z_hi(k, u, j):
                g, _, _ = steps(k, u)
                act.wait_ge(z_turned, J * g + j + 1)
                sc.activation(zT_hi[:, j, :, :].rearrange("p c q -> p (c q)"), ps[:, TR[j % 2], 0:KC * P],
                              ACT.Copy).then_inc(zT_hi_ok, 1)

            def xn_hi(k, u, j):
                g, _, _ = steps(k, u)
                act.wait_ge(xn_turned, J * g + j + 1)
                sc.activation(xT_hi[:, :, j, :], ps[:, TR[j % 2], 0:KC * P].rearrange("p (c q) -> p c q", q=P),
                              ACT.Copy).then_inc(xT_hi_ok, 1)

            def gelu(k, u, m):
                g, _, _ = steps(k, u)
                act.wait_ge(ffn1_done, 5 * g + 2 + m)
                after(act, h_lo_ok, 6 * (g - 1) + 3 + m)
                sc.activation(hid[:, m, :], ps[:, BANK[1 + m], 0:GN], ACT.Gelu, bias=b1[:, m:m + 1]).then_inc(act_done, 1)

            def h_high(k, u, m):
                g, _, _ = steps(k, u)
                act.wait_ge(weighed, J * g + m + 1)
                sc.activation(h_hi[:, m, :], hid[:, m, :], ACT.Copy).then_inc(h_hi_ok, 1)

            def tanh(k, u, n):
                g, _, _ = steps(k, u)
                act.wait_ge(gated, GATE * g + (7, 14)[n])
                sc.activation(gt[0:P, (1, 6)[n], :, :], gt[0:P, (0, 5)[n], :, :], ACT.Tanh, scale=0.5).then_inc(tanh_done, 1)

            def first():
                scale1(0, 0)
                for j in range(J):
                    z_hi(0, 0, j)
                scale1(0, 1)
                for j in range(J):
                    z_hi(0, 1, j)
                scale2(0, 0)
                for j in range(J):
                    xn_hi(0, 0, j)

            def body(k, u, more=2):
                g, _, _ = steps(k, u)
                act.wait_ge(ffn1_done, 5 * g + 1)
                after(act, lg_turned, g)
                sc.activation(logits_f[0:E, :], ps[0:E, BANK[0], 0:GN], ACT.Copy).then_inc(act_done, 1)
                after(act, h_lo_ok, 6 * (g - 1) + 1)
                sc.activation(hid[SH0:128, MC, :], ps[SH0:128, BANK[0], 0:GN], ACT.Gelu,
                              bias=b1[SH0:128, MC:MC + 1]).then_inc(act_done, 1)
                act.wait_ge(act_done, 6 * g + 2)
                sc.activation(h_hi[SH0:128, MC, :], hid[SH0:128, MC, :], ACT.Copy).then_inc(h_hi_ok, 1)
                gelu(k, u, 0)
                tanh(k, u, 0)
                gelu(k, u, 1)
                tanh(k, u, 1)
                if more == 2:
                    scale1(k, u + 2)
                gelu(k, u, 2)
                gelu(k, u, 3)
                act.wait_ge(comb_turned, g + 1)
                sc.activation(h_hi[0:E + SH, MC, :], ps[0:E + SH, SMALL, 0:GN], ACT.Copy).then_inc(h_hi_ok, 1)
                if more == 2:
                    z_hi(k, u + 2, 0)
                h_high(k, u, 0)
                h_high(k, u, 1)
                if more == 2:
                    z_hi(k, u + 2, 1)
                h_high(k, u, 2)
                h_high(k, u, 3)
                if more == 2:
                    z_hi(k, u + 2, 2)
                    z_hi(k, u + 2, 3)
                if more:
                    scale2(k, u + 1)
                    for j in range(J):
                        xn_hi(k, u + 1, j)

            pipeline(act, first, body, lambda k, u: body(k, u, more=G - 1 - u))

        @block.vector
        def _(dve):
            v = nc.vector

            v.memset(b1[0:SH0, MC:MC + 1], 0.0).then_inc(b1_clear, 1)
            dve.wait_ge(consts, 5)
            v.tensor_copy(row_iota_f[:, :], row_iota[:, :]).then_inc(copied, 1)
            dve.wait_ge(consts, 11)
            v.tensor_copy(ident16[:, :], ident[:, :]).then_inc(copied, 1)
            dve.wait_ge(idx_in, 32)
            v.tensor_copy(idx_rows_f[:, :, :], idx_rows[:, :, :]).then_inc(node_ready, 1)
            dve.wait_ge(idx_turned, 1)
            nodes = ps[0:P, 2, 0:2 * NB].rearrange("p (a b) -> p a b", a=2)
            v.tensor_copy(node_u[0:P, :, :], nodes).then_inc(node_ready, 1)
            v.tensor_copy(node_f[0:P, :, :], nodes).then_inc(node_ready, 1)
            dve.wait_ge(node_ready, 3)
            v.tensor_scalar(quot_r[0:P], node_f[0:P], -(T - 1) / 2.0, 1.0 / T, ALU.add, ALU.mult).then_inc(node_ready, 1)
            dve.wait_ge(node_ready, 4)
            v.tensor_scalar(quot[0:P], quot_r[0:P], ROUND, ROUND, ALU.add, ALU.subtract).then_inc(node_ready, 1)
            dve.wait_ge(node_ready, 5)
            v.scalar_tensor_tensor(out=rest[0:P], in0=quot[0:P], scalar=-float(T), in1=node_f[0:P],
                                   op0=ALU.mult, op1=ALU.add).then_inc(node_ready, 1)
            dve.wait_ge(copied, 1)

            def hot(out_ap, value, a, width):
                return v.tensor_tensor(out_ap, value[0:P, a, :].unsqueeze(2).to_broadcast((P, NB, width)),
                                       row_iota_f[0:P, 0:width].unsqueeze(1).to_broadcast((P, NB, width)), ALU.is_equal)

            def spread_over(value, s):
                return value[0:P, K * s:K * (s + 1)].unsqueeze(2).to_broadcast((P, K, T))

            hot(a_src[0:P], quot, 0, P).then_inc(hot_ready, 1)
            dve.wait_ge(node_ready, 6)
            hot(b_src[0:P], rest, 0, T).then_inc(hot_ready, 1)
            hot(a_dst16[0:P], quot, 1, P).then_inc(hot_ready, 1)
            dve.wait_ge(deg_counted, 1)
            v.tensor_scalar(deg[0:P, :], ps[0:P, 2, 128:128 + T], 1.0, None, ALU.add).then_inc(deg_ready, 1)
            v.tensor_scalar(degree[0:P, :], ps[0:P, 2, 128:128 + T], 1.0, None, ALU.add).then_inc(deg_ready, 1)
            hot(b_dst[0:P], rest, 1, T).then_inc(hot_ready, 1)

            def edge_same(s):
                if s >= 2:
                    dve.wait_ge(e_summed, K * (s - 1))
                for i in range(K):
                    b, first, w = K * s + i, same_cols(i, i).start, (K - i) * P
                    v.scalar_tensor_tensor(out=same[0:P, s % 2, first:first + w], in0=dst_bc[0:P, b * P:b * P + w],
                                           scalar=node_f[0:P, 1, b:b + 1], in1=not_before[0:P, 0:w], op0=ALU.is_equal,
                                           op1=ALU.mult, accum_out=matches[0:P, b:b + 1]).then_inc(same_ready, 1)

            def edge_last(s):
                cols = slice(K * s, K * (s + 1))
                dve.wait_ge(same_ready, K * (s + 1))
                v.scalar_tensor_tensor(out=last_row[0:P, cols], in0=matches[0:P, cols], scalar=1.0, in1=edge_row[0:P, cols],
                                       op0=ALU.is_equal, op1=ALU.mult).then_inc(last_ready, 1)
                dve.wait_ge(last_ready, 2 * s + 1)
                v.tensor_tensor(b_last[0:P, cols, :], b_dst[0:P, cols, :], spread_over(last_row, s), ALU.mult).then_inc(last_ready, 1)

            def edge_newest(s):
                here = ps[0:P, 5, s * T:(s + 1) * T]
                dve.wait_ge(last_spread, s + 1)
                if s == 0:
                    v.tensor_copy(newest[0:P, 0, :], here).then_inc(newest_ready, 1)
                    return
                dve.wait_ge(newest_ready, 2 * s - 1)
                v.scalar_tensor_tensor(out=kept[0:P, s, :], in0=here, scalar=0.0, in1=newest[0:P, s - 1, :],
                                       op0=ALU.is_equal, op1=ALU.mult).then_inc(newest_ready, 1)
                dve.wait_ge(newest_ready, 2 * s)
                v.tensor_tensor(newest[0:P, s, :], here, kept[0:P, s, :], ALU.add).then_inc(newest_ready, 1)

            def prior_pick(s):
                cols = slice(K * s, K * (s + 1))
                at = 4 * (s - 1)
                dve.wait_ge(prior_looked, s)
                v.tensor_tensor(b_prior[0:P, cols, :], ps[0:P, 6 + (s - 1) % 2, 0:K * T].rearrange("p (b t) -> p b t", t=T),
                                b_dst[0:P, cols, :], ALU.mult).then_inc(prior_rows, 1)
                dve.wait_ge(prior_rows, at + 1)
                v.tensor_reduce(prior_f[0:P, 0, cols], b_prior[0:P, cols, :], AX_X, ALU.add).then_inc(prior_rows, 1)
                dve.wait_ge(prior_rows, at + 2)
                v.tensor_scalar(prior_f[0:P, 1, cols], prior_f[0:P, 0, cols], 0.0, NOWHERE, ALU.is_equal, ALU.mult).then_inc(prior_rows, 1)
                dve.wait_ge(prior_rows, at + 3)
                v.scalar_tensor_tensor(out=prior_row[0:P, cols], in0=prior_f[0:P, 0, cols], scalar=-1.0,
                                       in1=prior_f[0:P, 1, cols], op0=ALU.add, op1=ALU.add).then_inc(prior_rows, 1)

            def deg_pick(s):
                cols = slice(K * s, K * (s + 1))
                dve.wait_ge(deg_looked, s + 1)
                v.tensor_tensor(picked[0:P, cols, :], ps[0:P, s, 0:K * T].rearrange("p (b t) -> p b t", t=T),
                                b_src[0:P, cols, :], ALU.mult).then_inc(deg_src_ready, 1)
                dve.wait_ge(deg_src_ready, 2 * s + 1)
                v.tensor_reduce(deg_src[0:P, cols], picked[0:P, cols, :], AX_X, ALU.add).then_inc(deg_src_ready, 1)

            def edge_stats(s):
                dve.wait_ge(xe_in[s], 16 * K)
                for b in range(K * s, K * (s + 1)):
                    v.bn_stats(e_stats[0:P, b, :], edge_rows(b)).then_inc(e_stats_ready, 1)
                for b in range(K * s, K * (s + 1)):
                    dve.wait_ge(e_stats_ready, b + 1)
                    v.bn_aggr(e_mv[0:P, b, :], e_stats[0:P, b, :]).then_inc(e_mv_ready, 1)

            def edge_lo(s):
                for b in range(K * s, K * (s + 1)):
                    dve.wait_ge(e_split_hi, b + 1)
                    v.tensor_tensor(low_edge_rows(b), edge_rows(b), f32(e_hi[0:P, s % 2, b - K * s, :]),
                                    ALU.subtract).then_inc(e_split_lo, 1)

            def edge_add(s):
                dve.wait_ge(prior_in, 16 * K * s)
                for i in range(K):
                    dve.wait_ge(e_summed, K * s + i + 1)
                    v.tensor_tensor(sums[0:P, s % 2, i, :], ps[0:P, i, :], sums[0:P, s % 2, i, :], ALU.add).then_inc(sum_ready, 1)

            dve.wait_ge(bc_in, 16)
            dve.wait_ge(consts, 12)
            edge_same(0)
            edge_last(0)
            edge_stats(0)
            for s in range(NS):
                deg_pick(s)
            edge_stats(1)
            edge_same(1)
            dve.wait_ge(at_ready, 6)
            dve.wait_ge(a_dst_ready, 1)
            dve.wait_ge(deg_src_ready, 2 * NS)
            dve.wait_ge(consts, 14)
            dve.wait_ge(at_turned, 10)
            v.memset(w1_n[:, :, MC, E:SH0], 0.0).then_inc(w1_clear, 1)
            edge_last(1)
            edge_newest(0)
            edge_lo(0)
            prior_pick(1)
            edge_stats(2)
            edge_lo(1)
            edge_newest(1)
            edge_same(2)
            edge_last(2)
            prior_pick(2)
            edge_stats(3)
            dve.wait_ge(w_in, 80)
            v.tensor_reduce(w_sum[:, :], wn[:, :, :], AX_X, ALU.add).then_inc(wsum_ready, 1)
            dve.wait_ge(wsum_ready, 1)
            v.tensor_tensor(w_sum[:, :], gb[:, :], w_sum[:, :], ALU.subtract).then_inc(wsum_ready, 1)
            dve.wait_ge(wsum_ready, 2)
            v.tensor_scalar(beta[:, :], w_sum[:, :], 1.0 / D, None, ALU.mult).then_inc(wsum_ready, 1)
            edge_add(1)
            edge_lo(2)
            edge_newest(2)
            edge_same(3)
            edge_last(3)
            prior_pick(3)
            edge_add(2)
            edge_newest(3)
            edge_lo(3)
            dve.wait_ge(dis_src_ready, 1)
            v.tensor_tensor(b_norm[0:P], b_dst[0:P], dis_src[0:P, :].unsqueeze(2).to_broadcast((P, NB, T)), ALU.mult).then_inc(b_norm_ready, 1)
            dve.wait_ge(newest_ready, 2 * NS - 1)
            v.tensor_scalar(no_edge[0:P, :], newest[0:P, NS - 1, :], 0.0, NOWHERE, ALU.is_equal, ALU.mult).then_inc(rows_ready, 1)
            dve.wait_ge(rows_ready, 1)
            v.scalar_tensor_tensor(out=table_row[0:P, :], in0=newest[0:P, NS - 1, :], scalar=-1.0, in1=no_edge[0:P, :],
                                   op0=ALU.add, op1=ALU.add).then_inc(rows_ready, 1)
            dve.wait_ge(prior_rows, 4 * (NS - 1))
            dve.wait_ge(s_summed, 1)
            v.memset(w2_n[0:SH0, MC, :], 0.0).then_inc(w2_clear, 1)
            for c in range(KC):
                dve.wait_ge(w_hi, c + 1)
                v.tensor_tensor(wg_lo[:, c, :], ps[:, W_BANK[c], :], f32(wg_hi[:, c, :]), ALU.subtract).then_inc(w_lo, 1)
            dve.wait_ge(w_turned, KC + 1)
            dve.wait_ge(w1_in, 16 * 2 * KC)
            v.tensor_copy(w1_n[:, :, MC, 0:E], ps[:, 7, 0:KC * E].rearrange("p (c e) -> p c e", e=E)).then_inc(gate_in, 1)
            dve.wait_ge(w_hi, KC + 1)
            v.tensor_tensor(w1_lo[:, :, :, :], w1_n[:, :, :, :], f32(w1_hi[:, :, :, :]), ALU.subtract).then_inc(w_lo, 1)
            edge_add(3)
            dve.wait_ge(dis_ready, T // NB)
            v.tensor_tensor(dis2[0:P, :], dis[0:P, :], dis[0:P, :], ALU.mult).then_inc(s_ready, 1)
            dve.wait_ge(s_ready, 1)
            v.tensor_tensor(dis2x2[0:P, :], dis2[0:P, :], dis2[0:P, :], ALU.add).then_inc(s_ready, 1)
            v.tensor_tensor(kept[0:P, 0, :], ps[0:P, 5, NS * T:(NS + 1) * T], dis[0:P, :], ALU.mult).then_inc(s_ready, 1)
            dve.wait_ge(s_ready, 3)
            v.tensor_tensor(s_node[0:P, :], kept[0:P, 0, :], dis2[0:P, :], ALU.add).then_inc(s_ready, 1)
            dve.wait_ge(w2_in, 64)
            v.tensor_scalar(w2_n[SH0:128, MC, :], w2_n[SH0:128, MC, :], 1.0 / SH, None, ALU.mult).then_inc(halved, 1)
            dve.wait_ge(w_hi, KC + 2)
            v.tensor_tensor(w2_lo[:, :, :], w2_n[:, :, :], f32(w2_hi[:, :, :]), ALU.subtract).then_inc(w_lo, 1)
            dve.wait_ge(table_in, 64 * NS)
            dve.wait_ge(s_ready, 4)
            v.memset(f32(h_hi[:, MC, :]), 0.0).then_inc(cleared, 1)
            v.memset(f32(h_lo[:, MC, :]), 0.0).then_inc(cleared, 1)
            v.memset(lg[0:P, :, E:E + TOP], LOWEST).then_inc(cleared, 1)
            v.memset(logits_f[:, :], 0.0).then_inc(cleared, 1)
            v.memset(comb[0:P, :, E:E + SH], 1.0 / SH).then_inc(cleared, 1)
            dve.wait_ge(cleared, 5)

            def stats1(k, u):
                g, slot, rnd = steps(k, u)
                dve.wait_ge(x_loaded[slot], 32 * (rnd + 1))
                after(dve, ln1_done, LN * g)
                for j in range(J):
                    v.bn_stats(st1[0:P, j, :], x_tile[slot][0:P, j, :]).then_inc(st1_done, 1)

            def add_edges(k, u):
                g, _, _ = steps(k, u)
                dve.wait_ge(u_in, 64 * (g + 1))
                for j in range(J):
                    dve.wait_ge(z_scaled, J * g + j + 1)
                    v.scalar_tensor_tensor(out=z_tile[0:P, j, :], in0=u_tile[0:P, j, :], scalar=sc1[0:P, 12, j:j + 1],
                                           in1=z_tile[0:P, j, :], op0=ALU.mult, op1=ALU.add).then_inc(z_ready, 1)

            def z_low(k, u, j):
                g, _, _ = steps(k, u)
                dve.wait_ge(zT_hi_ok, J * g + j + 1)
                hi = zT_hi[:, j, :, :].rearrange("p c q -> p (c q)")
                v.tensor_tensor(zT_lo[:, j, :, :].rearrange("p c q -> p (c q)"), ps[:, TR[j % 2], 0:KC * P], f32(hi),
                                ALU.subtract).then_inc(zT_lo_ok, 1)

            def xn_low(k, u, j):
                g, _, _ = steps(k, u)
                dve.wait_ge(xT_hi_ok, J * g + j + 1)
                v.tensor_tensor(xT_lo[:, :, j, :], ps[:, TR[j % 2], 0:KC * P].rearrange("p (c q) -> p c q", q=P),
                                f32(xT_hi[:, :, j, :]), ALU.subtract).then_inc(xT_lo_ok, 1)

            def residual1(k, u, j):
                g, slot, _ = steps(k, u)
                x_j = x_tile[slot][0:P, j, :]
                dve.wait_ge(gnn_done, J * g + j + 1)
                v.scalar_tensor_tensor(out=x_j, in0=ps[0:P, BANK[5 + j], :], scalar=0.0, in1=x_j,
                                       op0=ALU.max, op1=ALU.add).then_inc(x1_done, 1)
                if j == 0:
                    after(dve, ln2_done, (LN - 1) * g)
                dve.wait_ge(x1_done, J * g + j + 1)
                v.bn_stats(st2[0:P, j, :], x_j).then_inc(st2_done, 1)

            def residual2(k, u, j):
                g, slot, _ = steps(k, u)
                x_j = x_tile[slot][0:P, j, :]
                dve.wait_ge(ffn2_done, J * g + j + 1)
                v.tensor_tensor(x_j, ps[0:P, BANK[9 + j], :], x_j, ALU.add).then_inc(out_ready, 1)

            def weigh(k, u, m):
                g, _, _ = steps(k, u)
                dve.wait_ge(act_done, 6 * g + 3 + m)
                dve.wait_ge(spread, J * g + m + 1)
                v.tensor_tensor(hid[:, m, :], ps[:, SPREAD[m % 2], 0:GN], hid[:, m, :], ALU.mult).then_inc(weighed, 1)

            def h_low(k, u, m):
                g, _, _ = steps(k, u)
                dve.wait_ge(h_hi_ok, 6 * g + 3 + m)
                v.tensor_tensor(h_lo[:, m, :], hid[:, m, :], f32(h_hi[:, m, :]), ALU.subtract).then_inc(h_lo_ok, 1)

            def wide(col):
                return col.unsqueeze(2).to_broadcast((P, J, E))

            def gate_probs(k, u):
                g, _, _ = steps(k, u)
                at = GATE * g
                after(dve, gated, GATE * g)
                dve.wait_ge(lg_turned, g + 1)
                v.tensor_copy(lg[0:P, :, 0:E], ps[0:P, SMALL, :].rearrange("p (j e) -> p j e", e=128)[:, :, 0:E]).then_inc(gated, 1)
                dve.wait_ge(gated, at + 1)
                v.tensor_reduce(gs[0:P, 4, :], lg[0:P, :, 0:E], AX_X, ALU.max).then_inc(gated, 1)
                for j in range(J):
                    v.max(top8[0:P, j, :], lg[0:P, j, 0:E]).then_inc(gated, 1)
                dve.wait_ge(gated, at + 6)
                v.tensor_tensor(gt[0:P, 0], lg[0:P, :, 0:E], wide(gs[0:P, 4, :]), ALU.subtract).then_inc(gated, 1)
                v.memset(top8[0:P, :, TOP:8], LOWEST).then_inc(gated, 1)

            def gate_combine(k, u):
                g, _, _ = steps(k, u)
                at = GATE * g
                dve.wait_ge(tanh_done, 2 * g + 1)
                v.tensor_scalar(gt[0:P, 2], gt[0:P, 1], -1.0, 1.0, ALU.mult, ALU.add).then_inc(gated, 1)
                dve.wait_ge(gated, at + 9)
                v.reciprocal(gt[0:P, 3], gt[0:P, 2]).then_inc(gated, 1)
                dve.wait_ge(gated, at + 10)
                v.scalar_tensor_tensor(out=gt[0:P, 4], in0=gt[0:P, 1], scalar=1.0, in1=gt[0:P, 3],
                                       op0=ALU.add, op1=ALU.mult).then_inc(gated, 1)
                dve.wait_ge(gated, at + 11)
                v.tensor_reduce(gs[0:P, 0, :], gt[0:P, 4], AX_X, ALU.add).then_inc(gated, 1)
                dve.wait_ge(gated, at + 12)
                v.reciprocal(gs[0:P, 1, :], gs[0:P, 0, :]).then_inc(gated, 1)
                dve.wait_ge(gated, at + 13)
                v.scalar_tensor_tensor(out=gt[0:P, 5], in0=gt[0:P, 4], scalar=-1.0, in1=wide(gs[0:P, 1, :]),
                                       op0=ALU.add, op1=ALU.mult).then_inc(gated, 1)
                for j in range(J):
                    v.match_replace(left[0:P, j, :], top8[0:P, j, :], lg[0:P, j, :], -LOWEST).then_inc(gated, 1)
                dve.wait_ge(tanh_done, 2 * g + 2)
                v.tensor_scalar(gt[0:P, 7], gt[0:P, 6], -1.0, 1.0, ALU.mult, ALU.add).then_inc(gated, 1)
                dve.wait_ge(gated, at + 19)
                v.reciprocal(gt[0:P, 8], gt[0:P, 7]).then_inc(gated, 1)
                dve.wait_ge(gated, at + 20)
                v.scalar_tensor_tensor(out=gt[0:P, 9], in0=gt[0:P, 6], scalar=1.0, in1=gt[0:P, 8],
                                       op0=ALU.add, op1=ALU.mult).then_inc(gated, 1)
                dve.wait_ge(gated, at + 21)
                v.scalar_tensor_tensor(out=gt[0:P, 10], in0=left[0:P, :, 0:E], scalar=-LOWEST, in1=gt[0:P, 9],
                                       op0=ALU.is_equal, op1=ALU.mult).then_inc(gated, 1)
                dve.wait_ge(gated, at + 22)
                v.tensor_reduce(gs[0:P, 2, :], gt[0:P, 10], AX_X, ALU.add).then_inc(gated, 1)
                dve.wait_ge(gated, at + 23)
                v.reciprocal(gs[0:P, 3, :], gs[0:P, 2, :]).then_inc(gated, 1)
                dve.wait_ge(gated, at + 24)
                v.tensor_tensor(comb[0:P, :, 0:E], gt[0:P, 10], wide(gs[0:P, 3, :]), ALU.mult).then_inc(gated, 1)

            def first():
                stats1(0, 0)
                add_edges(0, 0)
                for j in range(J):
                    z_low(0, 0, j)
                stats1(0, 1)
                for j in range(J):
                    residual1(0, 0, j)
                add_edges(0, 1)
                for j in range(J):
                    z_low(0, 1, j)
                for j in range(J):
                    xn_low(0, 0, j)

            def body(k, u, more=2):
                g, _, _ = steps(k, u)
                if more == 2:
                    stats1(k, u + 2)
                gate_probs(k, u)
                dve.wait_ge(h_hi_ok, 6 * g + 1)
                v.tensor_tensor(h_lo[SH0:128, MC, :], hid[SH0:128, MC, :], f32(h_hi[SH0:128, MC, :]),
                                ALU.subtract).then_inc(h_lo_ok, 1)
                gate_combine(k, u)
                if more == 2:
                    add_edges(k, u + 2)
                if more:
                    residual1(k, u + 1, 0)
                dve.wait_ge(h_hi_ok, 6 * g + 2)
                v.tensor_tensor(h_lo[0:E + SH, MC, :], ps[0:E + SH, SMALL, 0:GN], f32(h_hi[0:E + SH, MC, :]),
                                ALU.subtract).then_inc(h_lo_ok, 1)
                if more:
                    residual1(k, u + 1, 1)
                if more == 2:
                    z_low(k, u + 2, 0)
                weigh(k, u, 0)
                weigh(k, u, 1)
                h_low(k, u, 0)
                h_low(k, u, 1)
                if more:
                    residual1(k, u + 1, 2)
                if more == 2:
                    z_low(k, u + 2, 1)
                weigh(k, u, 2)
                weigh(k, u, 3)
                if more:
                    residual1(k, u + 1, 3)
                h_low(k, u, 2)
                h_low(k, u, 3)
                if more == 2:
                    z_low(k, u + 2, 2)
                residual2(k, u, 0)
                if more == 2:
                    z_low(k, u + 2, 3)
                residual2(k, u, 1)
                if more:
                    xn_low(k, u + 1, 0)
                    xn_low(k, u + 1, 1)
                residual2(k, u, 2)
                if more:
                    xn_low(k, u + 1, 2)
                    xn_low(k, u + 1, 3)
                residual2(k, u, 3)

            pipeline(dve, first, body, lambda k, u: body(k, u, more=G - 1 - u))

        @block.tensor
        def _(pe):
            t = nc.tensor
            pe.wait_ge(node_ready, 1)
            pe.wait_ge(consts, 11)
            for a in range(2):
                op = t.transpose(ps[0:P, 2, a * NB:(a + 1) * NB], idx_rows_f[:, a, :], ident[0:NB, 0:NB])
            op.then_inc(idx_turned, 1)

            def turn_at(n, source, bank):
                for i in range(4):
                    op = t.matmul(ps[0:P, bank, i * P:(i + 1) * P], source[0:P, n % 5 * 4 + i, :], ident16[0:P, 0:P],
                                  start=True, stop=True)
                op.then_inc(at_turned, 1)

            pe.wait_ge(hot_ready, 1)
            pe.wait_ge(copied, 2)
            for n in range(5):
                turn_at(n, a_src, 3 + n)
            pe.wait_ge(hot_ready, 2)
            for b in range(NB):
                op = t.matmul(ps[0:P, 2, 128:128 + T], a_src[0:P, b, :], b_src[0:P, b, :], start=b == 0, stop=b == NB - 1)
            op.then_inc(deg_counted, 1)
            pe.wait_ge(deg_ready, 2)
            for s in range(NS):
                if s == 3:
                    pe.wait_ge(at_ready, 1)
                for i in range(K):
                    b = K * s + i
                    pe.wait_ge(at_ready, b // 4 + 1)
                    op = t.matmul(ps[0:P, s, i * T:(i + 1) * T], at_src[0:P, b * P:(b + 1) * P], deg[0:P, :], start=True, stop=True)
                op.then_inc(deg_looked, 1)
            pe.wait_ge(hot_ready, 3)
            for n in range(5, 10):
                pe.wait_ge(at_ready, 5 if n < 8 else n - 2)
                turn_at(n, a_dst16, 5 + (n - 5) % 3)

            def spread_last(s):
                if s == 0:
                    pe.wait_ge(at_ready, 9)
                    pe.wait_ge(a_dst_ready, 1)
                pe.wait_ge(last_ready, 2 * s + 2)
                for i in range(K):
                    b = K * s + i
                    op = t.matmul(ps[0:P, 5, s * T:(s + 1) * T], a_dst[0:P, b, :], b_last[0:P, b, :], start=i == 0, stop=i == K - 1)
                op.then_inc(last_spread, 1)

            def look_prior(s):
                pe.wait_ge(newest_ready, 2 * s - 1)
                if s == 1:
                    pe.wait_ge(at_ready, 10)
                if s == 3:
                    pe.wait_ge(prior_rows, 1)
                for i in range(K):
                    b = K * s + i
                    op = t.matmul(ps[0:P, 6 + (s - 1) % 2, i * T:(i + 1) * T], at_dst[0:P, b * P:(b + 1) * P],
                                  newest[0:P, s - 1, :], start=True, stop=True)
                op.then_inc(prior_looked, 1)

            def sum_edges(s):
                for i in range(K):
                    pe.wait_ge(same_ready, K * s + i + 1)
                    pe.wait_ge(e_split_lo, K * s + i + 1)
                    if s:
                        pe.wait_ge(sum_ready, K * (s - 1) + i + 1)
                    elif i < NS:
                        pe.wait_ge(deg_src_ready, 2 * i + 1)
                    for i2 in range(i + 1):
                        for low in range(2):
                            rhs = low_edge_rows(K * s + i2) if low else e_hi[0:P, s % 2, i2, :]
                            op = t.matmul(ps[0:P, i, :], same[0:P, s % 2, same_cols(i2, i)], rhs,
                                          start=i2 == 0 and not low, stop=i2 == i and low == 1)
                    op.then_inc(e_summed, 1)

            spread_last(0)
            for s in range(NS):
                if s + 1 < NS:
                    look_prior(s + 1)
                sum_edges(s)
                if s + 1 < NS:
                    spread_last(s + 1)
            pe.wait_ge(b_norm_ready, 1)
            for b in range(NB):
                op = t.matmul(ps[0:P, 5, NS * T:(NS + 1) * T], a_dst[0:P, b, :], b_norm[0:P, b, :], start=b == 0, stop=b == NB - 1)
            op.then_inc(s_summed, 1)

            pe.wait_ge(w_biased, KC)
            for c in range(KC):
                if c >= 2:
                    pe.wait_ge(w_lo, c - 1)
                else:
                    pe.wait_ge(prior_rows, 4 * (NS - 1))
                for o in range(KC):
                    op = t.transpose(ps[:, W_BANK[c], o * 128:(o + 1) * 128], wn[:, o, c * 128:(c + 1) * 128], ident[:, :])
                op.then_inc(w_turned, 1)
            pe.wait_ge(w_lo, KC)
            for c in range(KC):
                op = t.transpose(ps[:, 7, c * E:(c + 1) * E], gate_n[:, c * 128:(c + 1) * 128], ident[0:E, 0:E])
            op.then_inc(w_turned, 1)

            def turn_z(k, u, j):
                g, _, _ = steps(k, u)
                pe.wait_ge(z_ready, J * g + j + 1)
                if j >= 2:
                    pe.wait_ge(zT_lo_ok, J * g + j - 1)
                else:
                    after(pe, xT_lo_ok, J * (g - 2) + j + 3)
                for c in range(KC):
                    op = t.transpose(ps[:, TR[j % 2], c * P:(c + 1) * P], z_tile[0:P, j, c * 128:(c + 1) * 128],
                                     ident[0:P, 0:P])
                op.then_inc(z_turned, 1)

            def turn_xn(k, u, j, more):
                g, _, _ = steps(k, u)
                pe.wait_ge(xn_ready, J * g + j + 1)
                if j >= 2:
                    pe.wait_ge(xT_lo_ok, J * g + j - 1)
                elif more:
                    pe.wait_ge(zT_lo_ok, J * (g + 1) + j + 3)
                for c in range(KC):
                    op = t.transpose(ps[:, TR[j % 2], c * P:(c + 1) * P], xn_tile[0:P, j, c * 128:(c + 1) * 128],
                                     ident[0:P, 0:P])
                op.then_inc(xn_turned, 1)

            def gnn(k, u, j, steady=True):
                g, _, _ = steps(k, u)
                pe.wait_ge(zT_lo_ok, J * g + j + 1)
                if steady:
                    if j < 3:
                        pe.wait_ge(act_done, 6 * (g - 1) + 4 + j)
                    else:
                        pe.wait_ge(x1_done, J * g + 1)
                elif j == 3:
                    pe.wait_ge(x1_done, 1)
                n = 0
                for lhs, rhs in passes(zT_hi, zT_lo, wg_hi, wg_lo):
                    for c in range(KC):
                        op = t.matmul(ps[0:P, BANK[5 + j], :], lhs[:, j, c, :], rhs[:, c, :], start=n == 0, stop=n == 3 * KC - 1)
                        n += 1
                op.then_inc(gnn_done, 1)

            def ffn1(k, u, m):
                g, _, _ = steps(k, u)
                pos = (m + 1) % (MC + 1)
                if pos == 0:
                    pe.wait_ge(xT_lo_ok, J * (g + 1))
                    after(pe, out_ready, J * (g - 1) + 1)
                    pe.wait_ge(x1_done, J * (g + 1))
                elif pos == 1:
                    after(pe, out_ready, J * (g - 1) + 4)
                elif pos >= 3:
                    pe.wait_ge(act_done, 6 * g + pos - 1)
                n = 0
                for lhs, rhs in ((w1_hi, xT_hi), (w1_lo, xT_hi), (w1_hi, xT_lo)):
                    for c in range(KC):
                        op = t.matmul(ps[:, BANK[pos], 0:GN], lhs[:, c, m, :], rhs[:, c, :, :].rearrange("p j q -> p (j q)"),
                                      start=n == 0, stop=n == 3 * KC - 1)
                        n += 1
                op.then_inc(ffn1_done, 1)

            def ffn2(k, u, j, more):
                g, _, _ = steps(k, u)
                if more and j < 3:
                    pe.wait_ge(x1_done, J * (g + 1) + j + 2)
                if j == 3:
                    pe.wait_ge(out_ready, J * g + 2)
                order = [MC] + list(range(MC))
                n = 0
                for m in order:
                    if j == 0 and m < MC:
                        pe.wait_ge(h_lo_ok, 6 * g + 3 + m)
                    cols = slice(j * P, (j + 1) * P)
                    for lhs, rhs in passes(h_hi, h_lo, w2_hi, w2_lo):
                        op = t.matmul(ps[0:P, BANK[9 + j], :], lhs[:, m, cols], rhs[:, m, :],
                                      start=n == 0, stop=n == 3 * (MC + 1) - 1)
                        n += 1
                op.then_inc(ffn2_done, 1)

            def turn_logits(k, u):
                g, _, _ = steps(k, u)
                pe.wait_ge(act_done, 6 * g + 1)
                after(pe, h_lo_ok, 6 * (g - 1) + 2)
                for j in range(J):
                    op = t.transpose(ps[0:P, SMALL, j * 128:(j + 1) * 128], logits_f[:, j * P:(j + 1) * P], ident[:, :])
                op.then_inc(lg_turned, 1)

            def turn_comb(k, u):
                g, _, _ = steps(k, u)
                pe.wait_ge(gated, GATE * (g + 1))
                for j in range(J):
                    op = t.transpose(ps[0:E + SH, SMALL, j * P:(j + 1) * P], comb[0:P, j, :], ident[0:P, 0:P])
                op.then_inc(comb_turned, 1)

            def spread_comb(k, u, m):
                g, _, _ = steps(k, u)
                if m == 0:
                    pe.wait_ge(h_lo_ok, 6 * g + 2)
                if m >= 2:
                    pe.wait_ge(weighed, J * g + m - 1)
                else:
                    after(pe, weighed, J * (g - 1) + m + 3)
                for n, part in enumerate((h_hi, h_lo)):
                    op = t.matmul(ps[:, SPREAD[m % 2], 0:GN], expert_of[:, m, :], part[:, MC, :], start=n == 0, stop=n == 1)
                op.then_inc(spread, 1)

            def first():
                pe.wait_ge(w_lo, KC + 2)
                pe.wait_ge(cleared, 5)
                for j in range(J):
                    turn_z(0, 0, j)
                for j in range(J):
                    gnn(0, 0, j, steady=False)
                for j in range(J):
                    turn_z(0, 1, j)
                for j in range(J):
                    turn_xn(0, 0, j, True)

            def body(k, u, more=2):
                ffn1(k, u, MC)
                ffn1(k, u, 0)
                turn_logits(k, u)
                for m in range(1, MC):
                    ffn1(k, u, m)
                if more:
                    gnn(k, u + 1, 0)
                turn_comb(k, u)
                if more:
                    gnn(k, u + 1, 1)
                spread_comb(k, u, 0)
                spread_comb(k, u, 1)
                if more == 2:
                    turn_z(k, u + 2, 0)
                if more:
                    gnn(k, u + 1, 2)
                spread_comb(k, u, 2)
                spread_comb(k, u, 3)
                if more == 2:
                    turn_z(k, u + 2, 1)
                if more:
                    gnn(k, u + 1, 3)
                if more == 2:
                    turn_z(k, u + 2, 2)
                ffn2(k, u, 0, more)
                if more == 2:
                    turn_z(k, u + 2, 3)
                ffn2(k, u, 1, more)
                if more:
                    turn_xn(k, u + 1, 0, more == 2)
                    turn_xn(k, u + 1, 1, more == 2)
                ffn2(k, u, 2, more)
                if more:
                    turn_xn(k, u + 1, 2, more == 2)
                    turn_xn(k, u + 1, 3, more == 2)
                ffn2(k, u, 3, more)

            pipeline(pe, first, body, lambda k, u: body(k, u, more=G - 1 - u))


_INS = ["x", "src", "dst", "L0_gnn_W", "L0_gnn_b", "L0_ffn_gate_w", "L0_ffn_re_w1", "L0_ffn_re_b1", "L0_ffn_re_w2",
        "L0_ffn_re_b2", "L0_ffn_se_w1", "L0_ffn_se_b1", "L0_ffn_se_w2", "L0_ffn_se_b2"]


def kernel(**inputs):
    import numpy as _np
    import concourse.bacc as _bacc
    from concourse import mybir as _mybir
    from concourse.bass_utils import run_bass_kernel_spmd as _run

    nc = _bacc.Bacc("TRN2", target_bir_lowering=False, num_devices=1)
    arrays, args = {}, []
    for name in _INS:
        a = _np.ascontiguousarray(inputs[name])
        arrays[f"in_{name}"] = a
        args.append(nc.dram_tensor(f"in_{name}", a.shape, _mybir.dt.from_np(a.dtype), kind="ExternalInput").ap())
    shape = _np.shape(inputs["x"])
    args.append(nc.dram_tensor("out_0", shape, _mybir.dt.float32, kind="ExternalOutput").ap())
    gnn_moe(nc, *args)
    r = _run(nc, [arrays], core_ids=[0])
    return r.results[0]["out_0"]
```

```python
from contextlib import ExitStack

import concourse.bass as bass
from concourse import mybir

F32 = mybir.dt.float32
F32R = mybir.dt.float32r
BF16 = mybir.dt.bfloat16
I32 = mybir.dt.int32
U32 = mybir.dt.uint32
ALU = mybir.AluOpType
ACT = mybir.ActivationFunctionType
AX_X = mybir.AxisListType.X

EPS = 1e-5
ROUND = 12582912.0
NOWHERE = 1048576.0
LOWEST = -3.0e38


def gnn_moe(nc, x, src, dst, gnn_w, gnn_b, gate_w, re_w1, re_b1, re_w2, re_b2, se_w1, se_b1, se_w2, se_b2, out):
    N, D = x.shape
    NE = src.shape[0]
    E, _, F = re_w1.shape
    SH = se_w1.shape[0]
    TOP = 4
    KC = D // 128
    J = 4
    P = 125
    T = N // P
    G = T // J
    GN = P * J
    NB = NE // P
    K = 5
    NS = NB // K
    SB = K * P
    MC = E * F // 128
    SF = SH * F
    SH0 = 128 - SF
    LOW = 32
    CW = LOW + E
    LN1, LN2 = 13, 12
    XS = 4
    HALF = 112
    assert N == P * T and T == J * G and NE == P * NB and NB == K * NS and E * F == 128 * MC and SH == 2

    x_v = x.rearrange("(p t) d -> p (t d)", t=T)
    out_v = out.rearrange("(p t) d -> p (t d)", t=T)
    table = nc.dram_tensor("edge_sums", [NE, D], F32, kind="Internal").ap()

    ctx = ExitStack()
    with ctx:
        def sb(name, shape, dt=F32, scope=ctx):
            return scope.enter_context(nc.sbuf_tensor(name, shape, dt))

        def sem(name):
            return ctx.enter_context(nc.semaphore(name))

        ps = ctx.enter_context(nc.psum_tensor("ps", [128, 8, 512], F32))

        in_place = ExitStack()
        low_rows = [sb(f"low_rows{i}", [128, J, D], F32R, in_place) for i in range(XS)]
        in_place.close()
        x_tile = [sb(f"x_tile{i}", [128, J, D]) for i in range(XS)]
        b1 = sb("b1", [128, MC + 1])
        ident = sb("ident", [128, 128])
        expert_of = sb("expert_of", [128, MC, 128], F32R)
        neg_half = sb("neg_half", [128, NB])
        half, inv_128, eps4, zero4 = sb("half", [128, J]), sb("inv_128", [128, J]), sb("eps4", [128, J]), sb("zero4", [128, J])
        dis, dis2x2 = sb("dis", [128, T]), sb("dis2x2", [128, T])
        s_node = sb("s_node", [128, T])
        table_row = sb("table_row", [128, T], U32)

        neg_low = sb("neg_low", [128, 1])
        gb, w_sum, beta = sb("gb", [128, KC]), sb("w_sum", [128, KC]), sb("beta", [128, KC])

        early = ExitStack()
        at_src = sb("at_src", [128, NE], F32, early)
        a_src = sb("a_src", [128, NB, P], BF16, early)
        b_src = sb("b_src", [128, NB, T], BF16, early)
        a_dst16 = sb("a_dst16", [128, NB, P], BF16, early)
        picked = sb("picked", [128, NB, T], F32, early)
        idx_rows = sb("idx_rows", [NB, 2, P], I32, early)
        idx_rows_f = sb("idx_rows_f", [NB, 2, P], F32, early)
        row_iota = sb("row_iota", [128, 128], I32, early)
        row_iota_f = sb("row_iota_f", [128, 128], F32, early)
        ident16 = sb("ident16", [128, 128], BF16, early)
        expert_f = sb("expert_f", [128, MC, 128], F32, early)
        quot = sb("quot", [128, 2, NB], F32, early)
        quot_r = sb("quot_r", [128, 2, NB], F32, early)
        rest = sb("rest", [128, 2, NB], F32, early)
        deg = sb("deg", [128, T], F32, early)
        filler = sb("filler", [128, 320], F32, early)
        at_dst = sb("at_dst", [128, NE], F32, early)
        a_dst = sb("a_dst", [128, NB, P], F32, early)
        b_norm = sb("b_norm", [128, NB, T], F32, early)
        b_dst = sb("b_dst", [128, NB, T], F32, early)
        b_last = sb("b_last", [128, NB, T], F32, early)
        b_prior = sb("b_prior", [128, NB, T], F32, early)
        dst_bc = sb("dst_bc", [128, NE], I32, early)
        not_before = sb("not_before", [128, SB], F32, early)
        node_f = sb("node_f", [128, 2, NB], F32, early)
        node_u = sb("node_u", [128, 2, NB], U32, early)
        deg_src = sb("deg_src", [128, NB], F32, early)
        dis_src = sb("dis_src", [128, NB], F32, early)
        degree = sb("degree", [128, T], F32, early)
        dis2 = sb("dis2", [128, T], F32, early)
        edge_row = sb("edge_row", [128, NB], I32, early)
        matches = sb("matches", [128, NB], F32, early)
        last_row = sb("last_row", [128, NB], F32, early)
        kept = sb("kept", [128, NS, T], F32, early)
        newest = sb("newest", [128, NS, T], F32, early)
        no_edge = sb("no_edge", [128, T], F32, early)
        prior_f = sb("prior_f", [128, 2, NB], F32, early)
        prior_row = sb("prior_row", [128, NB], U32, early)
        with ExitStack() as in_place:
            low_more = sb("low_more", [128, NB - XS * J, D], F32R, in_place)
        x_more = sb("x_more", [128, NB - XS * J, D], F32, early)
        e_hi = sb("e_hi", [128, 2, K, D], F32R, early)
        same = sb("same", [128, 2, (K * (K + 1) // 2) * P], F32R, early)
        sums = sb("sums", [128, 2, K, D], F32, early)
        e_stats = sb("e_stats", [128, NB, 6], F32, early)
        e_mv = sb("e_mv", [128, NB, 2], F32, early)
        e_sc = sb("e_sc", [128, 5, NB], F32, early)
        wn = sb("wn", [128, KC, D], F32, early)
        gate_n = sb("gate_n", [E, D], F32, early)
        early.close()
        wg_lo = sb("wg_lo", [128, KC, D], F32R)
        with ExitStack() as as_read:
            w1_n = sb("w1_n", [128, KC, MC + 1, 128], F32, as_read)
        w1_lo = sb("w1_lo", [128, KC, MC + 1, 128], F32R)
        w1_hi = sb("w1_hi", [128, KC, MC + 1, 128], F32R)
        wg_hi = sb("wg_hi", [128, KC, D], F32R)
        with ExitStack() as as_read:
            w2_n = sb("w2_n", [128, MC + 1, D], F32, as_read)
        w2_lo, w2_hi = sb("w2_lo", [128, MC + 1, D], F32R), sb("w2_hi", [128, MC + 1, D], F32R)

        logits_f = sb("logits_f", [E, GN])
        row_idx = sb("row_idx", [128, J], U32)
        st1, sc1 = sb("st1", [128, J, 6]), sb("sc1", [128, LN1, J])
        st2, sc2 = sb("st2", [128, J, 6]), sb("sc2", [128, LN1, J])
        lg = sb("lg", [128, J, E + TOP])
        top8 = sb("top8", [128, J, 8])
        left = sb("left", [128, J, E + TOP])
        gt = sb("gt", [128, 12, J, E])
        gs = sb("gs", [128, 5, J])
        comb = sb("comb", [128, J, 128])
        u_tile = sb("u_tile", [128, J, D])
        z_tile = sb("z_tile", [128, J, D])
        zT_hi, zT_lo = sb("zT_hi", [128, J, KC, P], F32R), sb("zT_lo", [128, J, KC, P], F32R)
        xn_tile = sb("xn_tile", [128, J, D])
        xT_hi, xT_lo = sb("xT_hi", [128, KC, J, P], F32R), sb("xT_lo", [128, KC, J, P], F32R)
        hid = sb("hid", [128, MC + 1, GN])
        h_hi, h_lo = sb("h_hi", [128, MC + 1, GN], F32R), sb("h_lo", [128, MC + 1, GN], F32R)
        b2_n = sb("b2_n", [128, D])
        sb2_n = sb("sb2_n", [128, SH, D])
        b2_hi = sb("b2_hi", [128, D], F32R)

        idx_in, bc_in, w_in, w1_in, w2_in = sem("idx_in"), sem("bc_in"), sem("w_in"), sem("w1_in"), sem("w2_in")
        consts, copied, idx_turned, node_ready = sem("consts"), sem("copied"), sem("idx_turned"), sem("node_ready")
        hot_ready, at_turned, at_ready, a_dst_ready = sem("hot_ready"), sem("at_turned"), sem("at_ready"), sem("a_dst_ready")
        deg_counted, deg_ready, deg_looked, deg_src_ready = (
            sem("deg_counted"), sem("deg_ready"), sem("deg_looked"), sem("deg_src_ready"))
        same_ready, last_ready, last_spread, newest_ready = (
            sem("same_ready"), sem("last_ready"), sem("last_spread"), sem("newest_ready"))
        prior_looked, prior_rows, rows_ready = sem("prior_looked"), sem("prior_rows"), sem("rows_ready")
        dis_src_ready, dis_ready, b_norm_ready, s_summed, s_ready = (
            sem("dis_src_ready"), sem("dis_ready"), sem("b_norm_ready"), sem("s_summed"), sem("s_ready"))
        main_free, w1_clear, b1_clear = sem("main_free"), sem("w1_clear"), sem("b1_clear")
        wsum_ready, w_biased, w_turned, w_hi, w_lo, gate_in, halved, cleared = (
            sem("wsum_ready"), sem("w_biased"), sem("w_turned"), sem("w_hi"), sem("w_lo"), sem("gate_in"), sem("halved"), sem("cleared"))
        b2_clear, b2_in, b2_ready, b2_high, b2_placed = (
            sem("b2_clear"), sem("b2_in"), sem("b2_ready"), sem("b2_high"), sem("b2_placed"))

        xe_in = [sem(f"xe_in{s}") for s in range(NS)]
        e_stats_ready, e_mv_ready, e_scalars, e_normed = sem("e_stats_ready"), sem("e_mv_ready"), sem("e_scalars"), sem("e_normed")
        e_split_hi, e_split_lo, e_summed = sem("e_split_hi"), sem("e_split_lo"), sem("e_summed")
        prior_in = [sem(f"prior_in{i}") for i in range(K)]
        prior_clear, sum_ready, table_in = sem("prior_clear"), sem("sum_ready"), sem("table_in")
        x_loaded = [sem(f"x_loaded{i}") for i in range(XS)]
        stored = [sem(f"stored{i}") for i in range(XS)]
        last_stored = sem("last_stored")
        u_zeroed, u_in, idx_copied = sem("u_zeroed"), sem("u_in"), sem("idx_copied")
        st1_done, ln1_done = sem("st1_done"), sem("ln1_done")
        z_scaled, z_ready, z_turned = sem("z_scaled"), sem("z_ready"), sem("z_turned")
        zT_hi_ok, zT_lo_ok = sem("zT_hi_ok"), sem("zT_lo_ok")
        gnn_done, x1_done = sem("gnn_done"), sem("x1_done")
        st2_done, ln2_done = sem("st2_done"), sem("ln2_done")
        xn_ready, xn_turned = sem("xn_ready"), sem("xn_turned")
        xT_hi_ok, xT_lo_ok = sem("xT_hi_ok"), sem("xT_lo_ok")
        ffn1_done, act_done = sem("ffn1_done"), sem("act_done")
        lg_turned, gated, tanh_done = sem("lg_turned"), sem("gated"), sem("tanh_done")
        comb_turned, h_hi_ok, h_lo_ok = sem("comb_turned"), sem("h_hi_ok"), sem("h_lo_ok")
        spread, weighed = sem("spread"), sem("weighed")
        ffn2_done, out_ready = sem("ffn2_done"), sem("out_ready")
        GATE = 25

        ACC = [0, 1, 2]
        BANK = [ACC[i] for i in (0, 1, 2, 0, 1, 2, 0, 1, 2, 0, 1, 2, 1)]
        TR = [3, 4]
        SPREAD = [5, 6]
        SMALL = 7

        DEG_COL, S_COL, GATE_COL = 128, NS * T, (NS + 1) * T
        W_BANK = [6, 7, 6, 7]

        def after(eng, semaphore, value):
            if isinstance(value, int) and value <= 0:
                return
            eng.wait_ge(semaphore, value)

        def f32(ap):
            return ap.bitcast(F32)

        def steps(k, u):
            return XS * k + u, u % XS, k + u // XS

        def pipeline(eng, first, body, last):
            first()
            for u in range(2):
                body(0, u)
            with eng.Fori(0, (G - 4) // XS) as k:
                for u in range(2, 2 + XS):
                    body(k, u)
            for u in range(G - 2, G):
                last(0, u)

        def edge_rows(b):
            return x_tile[b // J][0:P, b % J, :] if b < XS * J else x_more[0:P, b - XS * J, :]

        def low_edge_rows(b):
            return low_rows[b // J][0:P, b % J, :] if b < XS * J else low_more[0:P, b - XS * J, :]

        def same_cols(i, i2):
            at = (i * K - i * (i - 1) // 2 + i2 - i) * P
            return slice(at, at + P)

        def passes(hi_l, lo_l, hi_r, lo_r):
            return ((hi_l, hi_r), (lo_l, hi_r), (hi_l, lo_r))

        block = ctx.enter_context(nc.Block())

        @block.sync
        def _(sp):
            sp.dma_start(idx_rows[:, 0, :], src.rearrange("(b q) -> b q", q=P)).then_inc(idx_in, 16)
            sp.dma_start(idx_rows[:, 1, :], dst.rearrange("(b q) -> b q", q=P)).then_inc(idx_in, 16)
            sp.dma_start(dst_bc[0:P, :], dst.rearrange("(a e) -> a e", a=1).to_broadcast((P, NE))).then_inc(bc_in, 16)
            sp.dma_start(b1[:, 0:MC], re_b1.rearrange("(m a) f -> (a f) m", m=MC), allow_slow_non_contiguous=True).then_inc(w_in, 16)
            sp.dma_start(wn[:, :, :], gnn_w.rearrange("(c p) i -> p c i", p=128)).then_inc(w_in, 16)
            sp.dma_start(gate_n[:, :], gate_w).then_inc(w_in, 16)
            sp.dma_start(gb[:, :], gnn_b.rearrange("(c p) -> p c", p=128), allow_slow_non_contiguous=True).then_inc(w_in, 16)
            sp.wait_ge(b1_clear, 1)
            sp.dma_start(b1[SH0:128, MC:MC + 1], se_b1.rearrange("j (f a) -> (j f) a", a=1), allow_slow_non_contiguous=True).then_inc(w_in, 16)

            def write_sums(s):
                for b_start, b_end in ((0, 3), (3, K)):
                    sp.wait_ge(sum_ready, K * s + b_end)
                    rows_v = table[(K * s + b_start) * P:(K * s + b_end) * P, :].rearrange("(i q) d -> q i d", q=P)
                    for rows in (slice(0, HALF), slice(HALF, P)):
                        sp.dma_start(rows_v[rows, :, :], sums[rows, s % 2, b_start:b_end, :]).then_inc(table_in, 16)

            def load(k, u):
                g, slot, rnd = steps(k, u)
                after(sp, stored[slot], 32 * rnd)
                for rows in (slice(0, HALF), slice(HALF, P)):
                    sp.dma_start(x_tile[slot][rows, :, :].rearrange("p j d -> p (j d)"),
                                 x_v[rows, bass.ds(g * J * D, J * D)]).then_inc(x_loaded[slot], 16)

            def store(k, u):
                g, slot, rnd = steps(k, u)
                sp.wait_ge(out_ready, J * (g + 1))
                for rows in (slice(0, HALF), slice(HALF, P)):
                    sp.dma_start(out_v[rows, bass.ds(g * J * D, J * D)],
                                 x_tile[slot][rows, :, :].rearrange("p j d -> p (j d)")).then_inc(stored[slot], 16)

            def first():
                sp.wait_ge(w1_clear, 1)
                for c in range(KC):
                    rows = slice(c * 128, (c + 1) * 128)
                    sp.dma_start(w1_n[:, c, 0:MC, :].rearrange("p m (a f) -> p (m a) f", f=F),
                                 re_w1[:, rows, :].rearrange("e p f -> p e f")).then_inc(w1_in, 16)
                    sp.dma_start(w1_n[:, c, MC, SH0:128].rearrange("p (j f) -> p j f", f=F),
                                 se_w1[:, rows, :].rearrange("j p f -> p j f")).then_inc(w1_in, 16)
                for s in range(NS - 1):
                    write_sums(s)
                    sp.wait_ge(e_summed, K * (s + 1))
                    load(0, s)
                write_sums(NS - 1)
                sp.wait_ge(u_in, 16 * J)
                sp.wait_ge(main_free, 1)
                sp.dma_start(w2_n[:, 0:MC, :], re_w2.rearrange("(m a) f d -> (a f) m d", m=MC)).then_inc(w2_in, 16)
                for row in (0, SH0):
                    sp.dma_start(w2_n[row:row + SF, MC, :], se_w2.rearrange("j f d -> (j f) d")).then_inc(w2_in, 16)
                sp.wait_ge(b2_clear, 1)
                for row in (0, E, LOW):
                    sp.dma_start(b2_n[row:row + E, :], re_b2).then_inc(b2_in, 16)
                sp.dma_start(sb2_n[0:CW, :, :].rearrange("p j d -> p (j d)"),
                             se_b2.rearrange("(a j) d -> a (j d)", a=1).to_broadcast((CW, SH * D))).then_inc(b2_in, 16)
                sp.wait_ge(e_summed, K * NS)
                load(0, NS - 1)

            def body(k, u):
                store(k, u)
                load(k, u + XS)

            first()
            with sp.Fori(0, (G - XS) // XS) as k:
                for u in range(XS):
                    body(k, u)
            for u in range(G - XS, G - 1):
                store(0, u)
            for j in range(J):
                sp.wait_ge(out_ready, J * (G - 1) + j + 1)
                at = ((G - 1) * J + j) * D
                for rows in (slice(0, HALF), slice(HALF, P)):
                    sp.dma_start(out_v[rows, at:at + D], x_tile[(G - 1) % XS][rows, j, :]).then_inc(last_stored, 16)
            for slot in range(XS):
                sp.wait_ge(stored[slot], 32 * len(range(slot, G - 1, XS)))
            sp.wait_ge(last_stored, 32 * J)

        @block.gpsimd
        def _(pool):
            gp = nc.gpsimd
            gp.memset(ident[:, :], 0.0).then_inc(consts, 1)
            gp.memset(expert_f[:, :, :], 0.0).then_inc(consts, 1)
            gp.memset(not_before[:, :], 1.0).then_inc(consts, 1)
            gp.memset(neg_half[:, :], -0.5).then_inc(consts, 1)
            gp.iota(row_iota[:, :], [[1, 128]], base=0, channel_multiplier=0).then_inc(consts, 1)
            gp.iota(edge_row[:, :], [[P, NB]], base=1, channel_multiplier=1).then_inc(consts, 1)
            gp.memset(half[:, :], 0.5).then_inc(consts, 1)
            gp.memset(inv_128[:, :], 4.0 / D).then_inc(consts, 1)
            gp.memset(eps4[:, :], 4.0 * EPS).then_inc(consts, 1)
            gp.memset(zero4[:, :], 0.0).then_inc(consts, 1)
            gp.memset(neg_low[:, :], 0.0).then_inc(consts, 1)
            pool.wait_ge(consts, 11)
            gp.affine_select(out=ident[:, :], in_=ident[:, :], compare_op=ALU.not_equal, fill=1.0, base=0,
                             pattern=[[-1, 128]], channel_multiplier=1).then_inc(consts, 1)
            gp.affine_select(out=not_before[0:P, 0:P], in_=not_before[0:P, 0:P], compare_op=ALU.is_ge,
                             fill=0.0, base=0, pattern=[[1, P]], channel_multiplier=-1).then_inc(consts, 1)
            gp.affine_select(out=expert_f[:, :, :].rearrange("p m (a f) -> p m a f", f=F),
                             in_=expert_f[:, :, :].rearrange("p m (a f) -> p m a f", f=F),
                             compare_op=ALU.not_equal, fill=1.0, base=0,
                             pattern=[[-(128 // F), MC], [-1, 128 // F], [0, F]], channel_multiplier=1).then_inc(consts, 1)
            gp.affine_select(out=neg_low[:, :], in_=neg_low[:, :], compare_op=ALU.is_ge, fill=-1.0, base=E - 1,
                             pattern=[[0, 1]], channel_multiplier=-1).then_inc(consts, 1)
            pool.wait_ge(consts, 15)
            gp.affine_select(out=neg_low[:, :], in_=neg_low[:, :], compare_op=ALU.is_ge, fill=0.0, base=2 * E - 1,
                             pattern=[[0, 1]], channel_multiplier=-1).then_inc(consts, 1)
            gp.affine_select(out=expert_f[:, :, :].rearrange("p m (a f) -> p m a f", f=F),
                             in_=expert_f[:, :, :].rearrange("p m (a f) -> p m a f", f=F),
                             compare_op=ALU.not_equal, fill=1.0, base=-LOW,
                             pattern=[[-(128 // F), MC], [-1, 128 // F], [0, F]], channel_multiplier=1).then_inc(consts, 1)
            pool.wait_ge(consts, 17)
            gp.tensor_copy(expert_of[:, :, :], expert_f[:, :, :]).then_inc(consts, 1)

            table_end = pool.snap(pool.to_reg(NE - 1))

            def gather_edges(b):
                gp.indirect_dma_start(edge_rows(b), None, x, bass.IndirectOffsetOnAxis(node_u[0:P, 0, b:b + 1], 0),
                                      bounds_check=N - 1, oob_is_err=False).then_inc(xe_in[b // K], 16)

            def edge_scalars(s):
                cols = slice(K * s, K * (s + 1))
                pool.wait_ge(e_mv_ready, K * (s + 1))
                at = 5 * s
                gp.tensor_scalar(e_sc[0:P, 0, cols], e_mv[0:P, cols, 1], EPS, None, ALU.add).then_inc(e_scalars, 1)
                pool.wait_ge(e_scalars, at + 1)
                pool.wait_ge(deg_src_ready, 2 * (s + 1))
                gp.tensor_tensor(e_sc[0:P, 1, cols], e_sc[0:P, 0, cols], deg_src[0:P, cols], ALU.mult).then_inc(e_scalars, 1)
                pool.wait_ge(e_scalars, at + 2)
                gp.tensor_tensor(e_sc[0:P, 2, cols], e_sc[0:P, 1, cols], neg_half[0:P, cols], ALU.pow).then_inc(e_scalars, 1)
                pool.wait_ge(e_scalars, at + 3)
                gp.tensor_tensor(e_sc[0:P, 3, cols], e_sc[0:P, 2, cols], e_mv[0:P, cols, 0], ALU.mult).then_inc(e_scalars, 1)
                pool.wait_ge(e_scalars, at + 4)
                gp.tensor_scalar(e_sc[0:P, 4, cols], e_sc[0:P, 3, cols], -1.0, None, ALU.mult).then_inc(e_scalars, 1)

            def clear_prior(s):
                if s >= 2:
                    pool.wait_ge(table_in, 64 * (s - 1))
                gp.memset(sums[0:P, s % 2, :, :], 0.0).then_inc(prior_clear, 1)

            def gather_prior(s):
                pool.wait_ge(prior_clear, s)
                pool.wait_ge(prior_rows, 4 * s)
                pool.wait_ge(table_in, 64 * s)
                for i in range(K):
                    gp.indirect_dma_start(sums[0:P, s % 2, i, :], None, table[0:s * SB, :],
                                          bass.IndirectOffsetOnAxis(prior_row[0:P, K * s + i:K * s + i + 1], 0),
                                          bounds_check=s * SB - 1, oob_is_err=False).then_inc(prior_in[i], 16)

            def dis_quarter(n):
                cols = slice(n * NB, (n + 1) * NB)
                gp.tensor_tensor(dis[0:P, cols], degree[0:P, cols], neg_half[0:P, :], ALU.pow).then_inc(dis_ready, 1)

            pool.wait_ge(node_ready, 3)
            for b in range(3 * K):
                gather_edges(b)
            edge_scalars(0)
            for b in range(3 * K, NB):
                gather_edges(b)
            edge_scalars(1)
            clear_prior(1)
            gp.tensor_tensor(dis_src[0:P, :], deg_src[0:P, :], neg_half[0:P, :], ALU.pow).then_inc(dis_src_ready, 1)
            dis_quarter(0)
            edge_scalars(2)
            gather_prior(1)
            clear_prior(2)
            edge_scalars(3)
            dis_quarter(1)
            gather_prior(2)
            clear_prior(3)
            dis_quarter(2)
            gather_prior(3)
            dis_quarter(3)

            def half_rstd(stats, t, done, at):
                tt = gp.tensor_tensor
                tt(t[0:P, 0, :], stats[0:P, :, 1], stats[0:P, :, 4], ALU.add).then_inc(done, 1)
                tt(t[0:P, 1, :], stats[0:P, :, 1], stats[0:P, :, 4], ALU.subtract).then_inc(done, 1)
                tt(t[0:P, 2, :], stats[0:P, :, 2], stats[0:P, :, 5], ALU.add).then_inc(done, 1)
                pool.wait_ge(done, at + 3)
                tt(t[0:P, 3, :], t[0:P, 1, :], t[0:P, 1, :], ALU.mult).then_inc(done, 1)
                tt(t[0:P, 4, :], t[0:P, 2, :], inv_128[0:P, :], ALU.mult).then_inc(done, 1)
                tt(t[0:P, 5, :], t[0:P, 0, :], half[0:P, :], ALU.mult).then_inc(done, 1)
                pool.wait_ge(done, at + 6)
                tt(t[0:P, 6, :], t[0:P, 3, :], t[0:P, 4, :], ALU.add).then_inc(done, 1)
                pool.wait_ge(done, at + 7)
                tt(t[0:P, 7, :], t[0:P, 6, :], eps4[0:P, :], ALU.add).then_inc(done, 1)
                pool.wait_ge(done, at + 8)
                tt(t[0:P, 8, :], t[0:P, 7, :], neg_half[0:P, 0:J], ALU.pow).then_inc(done, 1)

            def rows_for(k, u):
                g, _, _ = steps(k, u)
                after(pool, z_ready, J * g)
                gp.tensor_copy(row_idx[0:P, :], table_row[0:P, bass.ds(g * J, J)]).then_inc(idx_copied, 1)
                gp.memset(u_tile[0:P, :, :], 0.0).then_inc(u_zeroed, 1)
                pool.wait_ge(idx_copied, g + 1)
                pool.wait_ge(u_zeroed, g + 1)
                gp.tensor_tensor(sc1[0:P, 12, :], dis[0:P, bass.ds(g * J, J)], zero4[0:P, :], ALU.add).then_inc(ln1_done, 1)

            def fetch(k, u):
                for j in range(J):
                    gp.indirect_dma_start(u_tile[0:P, j, :], None, table,
                                          bass.IndirectOffsetOnAxis(row_idx[0:P, j:j + 1], 0),
                                          bounds_check=table_end, oob_is_err=False).then_inc(u_in, 16)

            def ln1(k, u):
                g, _, _ = steps(k, u)
                cols = bass.ds(g * J, J)
                at = LN1 * g + 1
                pool.wait_ge(st1_done, J * (g + 1))
                half_rstd(st1, sc1, ln1_done, at)
                pool.wait_ge(ln1_done, at + 9)
                gp.tensor_tensor(sc1[0:P, 9, :], sc1[0:P, 8, :], dis2x2[0:P, cols], ALU.mult).then_inc(ln1_done, 1)
                pool.wait_ge(ln1_done, at + 10)
                gp.tensor_tensor(sc1[0:P, 10, :], sc1[0:P, 9, :], sc1[0:P, 5, :], ALU.mult).then_inc(ln1_done, 1)
                pool.wait_ge(ln1_done, at + 11)
                gp.tensor_tensor(sc1[0:P, 11, :], s_node[0:P, cols], sc1[0:P, 10, :], ALU.subtract).then_inc(ln1_done, 1)

            def ln2(k, u):
                g, _, _ = steps(k, u)
                at = LN2 * g
                after(pool, xn_ready, J * g)
                pool.wait_ge(st2_done, J * (g + 1))
                half_rstd(st2, sc2, ln2_done, at)
                pool.wait_ge(ln2_done, at + 9)
                gp.tensor_tensor(sc2[0:P, 9, :], sc2[0:P, 8, :], sc2[0:P, 8, :], ALU.add).then_inc(ln2_done, 1)
                pool.wait_ge(ln2_done, at + 10)
                gp.tensor_tensor(sc2[0:P, 10, :], sc2[0:P, 9, :], sc2[0:P, 5, :], ALU.mult).then_inc(ln2_done, 1)
                pool.wait_ge(ln2_done, at + 11)
                gp.tensor_tensor(sc2[0:P, 11, :], zero4[0:P, :], sc2[0:P, 10, :], ALU.subtract).then_inc(ln2_done, 1)

            def first():
                pool.wait_ge(rows_ready, 2)
                pool.wait_ge(main_free, 1)
                rows_for(0, 0)
                pool.wait_ge(s_ready, 4)
                ln1(0, 0)
                pool.wait_ge(table_in, 64 * NS)
                fetch(0, 0)
                rows_for(0, 1)
                ln1(0, 1)
                fetch(0, 1)
                ln2(0, 0)

            def body(k, u):
                rows_for(k, u + 2)
                fetch(k, u + 2)
                ln1(k, u + 2)
                ln2(k, u + 1)

            def last(k, u):
                if u + 1 < G:
                    ln2(k, u + 1)

            pipeline(pool, first, body, last)

        @block.scalar
        def _(act):
            sc = nc.scalar

            def turn_evacuate(n, bank):
                act.wait_ge(at_turned, n + 1)
                at = at_src if n < 5 else at_dst
                cols = slice(n % 5 * GN, (n % 5 + 1) * GN)
                sc.activation(at[0:P, cols], ps[0:P, bank, 0:GN], ACT.Copy).then_inc(at_ready, 1)

            def normalise(s):
                act.wait_ge(e_scalars, 5 * (s + 1))
                for b in range(K * s, K * (s + 1)):
                    sc.activation(edge_rows(b), edge_rows(b), ACT.Identity,
                                  bias=e_sc[0:P, 4, b:b + 1], scale=e_sc[0:P, 2, b:b + 1]).then_inc(e_normed, 1)

            def high(s):
                if s >= 2:
                    act.wait_ge(e_summed, K * (s - 1))
                for b in range(K * s, K * (s + 1)):
                    act.wait_ge(e_normed, b + 1)
                    sc.activation(e_hi[0:P, s % 2, b - K * s, :], edge_rows(b), ACT.Copy).then_inc(e_split_hi, 1)

            for n in range(5):
                turn_evacuate(n, 3 + n)
            act.wait_ge(hot_ready, 3)
            sc.activation(a_dst[0:P, :, :], a_dst16[0:P, :, :], ACT.Copy).then_inc(a_dst_ready, 1)
            for n in range(5, 10):
                turn_evacuate(n, 5 + (n - 5) % 3)
            normalise(0)
            high(0)
            normalise(1)
            for i in range(K):
                act.wait_ge(e_summed, i + 1)
                sc.activation(sums[0:P, 0, i, :], ps[0:P, i, :], ACT.Copy).then_inc(sum_ready, 1)
            high(1)
            normalise(2)
            high(2)
            act.wait_ge(w_in, 80)
            for c in range(KC):
                op = sc.activation(wn[:, c, :], wn[:, c, :], ACT.Copy, accum_out=w_sum[:, c:c + 1])
            op.then_inc(wsum_ready, 1)
            act.wait_ge(wsum_ready, 3)
            for c in range(KC):
                sc.activation(wn[:, c, :], wn[:, c, :], ACT.Identity, bias=beta[:, c:c + 1]).then_inc(w_biased, 1)
            normalise(3)
            high(3)

            def wg_high(c):
                act.wait_ge(w_turned, c + 2)
                sc.activation(wg_hi[:, c, :], ps[:, W_BANK[c], :], ACT.Copy).then_inc(w_hi, 1)

            wg_high(0)
            wg_high(1)
            act.wait_ge(gate_in, 1)
            sc.activation(w1_hi[:, :, :, :], w1_n[:, :, :, :], ACT.Copy).then_inc(w_hi, 1)
            wg_high(2)
            wg_high(3)

            def scale1(k, u):
                g, slot, _ = steps(k, u)
                act.wait_ge(ln1_done, LN1 * (g + 1))
                for j in range(J):
                    after(act, z_turned, J * (g - 1) + j + 1)
                    sc.activation(z_tile[0:P, j, :], x_tile[slot][0:P, j, :], ACT.Identity,
                                  bias=sc1[0:P, 11, j:j + 1], scale=sc1[0:P, 9, j:j + 1]).then_inc(z_scaled, 1)

            def scale2(k, u):
                g, slot, _ = steps(k, u)
                act.wait_ge(ln2_done, LN2 * (g + 1))
                for j in range(J):
                    after(act, xn_turned, J * (g - 1) + j + 1)
                    sc.activation(xn_tile[0:P, j, :], x_tile[slot][0:P, j, :], ACT.Identity,
                                  bias=sc2[0:P, 11, j:j + 1], scale=sc2[0:P, 9, j:j + 1]).then_inc(xn_ready, 1)

            def z_hi(k, u, j):
                g, _, _ = steps(k, u)
                act.wait_ge(z_turned, J * g + j + 1)
                sc.activation(zT_hi[:, j, :, :].rearrange("p c q -> p (c q)"), ps[:, TR[j % 2], 0:KC * P],
                              ACT.Copy).then_inc(zT_hi_ok, 1)

            def xn_hi(k, u, j):
                g, _, _ = steps(k, u)
                act.wait_ge(xn_turned, J * g + j + 1)
                sc.activation(xT_hi[:, :, j, :], ps[:, TR[j % 2], 0:KC * P].rearrange("p (c q) -> p c q", q=P),
                              ACT.Copy).then_inc(xT_hi_ok, 1)

            def gelu(k, u, m):
                g, _, _ = steps(k, u)
                act.wait_ge(ffn1_done, 5 * g + 2 + m)
                after(act, h_lo_ok, 6 * (g - 1) + 3 + m)
                sc.activation(hid[:, m, :], ps[:, BANK[1 + m], 0:GN], ACT.Gelu, bias=b1[:, m:m + 1]).then_inc(act_done, 1)

            def h_high(k, u, m):
                g, _, _ = steps(k, u)
                act.wait_ge(weighed, J * g + m + 1)
                sc.activation(h_hi[:, m, :], hid[:, m, :], ACT.Copy).then_inc(h_hi_ok, 1)

            def tanh(k, u, n):
                g, _, _ = steps(k, u)
                act.wait_ge(gated, GATE * g + (7, 14)[n])
                sc.activation(gt[0:P, (1, 6)[n], :, :], gt[0:P, (0, 5)[n], :, :], ACT.Tanh, scale=0.5).then_inc(tanh_done, 1)

            def first():
                scale1(0, 0)
                for j in range(J):
                    z_hi(0, 0, j)
                scale1(0, 1)
                for j in range(J):
                    z_hi(0, 1, j)
                scale2(0, 0)
                act.wait_ge(halved, 1)
                sc.activation(w2_hi[:, :, :], w2_n[:, :, :], ACT.Copy).then_inc(w_hi, 1)
                for j in range(J):
                    xn_hi(0, 0, j)
                act.wait_ge(b2_ready, 2)
                sc.activation(b2_hi[0:SH0, :], b2_n[0:SH0, :], ACT.Copy).then_inc(b2_high, 1)

            def body(k, u, more=2):
                g, _, _ = steps(k, u)
                act.wait_ge(ffn1_done, 5 * g + 1)
                after(act, lg_turned, g)
                sc.activation(logits_f[0:E, :], ps[0:E, BANK[0], 0:GN], ACT.Copy).then_inc(act_done, 1)
                after(act, h_lo_ok, 6 * (g - 1) + 1)
                sc.activation(hid[SH0:128, MC, :], ps[SH0:128, BANK[0], 0:GN], ACT.Gelu,
                              bias=b1[SH0:128, MC:MC + 1]).then_inc(act_done, 1)
                act.wait_ge(act_done, 6 * g + 2)
                sc.activation(h_lo[SH0:128, MC, :], hid[SH0:128, MC, :], ACT.Copy)
                sc.activation(h_hi[SH0:128, MC, :], hid[SH0:128, MC, :], ACT.Copy).then_inc(h_hi_ok, 1)
                gelu(k, u, 0)
                tanh(k, u, 0)
                gelu(k, u, 1)
                tanh(k, u, 1)
                if more == 2:
                    scale1(k, u + 2)
                gelu(k, u, 2)
                gelu(k, u, 3)
                act.wait_ge(comb_turned, g + 1)
                sc.activation(h_hi[0:CW, MC, :], ps[0:CW, SMALL, 0:GN], ACT.Copy).then_inc(h_hi_ok, 1)
                h_high(k, u, 0)
                h_high(k, u, 1)
                if more == 2:
                    z_hi(k, u + 2, 0)
                h_high(k, u, 2)
                h_high(k, u, 3)
                if more == 2:
                    z_hi(k, u + 2, 1)
                if more == 2:
                    z_hi(k, u + 2, 2)
                    z_hi(k, u + 2, 3)
                if more:
                    scale2(k, u + 1)
                    for j in range(J):
                        xn_hi(k, u + 1, j)

            pipeline(act, first, body, lambda k, u: body(k, u, more=G - 1 - u))

        @block.vector
        def _(dve):
            v = nc.vector

            v.memset(b1[0:SH0, MC:MC + 1], 0.0).then_inc(b1_clear, 1)
            dve.wait_ge(consts, 5)
            v.tensor_copy(row_iota_f[:, :], row_iota[:, :]).then_inc(copied, 1)
            dve.wait_ge(consts, 12)
            v.tensor_copy(ident16[:, :], ident[:, :]).then_inc(copied, 1)
            dve.wait_ge(idx_in, 32)
            v.tensor_copy(idx_rows_f[:, :, :], idx_rows[:, :, :]).then_inc(node_ready, 1)
            dve.wait_ge(idx_turned, 1)
            nodes = ps[0:P, 2, 0:2 * NB].rearrange("p (a b) -> p a b", a=2)
            v.tensor_copy(node_u[0:P, :, :], nodes).then_inc(node_ready, 1)
            v.tensor_copy(node_f[0:P, :, :], nodes).then_inc(node_ready, 1)
            dve.wait_ge(node_ready, 3)
            v.tensor_scalar(quot_r[0:P], node_f[0:P], -(T - 1) / 2.0, 1.0 / T, ALU.add, ALU.mult).then_inc(node_ready, 1)
            dve.wait_ge(node_ready, 4)
            v.tensor_scalar(quot[0:P], quot_r[0:P], ROUND, ROUND, ALU.add, ALU.subtract).then_inc(node_ready, 1)
            dve.wait_ge(node_ready, 5)
            v.scalar_tensor_tensor(out=rest[0:P], in0=quot[0:P], scalar=-float(T), in1=node_f[0:P],
                                   op0=ALU.mult, op1=ALU.add).then_inc(node_ready, 1)
            dve.wait_ge(copied, 1)

            def hot(out_ap, value, a, width):
                return v.tensor_tensor(out_ap, value[0:P, a, :].unsqueeze(2).to_broadcast((P, NB, width)),
                                       row_iota_f[0:P, 0:width].unsqueeze(1).to_broadcast((P, NB, width)), ALU.is_equal)

            def spread_over(value, s):
                return value[0:P, K * s:K * (s + 1)].unsqueeze(2).to_broadcast((P, K, T))

            hot(a_src[0:P], quot, 0, P).then_inc(hot_ready, 1)
            dve.wait_ge(node_ready, 6)
            hot(b_src[0:P], rest, 0, T).then_inc(hot_ready, 1)
            hot(a_dst16[0:P], quot, 1, P).then_inc(hot_ready, 1)
            dve.wait_ge(deg_counted, 1)
            v.tensor_scalar(deg[0:P, :], ps[0:P, 2, DEG_COL:DEG_COL + T], 1.0, None, ALU.add).then_inc(deg_ready, 1)
            v.tensor_scalar(degree[0:P, :], ps[0:P, 2, DEG_COL:DEG_COL + T], 1.0, None, ALU.add).then_inc(deg_ready, 1)
            hot(b_dst[0:P], rest, 1, T).then_inc(hot_ready, 1)

            def edge_same(s):
                if s >= 2:
                    dve.wait_ge(e_summed, K * (s - 1))
                for i in range(K):
                    b, first, w = K * s + i, same_cols(i, i).start, (K - i) * P
                    v.scalar_tensor_tensor(out=same[0:P, s % 2, first:first + w], in0=dst_bc[0:P, b * P:b * P + w],
                                           scalar=node_f[0:P, 1, b:b + 1], in1=not_before[0:P, 0:w], op0=ALU.is_equal,
                                           op1=ALU.mult, accum_out=matches[0:P, b:b + 1]).then_inc(same_ready, 1)

            def edge_last(s):
                cols = slice(K * s, K * (s + 1))
                dve.wait_ge(same_ready, K * (s + 1))
                v.scalar_tensor_tensor(out=last_row[0:P, cols], in0=matches[0:P, cols], scalar=1.0, in1=edge_row[0:P, cols],
                                       op0=ALU.is_equal, op1=ALU.mult).then_inc(last_ready, 1)
                dve.wait_ge(last_ready, 2 * s + 1)
                v.tensor_tensor(b_last[0:P, cols, :], b_dst[0:P, cols, :], spread_over(last_row, s), ALU.mult).then_inc(last_ready, 1)

            def edge_newest(s):
                here = ps[0:P, 5, s * T:(s + 1) * T]
                dve.wait_ge(last_spread, s + 1)
                if s == 0:
                    v.tensor_copy(newest[0:P, 0, :], here).then_inc(newest_ready, 1)
                    return
                dve.wait_ge(newest_ready, 2 * s - 1)
                v.scalar_tensor_tensor(out=kept[0:P, s, :], in0=here, scalar=0.0, in1=newest[0:P, s - 1, :],
                                       op0=ALU.is_equal, op1=ALU.mult).then_inc(newest_ready, 1)
                dve.wait_ge(newest_ready, 2 * s)
                v.tensor_tensor(newest[0:P, s, :], here, kept[0:P, s, :], ALU.add).then_inc(newest_ready, 1)

            def prior_pick(s):
                cols = slice(K * s, K * (s + 1))
                at = 4 * (s - 1)
                dve.wait_ge(prior_looked, s)
                v.tensor_tensor(b_prior[0:P, cols, :], ps[0:P, 6 + (s - 1) % 2, 0:K * T].rearrange("p (b t) -> p b t", t=T),
                                b_dst[0:P, cols, :], ALU.mult).then_inc(prior_rows, 1)
                dve.wait_ge(prior_rows, at + 1)
                v.tensor_reduce(prior_f[0:P, 0, cols], b_prior[0:P, cols, :], AX_X, ALU.add).then_inc(prior_rows, 1)
                dve.wait_ge(prior_rows, at + 2)
                v.tensor_scalar(prior_f[0:P, 1, cols], prior_f[0:P, 0, cols], 0.0, NOWHERE, ALU.is_equal, ALU.mult).then_inc(prior_rows, 1)
                dve.wait_ge(prior_rows, at + 3)
                v.scalar_tensor_tensor(out=prior_row[0:P, cols], in0=prior_f[0:P, 0, cols], scalar=-1.0,
                                       in1=prior_f[0:P, 1, cols], op0=ALU.add, op1=ALU.add).then_inc(prior_rows, 1)

            def deg_pick(s):
                cols = slice(K * s, K * (s + 1))
                dve.wait_ge(deg_looked, s + 1)
                v.tensor_tensor(picked[0:P, cols, :], ps[0:P, s, 0:K * T].rearrange("p (b t) -> p b t", t=T),
                                b_src[0:P, cols, :], ALU.mult).then_inc(deg_src_ready, 1)
                dve.wait_ge(deg_src_ready, 2 * s + 1)
                v.tensor_reduce(deg_src[0:P, cols], picked[0:P, cols, :], AX_X, ALU.add).then_inc(deg_src_ready, 1)

            def edge_stats(s):
                dve.wait_ge(xe_in[s], 16 * K)
                for b in range(K * s, K * (s + 1)):
                    v.bn_stats(e_stats[0:P, b, :], edge_rows(b)).then_inc(e_stats_ready, 1)
                for b in range(K * s, K * (s + 1)):
                    dve.wait_ge(e_stats_ready, b + 1)
                    v.bn_aggr(e_mv[0:P, b, :], e_stats[0:P, b, :]).then_inc(e_mv_ready, 1)

            def edge_lo(s):
                for b in range(K * s, K * (s + 1)):
                    dve.wait_ge(e_split_hi, b + 1)
                    v.tensor_tensor(low_edge_rows(b), edge_rows(b), f32(e_hi[0:P, s % 2, b - K * s, :]),
                                    ALU.subtract).then_inc(e_split_lo, 1)

            def edge_add(s):
                for i in range(K):
                    dve.wait_ge(prior_in[i], 16 * s)
                    dve.wait_ge(e_summed, K * s + i + 1)
                    v.tensor_tensor(sums[0:P, s % 2, i, :], ps[0:P, i, :], sums[0:P, s % 2, i, :], ALU.add).then_inc(sum_ready, 1)

            dve.wait_ge(bc_in, 16)
            dve.wait_ge(consts, 13)
            edge_same(0)
            edge_last(0)
            edge_stats(0)
            for s in range(NS):
                deg_pick(s)
            dve.wait_ge(at_ready, 6)
            dve.wait_ge(a_dst_ready, 1)
            dve.wait_ge(deg_src_ready, 2 * NS)
            dve.wait_ge(consts, 18)
            dve.wait_ge(at_turned, 10)
            v.memset(w1_n[:, :, MC, E:SH0], 0.0).then_inc(w1_clear, 1)
            edge_newest(0)
            edge_stats(1)
            edge_lo(0)
            edge_same(1)
            edge_last(1)
            prior_pick(1)
            edge_stats(2)
            edge_lo(1)
            edge_newest(1)
            edge_stats(3)
            edge_add(1)
            prior_pick(2)
            edge_same(2)
            edge_last(2)
            edge_lo(2)
            dve.wait_ge(wsum_ready, 1)
            v.tensor_tensor(w_sum[:, :], gb[:, :], w_sum[:, :], ALU.subtract).then_inc(wsum_ready, 1)
            dve.wait_ge(wsum_ready, 2)
            v.tensor_scalar(beta[:, :], w_sum[:, :], 1.0 / D, None, ALU.mult).then_inc(wsum_ready, 1)
            edge_newest(2)
            dve.wait_ge(dis_src_ready, 1)
            v.tensor_tensor(b_norm[0:P], b_dst[0:P], dis_src[0:P, :].unsqueeze(2).to_broadcast((P, NB, T)), ALU.mult).then_inc(b_norm_ready, 1)
            edge_add(2)
            prior_pick(3)
            edge_same(3)
            edge_last(3)
            edge_newest(3)
            dve.wait_ge(prior_looked, NS - 1)
            dve.wait_ge(last_spread, NS)
            dve.wait_ge(s_summed, 1)
            dve.wait_ge(newest_ready, 2 * NS - 1)
            v.tensor_scalar(no_edge[0:P, :], newest[0:P, NS - 1, :], 0.0, NOWHERE, ALU.is_equal, ALU.mult).then_inc(rows_ready, 1)
            edge_lo(3)
            dve.wait_ge(rows_ready, 1)
            v.scalar_tensor_tensor(out=table_row[0:P, :], in0=newest[0:P, NS - 1, :], scalar=-1.0, in1=no_edge[0:P, :],
                                   op0=ALU.add, op1=ALU.add).then_inc(rows_ready, 1)
            dve.wait_ge(prior_rows, 4 * (NS - 1))
            v.memset(lg[0:P, :, E:E + TOP], LOWEST).then_inc(main_free, 1)

            def wg_low(c):
                dve.wait_ge(w_hi, c + 1 if c < 2 else c + 2)
                v.tensor_tensor(wg_lo[:, c, :], ps[:, W_BANK[c], :], f32(wg_hi[:, c, :]), ALU.subtract).then_inc(w_lo, 1)

            dve.wait_ge(w_turned, 1)
            dve.wait_ge(w1_in, 16 * 2 * KC)
            v.tensor_copy(w1_n[:, :, MC, 0:E], ps[:, 5, GATE_COL:GATE_COL + KC * E].rearrange("p (c e) -> p c e", e=E)).then_inc(gate_in, 1)
            wg_low(0)
            wg_low(1)
            dve.wait_ge(x_loaded[0], 32)
            for j in range(J):
                v.bn_stats(st1[0:P, j, :], x_tile[0][0:P, j, :]).then_inc(st1_done, 1)
            edge_add(3)
            dve.wait_ge(dis_ready, T // NB)
            v.tensor_tensor(dis2[0:P, :], dis[0:P, :], dis[0:P, :], ALU.mult).then_inc(s_ready, 1)
            dve.wait_ge(s_ready, 1)
            v.tensor_tensor(dis2x2[0:P, :], dis2[0:P, :], dis2[0:P, :], ALU.add).then_inc(s_ready, 1)
            v.tensor_tensor(kept[0:P, 0, :], ps[0:P, 5, S_COL:S_COL + T], dis[0:P, :], ALU.mult).then_inc(s_ready, 1)
            dve.wait_ge(s_ready, 3)
            v.tensor_tensor(s_node[0:P, :], kept[0:P, 0, :], dis2[0:P, :], ALU.add).then_inc(s_ready, 1)
            dve.wait_ge(w_hi, 3)
            v.tensor_tensor(w1_lo[:, :, :, :], w1_n[:, :, :, :], f32(w1_hi[:, :, :, :]), ALU.subtract).then_inc(w_lo, 1)
            wg_low(2)
            wg_low(3)
            dve.wait_ge(table_in, 64 * NS)
            v.memset(f32(h_hi[:, MC, :]), 0.0).then_inc(cleared, 1)
            v.memset(comb[:, :, :], 0.0).then_inc(cleared, 1)
            v.memset(b2_n[0:SH0, :], 0.0).then_inc(b2_clear, 1)
            dve.wait_ge(cleared, 2)

            def stats1(k, u):
                g, slot, rnd = steps(k, u)
                dve.wait_ge(x_loaded[slot], 32 * (rnd + 1))
                after(dve, ln1_done, LN1 * g)
                for j in range(J):
                    v.bn_stats(st1[0:P, j, :], x_tile[slot][0:P, j, :]).then_inc(st1_done, 1)

            def add_edges(k, u):
                g, _, _ = steps(k, u)
                dve.wait_ge(u_in, 64 * (g + 1))
                for j in range(J):
                    dve.wait_ge(z_scaled, J * g + j + 1)
                    v.scalar_tensor_tensor(out=z_tile[0:P, j, :], in0=u_tile[0:P, j, :], scalar=sc1[0:P, 12, j:j + 1],
                                           in1=z_tile[0:P, j, :], op0=ALU.mult, op1=ALU.add).then_inc(z_ready, 1)

            def z_low(k, u, j):
                g, _, _ = steps(k, u)
                dve.wait_ge(zT_hi_ok, J * g + j + 1)
                hi = zT_hi[:, j, :, :].rearrange("p c q -> p (c q)")
                v.tensor_tensor(zT_lo[:, j, :, :].rearrange("p c q -> p (c q)"), ps[:, TR[j % 2], 0:KC * P], f32(hi),
                                ALU.subtract).then_inc(zT_lo_ok, 1)

            def xn_low(k, u, j):
                g, _, _ = steps(k, u)
                dve.wait_ge(xT_hi_ok, J * g + j + 1)
                v.tensor_tensor(xT_lo[:, :, j, :], ps[:, TR[j % 2], 0:KC * P].rearrange("p (c q) -> p c q", q=P),
                                f32(xT_hi[:, :, j, :]), ALU.subtract).then_inc(xT_lo_ok, 1)

            def residual1(k, u, j):
                g, slot, _ = steps(k, u)
                x_j = x_tile[slot][0:P, j, :]
                dve.wait_ge(gnn_done, J * g + j + 1)
                v.scalar_tensor_tensor(out=x_j, in0=ps[0:P, BANK[5 + j], :], scalar=0.0, in1=x_j,
                                       op0=ALU.max, op1=ALU.add).then_inc(x1_done, 1)
                if j == 0:
                    after(dve, ln2_done, LN2 * g)
                dve.wait_ge(x1_done, J * g + j + 1)
                v.bn_stats(st2[0:P, j, :], x_j).then_inc(st2_done, 1)

            def residual2(k, u, j):
                g, slot, _ = steps(k, u)
                x_j = x_tile[slot][0:P, j, :]
                dve.wait_ge(ffn2_done, J * g + j + 1)
                v.tensor_tensor(x_j, ps[0:P, BANK[9 + j], :], x_j, ALU.add).then_inc(out_ready, 1)

            def weigh(k, u, m):
                g, _, _ = steps(k, u)
                dve.wait_ge(act_done, 6 * g + 3 + m)
                dve.wait_ge(spread, J * g + m + 1)
                v.tensor_tensor(hid[:, m, :], ps[:, SPREAD[m % 2], 0:GN], hid[:, m, :], ALU.mult).then_inc(weighed, 1)

            def h_low(k, u, m):
                g, _, _ = steps(k, u)
                dve.wait_ge(h_hi_ok, 6 * g + 3 + m)
                v.tensor_tensor(h_lo[:, m, :], hid[:, m, :], f32(h_hi[:, m, :]), ALU.subtract).then_inc(h_lo_ok, 1)

            def wide(col):
                return col.unsqueeze(2).to_broadcast((P, J, E))

            def gate_probs(k, u):
                g, _, _ = steps(k, u)
                at = GATE * g
                after(dve, gated, GATE * g)
                dve.wait_ge(lg_turned, g + 1)
                v.tensor_copy(lg[0:P, :, 0:E], ps[0:P, SMALL, 0:J * E].rearrange("p (j e) -> p j e", e=E)).then_inc(gated, 1)
                dve.wait_ge(gated, at + 1)
                v.tensor_reduce(gs[0:P, 4, :], lg[0:P, :, 0:E], AX_X, ALU.max).then_inc(gated, 1)
                for j in range(J):
                    v.max(top8[0:P, j, :], lg[0:P, j, 0:E]).then_inc(gated, 1)
                dve.wait_ge(gated, at + 6)
                v.tensor_tensor(gt[0:P, 0], lg[0:P, :, 0:E], wide(gs[0:P, 4, :]), ALU.subtract).then_inc(gated, 1)
                v.memset(top8[0:P, :, TOP:8], LOWEST).then_inc(gated, 1)

            def gate_combine(k, u):
                g, _, _ = steps(k, u)
                at = GATE * g
                dve.wait_ge(tanh_done, 2 * g + 1)
                v.tensor_scalar(gt[0:P, 2], gt[0:P, 1], -1.0, 1.0, ALU.mult, ALU.add).then_inc(gated, 1)
                dve.wait_ge(gated, at + 9)
                v.reciprocal(gt[0:P, 3], gt[0:P, 2]).then_inc(gated, 1)
                dve.wait_ge(gated, at + 10)
                v.scalar_tensor_tensor(out=gt[0:P, 4], in0=gt[0:P, 1], scalar=1.0, in1=gt[0:P, 3],
                                       op0=ALU.add, op1=ALU.mult).then_inc(gated, 1)
                dve.wait_ge(gated, at + 11)
                v.tensor_reduce(gs[0:P, 0, :], gt[0:P, 4], AX_X, ALU.add).then_inc(gated, 1)
                dve.wait_ge(gated, at + 12)
                v.reciprocal(gs[0:P, 1, :], gs[0:P, 0, :]).then_inc(gated, 1)
                dve.wait_ge(gated, at + 13)
                v.scalar_tensor_tensor(out=gt[0:P, 5], in0=gt[0:P, 4], scalar=-1.0, in1=wide(gs[0:P, 1, :]),
                                       op0=ALU.add, op1=ALU.mult).then_inc(gated, 1)
                for j in range(J):
                    v.match_replace(left[0:P, j, :], top8[0:P, j, :], lg[0:P, j, :], -LOWEST).then_inc(gated, 1)
                dve.wait_ge(tanh_done, 2 * g + 2)
                v.tensor_scalar(gt[0:P, 7], gt[0:P, 6], -1.0, 1.0, ALU.mult, ALU.add).then_inc(gated, 1)
                dve.wait_ge(gated, at + 19)
                v.reciprocal(gt[0:P, 8], gt[0:P, 7]).then_inc(gated, 1)
                dve.wait_ge(gated, at + 20)
                v.scalar_tensor_tensor(out=gt[0:P, 9], in0=gt[0:P, 6], scalar=1.0, in1=gt[0:P, 8],
                                       op0=ALU.add, op1=ALU.mult).then_inc(gated, 1)
                dve.wait_ge(gated, at + 21)
                v.scalar_tensor_tensor(out=gt[0:P, 10], in0=left[0:P, :, 0:E], scalar=-LOWEST, in1=gt[0:P, 9],
                                       op0=ALU.is_equal, op1=ALU.mult).then_inc(gated, 1)
                dve.wait_ge(gated, at + 22)
                v.tensor_reduce(gs[0:P, 2, :], gt[0:P, 10], AX_X, ALU.add).then_inc(gated, 1)
                dve.wait_ge(gated, at + 23)
                v.reciprocal(gs[0:P, 3, :], gs[0:P, 2, :]).then_inc(gated, 1)
                dve.wait_ge(gated, at + 24)
                v.tensor_tensor(comb[0:P, :, 0:CW].rearrange("p j (r e) -> p j r e", e=E),
                                gt[0:P, 10].unsqueeze(2).to_broadcast((P, J, 3, E)),
                                gs[0:P, 3, :].unsqueeze(2).unsqueeze(3).to_broadcast((P, J, 3, E)), ALU.mult).then_inc(gated, 1)

            def first():
                stats1(0, 1)
                add_edges(0, 0)
                for j in range(J):
                    z_low(0, 0, j)
                residual1(0, 0, 0)
                residual1(0, 0, 1)
                dve.wait_ge(w2_in, 48)
                v.tensor_scalar(w2_n[:, MC, :], w2_n[:, MC, :], 1.0 / SH, None, ALU.mult).then_inc(halved, 1)
                add_edges(0, 1)
                z_low(0, 1, 0)
                z_low(0, 1, 1)
                residual1(0, 0, 2)
                residual1(0, 0, 3)
                z_low(0, 1, 2)
                z_low(0, 1, 3)
                residual1(0, 1, 0)
                residual1(0, 1, 1)
                for j in range(J):
                    xn_low(0, 0, j)
                dve.wait_ge(w_hi, KC + 2)
                v.tensor_tensor(w2_lo[:, :, :], w2_n[:, :, :], f32(w2_hi[:, :, :]), ALU.subtract).then_inc(w_lo, 1)
                dve.wait_ge(b2_in, 64)
                for j in range(SH):
                    if j:
                        dve.wait_ge(b2_ready, j)
                    v.scalar_tensor_tensor(out=b2_n[0:CW, :], in0=sb2_n[0:CW, j, :], scalar=1.0 / SH, in1=b2_n[0:CW, :],
                                           op0=ALU.mult, op1=ALU.add).then_inc(b2_ready, 1)
                dve.wait_ge(b2_high, 1)
                dve.wait_ge(w_lo, KC + 2)
                v.scalar_tensor_tensor(out=w2_lo[0:SH0, MC, :], in0=f32(b2_hi[0:SH0, :]), scalar=neg_low[0:SH0, 0:1],
                                       in1=b2_n[0:SH0, :], op0=ALU.mult, op1=ALU.add).then_inc(b2_placed, 1)

            def body(k, u, more=2):
                g, _, _ = steps(k, u)
                if more == 2:
                    stats1(k, u + 2)
                gate_probs(k, u)
                dve.wait_ge(h_hi_ok, 6 * g + 1)
                v.tensor_tensor(h_lo[0:SF, MC, :], hid[SH0:128, MC, :], f32(h_hi[SH0:128, MC, :]),
                                ALU.subtract).then_inc(h_lo_ok, 1)
                gate_combine(k, u)
                if more == 2:
                    add_edges(k, u + 2)
                dve.wait_ge(h_hi_ok, 6 * g + 2)
                v.tensor_tensor(h_hi[LOW:CW, MC, :], ps[LOW:CW, SMALL, 0:GN], f32(h_hi[LOW:CW, MC, :]),
                                ALU.subtract).then_inc(h_lo_ok, 1)
                if more and u:
                    residual1(k, u + 1, 0)
                weigh(k, u, 0)
                weigh(k, u, 1)
                if more and u:
                    residual1(k, u + 1, 1)
                if more == 2:
                    z_low(k, u + 2, 0)
                h_low(k, u, 0)
                h_low(k, u, 1)
                weigh(k, u, 2)
                weigh(k, u, 3)
                if more:
                    residual1(k, u + 1, 2)
                if more == 2:
                    z_low(k, u + 2, 1)
                h_low(k, u, 2)
                h_low(k, u, 3)
                if more:
                    residual1(k, u + 1, 3)
                if more == 2:
                    z_low(k, u + 2, 2)
                residual2(k, u, 0)
                if more == 2:
                    z_low(k, u + 2, 3)
                residual2(k, u, 1)
                if more:
                    xn_low(k, u + 1, 0)
                    xn_low(k, u + 1, 1)
                residual2(k, u, 2)
                if more:
                    xn_low(k, u + 1, 2)
                    xn_low(k, u + 1, 3)
                residual2(k, u, 3)

            pipeline(dve, first, body, lambda k, u: body(k, u, more=G - 1 - u))

        @block.tensor
        def _(pe):
            t = nc.tensor
            pe.wait_ge(node_ready, 1)
            pe.wait_ge(consts, 12)
            for a in range(2):
                op = t.transpose(ps[0:P, 2, a * NB:(a + 1) * NB], idx_rows_f[:, a, :], ident[0:NB, 0:NB])
            op.then_inc(idx_turned, 1)

            def turn_at(n, source, bank):
                for i in range(4):
                    op = t.matmul(ps[0:P, bank, i * P:(i + 1) * P], source[0:P, n % 5 * 4 + i, :], ident16[0:P, 0:P],
                                  start=True, stop=True)
                op.then_inc(at_turned, 1)

            pe.wait_ge(hot_ready, 1)
            pe.wait_ge(copied, 2)
            for n in range(5):
                turn_at(n, a_src, 3 + n)
            pe.wait_ge(hot_ready, 2)
            for b in range(NB):
                op = t.matmul(ps[0:P, 2, DEG_COL:DEG_COL + T], a_src[0:P, b, :], b_src[0:P, b, :], start=b == 0, stop=b == NB - 1)
            op.then_inc(deg_counted, 1)
            pe.wait_ge(deg_ready, 2)
            for s in range(NS):
                if s == 3:
                    pe.wait_ge(at_ready, 1)
                for i in range(K):
                    b = K * s + i
                    pe.wait_ge(at_ready, b // 4 + 1)
                    op = t.matmul(ps[0:P, s, i * T:(i + 1) * T], at_src[0:P, b * P:(b + 1) * P], deg[0:P, :], start=True, stop=True)
                op.then_inc(deg_looked, 1)
            pe.wait_ge(hot_ready, 3)
            for n in range(5, 10):
                pe.wait_ge(at_ready, 5 if n < 8 else n - 2)
                turn_at(n, a_dst16, 5 + (n - 5) % 3)

            def spread_last(s):
                if s == 0:
                    pe.wait_ge(at_ready, 9)
                    pe.wait_ge(a_dst_ready, 1)
                pe.wait_ge(last_ready, 2 * s + 2)
                for i in range(K):
                    b = K * s + i
                    op = t.matmul(ps[0:P, 5, s * T:(s + 1) * T], a_dst[0:P, b, :], b_last[0:P, b, :], start=i == 0, stop=i == K - 1)
                op.then_inc(last_spread, 1)

            def look_prior(s):
                pe.wait_ge(newest_ready, 2 * s - 1)
                if s == 1:
                    pe.wait_ge(at_ready, 10)
                if s == 3:
                    pe.wait_ge(prior_rows, 1)
                for i in range(K):
                    b = K * s + i
                    op = t.matmul(ps[0:P, 6 + (s - 1) % 2, i * T:(i + 1) * T], at_dst[0:P, b * P:(b + 1) * P],
                                  newest[0:P, s - 1, :], start=True, stop=True)
                op.then_inc(prior_looked, 1)

            def sum_edges(s):
                for i in range(K):
                    pe.wait_ge(same_ready, K * s + i + 1)
                    pe.wait_ge(e_split_lo, K * s + i + 1)
                    if s:
                        pe.wait_ge(sum_ready, K * (s - 1) + i + 1)
                    elif i < NS:
                        pe.wait_ge(deg_src_ready, 2 * i + 1)
                    for i2 in range(i + 1):
                        for low in range(2):
                            rhs = low_edge_rows(K * s + i2) if low else e_hi[0:P, s % 2, i2, :]
                            op = t.matmul(ps[0:P, i, :], same[0:P, s % 2, same_cols(i2, i)], rhs,
                                          start=i2 == 0 and not low, stop=i2 == i and low == 1)
                    op.then_inc(e_summed, 1)

            def turn_w(c):
                for o in range(KC):
                    op = t.transpose(ps[:, W_BANK[c], o * 128:(o + 1) * 128], wn[:, o, c * 128:(c + 1) * 128], ident[:, :])
                op.then_inc(w_turned, 1)

            spread_last(0)
            look_prior(1)
            sum_edges(0)
            spread_last(1)
            sum_edges(1)
            look_prior(2)
            spread_last(2)
            sum_edges(2)
            look_prior(3)
            pe.wait_ge(b_norm_ready, 1)
            for b in range(NB):
                op = t.matmul(ps[0:P, 5, S_COL:S_COL + T], a_dst[0:P, b, :], b_norm[0:P, b, :], start=b == 0, stop=b == NB - 1)
            op.then_inc(s_summed, 1)
            pe.wait_ge(w_biased, KC)
            pe.wait_ge(newest_ready, 5)
            for c in range(KC):
                op = t.transpose(ps[:, 5, GATE_COL + c * E:GATE_COL + (c + 1) * E], gate_n[:, c * 128:(c + 1) * 128], ident[0:E, 0:E])
            op.then_inc(w_turned, 1)
            spread_last(3)
            pe.wait_ge(prior_rows, 4 * (NS - 2) + 1)
            turn_w(0)
            turn_w(1)
            sum_edges(3)
            for c in (2, 3):
                pe.wait_ge(w_lo, c - 1)
                turn_w(c)

            def turn_z(k, u, j):
                g, _, _ = steps(k, u)
                pe.wait_ge(z_ready, J * g + j + 1)
                if j >= 2:
                    pe.wait_ge(zT_lo_ok, J * g + j - 1)
                else:
                    after(pe, xT_lo_ok, J * (g - 2) + j + 3)
                for c in range(KC):
                    op = t.transpose(ps[:, TR[j % 2], c * P:(c + 1) * P], z_tile[0:P, j, c * 128:(c + 1) * 128],
                                     ident[0:P, 0:P])
                op.then_inc(z_turned, 1)

            def turn_xn(k, u, j, more):
                g, _, _ = steps(k, u)
                pe.wait_ge(xn_ready, J * g + j + 1)
                if j >= 2:
                    pe.wait_ge(xT_lo_ok, J * g + j - 1)
                elif more:
                    pe.wait_ge(zT_lo_ok, J * (g + 1) + j + 3)
                for c in range(KC):
                    op = t.transpose(ps[:, TR[j % 2], c * P:(c + 1) * P], xn_tile[0:P, j, c * 128:(c + 1) * 128],
                                     ident[0:P, 0:P])
                op.then_inc(xn_turned, 1)

            def gnn(k, u, j, steady=True):
                g, _, _ = steps(k, u)
                pe.wait_ge(zT_lo_ok, J * g + j + 1)
                if steady:
                    if j < 3:
                        pe.wait_ge(act_done, 6 * (g - 1) + 4 + j)
                    else:
                        pe.wait_ge(x1_done, J * g + 1)
                elif u == 1:
                    pe.wait_ge(x1_done, J)
                elif j == 3:
                    pe.wait_ge(x1_done, 1)
                n = 0
                for lhs, rhs in passes(zT_hi, zT_lo, wg_hi, wg_lo):
                    for c in range(KC):
                        op = t.matmul(ps[0:P, BANK[5 + j], :], lhs[:, j, c, :], rhs[:, c, :], start=n == 0, stop=n == 3 * KC - 1)
                        n += 1
                op.then_inc(gnn_done, 1)

            def turn_logits():
                for j in range(J):
                    op = t.transpose(ps[0:P, SMALL, j * E:(j + 1) * E], logits_f[0:E, j * P:(j + 1) * P], ident[0:E, 0:E])
                op.then_inc(lg_turned, 1)

            def ffn1(k, u, m):
                g, _, _ = steps(k, u)
                pos = (m + 1) % (MC + 1)
                if pos == 0:
                    pe.wait_ge(xT_lo_ok, J * (g + 1))
                    after(pe, out_ready, J * (g - 1) + 1)
                    pe.wait_ge(x1_done, J * (g + 1) + (0 if u else 2))
                elif pos == 1:
                    after(pe, out_ready, J * (g - 1) + 4)
                elif pos >= 3:
                    pe.wait_ge(act_done, 6 * g + pos - 1)
                if m == 1:
                    pe.wait_ge(act_done, 6 * g + 1)
                    after(pe, h_lo_ok, 6 * (g - 1) + 2)
                n = 0
                for lhs, rhs in ((w1_hi, xT_hi), (w1_lo, xT_hi), (w1_hi, xT_lo)):
                    for c in range(KC):
                        op = t.matmul(ps[:, BANK[pos], 0:GN], lhs[:, c, m, :], rhs[:, c, :, :].rearrange("p j q -> p (j q)"),
                                      start=n == 0, stop=n == 3 * KC - 1)
                        if m == 1 and n == 0:
                            turn_logits()
                        n += 1
                op.then_inc(ffn1_done, 1)

            def ffn2_start(k, u, j, more):
                g, _, _ = steps(k, u)
                if more and j < 3:
                    pe.wait_ge(x1_done, J * (g + 1) + j + 2)
                if j == 3:
                    pe.wait_ge(out_ready, J * g + 2)
                if u == 0 and j == 0:
                    pe.wait_ge(b2_placed, 1)
                for n, (lhs, rhs) in enumerate(((h_hi, w2_lo), (h_lo, w2_hi))):
                    t.matmul(ps[0:P, BANK[9 + j], :], lhs[:, MC, j * P:(j + 1) * P], rhs[:, MC, :], start=n == 0, stop=False)

            def ffn2_rest(k, u, j):
                g, _, _ = steps(k, u)
                for m in range(MC):
                    if j == 0:
                        pe.wait_ge(h_lo_ok, 6 * g + 3 + m)
                    for n, (lhs, rhs) in enumerate(passes(h_hi, h_lo, w2_hi, w2_lo)):
                        op = t.matmul(ps[0:P, BANK[9 + j], :], lhs[:, m, j * P:(j + 1) * P], rhs[:, m, :],
                                      start=False, stop=m == MC - 1 and n == 2)
                op.then_inc(ffn2_done, 1)

            def ffn2(k, u, j, more):
                ffn2_start(k, u, j, more)
                ffn2_rest(k, u, j)

            def turn_comb(k, u):
                g, _, _ = steps(k, u)
                pe.wait_ge(gated, GATE * (g + 1))
                for j in range(J):
                    op = t.transpose(ps[:, SMALL, j * P:(j + 1) * P], comb[0:P, j, :], ident[0:P, 0:P])
                op.then_inc(comb_turned, 1)

            def spread_comb(k, u, m):
                g, _, _ = steps(k, u)
                if m == 0:
                    pe.wait_ge(h_lo_ok, 6 * g + 2)
                if m >= 2:
                    pe.wait_ge(weighed, J * g + m - 1)
                else:
                    after(pe, weighed, J * (g - 1) + m + 3)
                t.matmul(ps[:, SPREAD[m % 2], 0:GN], expert_of[0:CW, m, :], h_hi[0:CW, MC, :],
                         start=True, stop=True).then_inc(spread, 1)

            def first():
                pe.wait_ge(w_lo, KC + 1)
                pe.wait_ge(cleared, 2)
                for j in range(J):
                    turn_z(0, 0, j)
                for j in range(J):
                    gnn(0, 0, j, steady=False)
                for j in range(J):
                    turn_z(0, 1, j)
                gnn(0, 1, 0, steady=False)
                gnn(0, 1, 1, steady=False)
                for j in range(J):
                    turn_xn(0, 0, j, True)

            def body(k, u, more=2):
                ffn1(k, u, MC)
                ffn1(k, u, 0)
                for m in range(1, MC):
                    ffn1(k, u, m)
                turn_comb(k, u)
                if more and u:
                    gnn(k, u + 1, 0)
                spread_comb(k, u, 0)
                spread_comb(k, u, 1)
                if more and u:
                    gnn(k, u + 1, 1)
                if more == 2:
                    turn_z(k, u + 2, 0)
                early = not more
                if early:
                    ffn2_start(k, u, 0, more)
                spread_comb(k, u, 2)
                if early:
                    ffn2_start(k, u, 1, more)
                spread_comb(k, u, 3)
                if more:
                    gnn(k, u + 1, 2)
                if more == 2:
                    turn_z(k, u + 2, 1)
                if more:
                    gnn(k, u + 1, 3)
                if more == 2:
                    turn_z(k, u + 2, 2)
                if early:
                    ffn2_rest(k, u, 0)
                else:
                    ffn2(k, u, 0, more)
                if more == 2:
                    turn_z(k, u + 2, 3)
                if early:
                    ffn2_rest(k, u, 1)
                else:
                    ffn2(k, u, 1, more)
                if more:
                    turn_xn(k, u + 1, 0, more == 2)
                    turn_xn(k, u + 1, 1, more == 2)
                ffn2(k, u, 2, more)
                if more:
                    turn_xn(k, u + 1, 2, more == 2)
                    turn_xn(k, u + 1, 3, more == 2)
                ffn2(k, u, 3, more)

            pipeline(pe, first, body, lambda k, u: body(k, u, more=G - 1 - u))


_INS = ["x", "src", "dst", "L0_gnn_W", "L0_gnn_b", "L0_ffn_gate_w", "L0_ffn_re_w1", "L0_ffn_re_b1", "L0_ffn_re_w2",
        "L0_ffn_re_b2", "L0_ffn_se_w1", "L0_ffn_se_b1", "L0_ffn_se_w2", "L0_ffn_se_b2"]


def kernel(**inputs):
    import numpy as _np
    import concourse.bacc as _bacc
    from concourse import mybir as _mybir
    from concourse.bass_utils import run_bass_kernel_spmd as _run

    nc = _bacc.Bacc("TRN2", target_bir_lowering=False, num_devices=1)
    arrays, args = {}, []
    for name in _INS:
        a = _np.ascontiguousarray(inputs[name])
        arrays[f"in_{name}"] = a
        args.append(nc.dram_tensor(f"in_{name}", a.shape, _mybir.dt.from_np(a.dtype), kind="ExternalInput").ap())
    shape = _np.shape(inputs["x"])
    args.append(nc.dram_tensor("out_0", shape, _mybir.dt.float32, kind="ExternalOutput").ap())
    gnn_moe(nc, *args)
    r = _run(nc, [arrays], core_ids=[0])
    return r.results[0]["out_0"]
```
